# Optimizing a Trainium2 kernel written in Bass

```python
import numpy as np
import jax
import jax.numpy as jnp

def _softmax(x, axis=-1):
    return jax.nn.softmax(x, axis=axis)

def _gelu(x):
    return jax.nn.gelu(x, approximate=True)

def _silu(x):
    return jax.nn.silu(x)

def _sigmoid(x):
    return jax.nn.sigmoid(x)

def _layernorm(x, axis=-1, eps=1e-05):
    m = jnp.mean(x, axis=axis, keepdims=True)
    v = jnp.var(x, axis=axis, keepdims=True)
    return (x - m) / jnp.sqrt(v + eps)

def _scatter_add(tgt, idx, src, axis=0):
    return tgt.at[idx].add(src)

def _segment_sum(src, seg, n):
    return jax.ops.segment_sum(src, seg, n)
kernel_name = 'mk_flamingo_gated_d2_seqx_r8_09ebe9'

def setup_inputs(seed: int=0):
    np.random.seed(seed)
    _w = jnp.asarray

    def _rec_inputs():
        import jax
        import jax.numpy as jnp
        _rk = jax.random.key(seed)
        x = -0.0002928 + 1 * jax.random.normal(jax.random.fold_in(_rk, 1), (2, 512, 128), jnp.float32)
        _lenS = 512 - jax.random.randint(jax.random.fold_in(_rk, 7), (2,), 0, max(1, 512 // 4) + 1, jnp.int32)
        _lenS2 = 77 - jax.random.randint(jax.random.fold_in(_rk, 8), (2,), 0, max(1, 77 // 4) + 1, jnp.int32)
        _ctx_1024P = jax.random.normal(jax.random.fold_in(_rk, 11), (2, 16, 128), jnp.float32)
        _ctx_1024c = jax.random.dirichlet(jax.random.fold_in(_rk, 511), 0.3 * jnp.ones((16,), jnp.float32), (2, 77))
        _ctx_1024t = jnp.einsum('bsk,bkd->bsd', _ctx_1024c, _ctx_1024P)
        _ctx_1024t = _ctx_1024t * jax.lax.rsqrt(jnp.mean(jnp.square(_ctx_1024t)) + 1e-12) * 0.953939
        ctx_1024 = -1.39393e-06 + 0.999914 * (_ctx_1024t + 0.3 * jax.random.normal(jax.random.fold_in(_rk, 611), (2, 77, 128), jnp.float32))
        _validS = jnp.arange(512)[None, :] < _lenS[:, None]
        _validS2 = jnp.arange(77)[None, :] < _lenS2[:, None]
        _causal = jnp.tril(jnp.ones((512, 512), dtype=bool))
        mask_Bx1xSxS2_ik1 = jnp.where(jnp.broadcast_to(_validS2[:, None, None, :], (2, 1, 512, 77)), 1, 0).astype(jnp.int32)
        _g = jax.random.normal(jax.random.fold_in(_rk, 9001), (2, 2), jnp.float32)
        _g = jnp.sign(_g) * jnp.maximum(jnp.abs(_g), 1.0) + (_g == 0) * 1.0
        g_xattn = _g[0]
        g_ffn = _g[1]
        return (x, ctx_1024, mask_Bx1xSxS2_ik1, g_xattn, g_ffn)
    x, ctx_1024, mask_Bx1xSxS2_ik1, g_xattn, g_ffn = _rec_inputs()

    def _L0_xattn_setup():
        import jax, jax.numpy as jnp
        import numpy as np
        import math
        D_MODEL = 128
        N_HEAD = 16
        D_HEAD = D_MODEL // N_HEAD
        B, TQ, TK = (2, 256, 256)
        key = jax.random.key(seed)
        ks = jax.random.split(key, 12)
        s = 1.0 / math.sqrt(D_MODEL)
        return {'q': jax.random.normal(ks[0], (B, TQ, D_MODEL), jnp.float32), 'k': jax.random.normal(ks[1], (B, TK, D_MODEL), jnp.float32), 'v': jax.random.normal(ks[2], (B, TK, D_MODEL), jnp.float32), 'mask': jax.random.randint(ks[3], (B, 1, TQ, TK), 0, 2, jnp.int32), 'Wq': jax.random.normal(ks[4], (D_MODEL, D_MODEL), jnp.float32) * s, 'bq': jnp.zeros((D_MODEL,), jnp.float32), 'Wk': jax.random.normal(ks[5], (D_MODEL, D_MODEL), jnp.float32) * s, 'bk': jnp.zeros((D_MODEL,), jnp.float32), 'Wv': jax.random.normal(ks[6], (D_MODEL, D_MODEL), jnp.float32) * s, 'bv': jnp.zeros((D_MODEL,), jnp.float32), 'Wo': jax.random.normal(ks[7], (D_MODEL, D_MODEL), jnp.float32) * s, 'bo': jnp.zeros((D_MODEL,), jnp.float32)}
    _L0_xattn_all = _L0_xattn_setup()
    _L0_xattn_in = {k: v for k, v in _L0_xattn_all.items() if k in ('Wq', 'bq', 'Wk', 'bk', 'Wv', 'bv', 'Wo', 'bo')}
    del _L0_xattn_all

    def _L0_ffn_setup():
        import math
        import jax, jax.numpy as jnp
        import numpy as np
        H = 128
        F = 512
        E = 8
        TOP_K = 2
        CAP_FACTOR = 1.25
        MIN_CAP = 4
        SHARED_SCALE = 0.1

        def _top2_gating(logits, capacity):
            N, nE = logits.shape
            gates = jax.nn.softmax(logits, axis=-1)
            idx1 = jnp.argmax(gates, axis=-1)
            mask1 = jax.nn.one_hot(idx1, nE, dtype=gates.dtype)
            idx2 = jnp.argmax(gates * (1.0 - mask1), axis=-1)
            mask2 = jax.nn.one_hot(idx2, nE, dtype=gates.dtype)
            pos1 = jnp.cumsum(mask1, axis=0) - mask1
            mask1 = mask1 * (pos1 < capacity)
            pos2 = jnp.cumsum(mask2, axis=0) - mask2 + jnp.sum(mask1, axis=0, keepdims=True)
            mask2 = mask2 * (pos2 < capacity)
            g1 = jnp.sum(gates * mask1, axis=-1)
            g2 = jnp.sum(gates * mask2, axis=-1)
            denom = jnp.maximum(g1 + g2, jnp.finfo(gates.dtype).eps)
            g1, g2 = (g1 / denom, g2 / denom)
            loc1 = jnp.sum(pos1 * mask1, axis=-1).astype(jnp.int32)
            loc2 = jnp.sum(pos2 * mask2, axis=-1).astype(jnp.int32)
            oh1 = jax.nn.one_hot(loc1, capacity, dtype=gates.dtype)
            oh2 = jax.nn.one_hot(loc2, capacity, dtype=gates.dtype)
            combine = (g1[:, None] * mask1)[:, :, None] * oh1[:, None, :] + (g2[:, None] * mask2)[:, :, None] * oh2[:, None, :]
            dispatch = (combine > 0).astype(gates.dtype)
            return (combine, dispatch)
        key = jax.random.key(seed)
        ks = jax.random.split(key, 10)
        s_h = 1.0 / math.sqrt(H)
        s_f = 1.0 / math.sqrt(F)
        return {'hidden_states': jax.random.normal(ks[0], (2, 256, H), jnp.float32), 'router_w': jax.random.uniform(ks[1], (H, E), jnp.float32, -s_h, s_h), 'w1': jax.random.uniform(ks[2], (E, H, F), jnp.float32, -s_h, s_h), 'b1': jax.random.uniform(ks[3], (E, F), jnp.float32, -s_h, s_h), 'w2': jax.random.uniform(ks[4], (E, F, H), jnp.float32, -s_f, s_f), 'b2': jax.random.uniform(ks[5], (E, H), jnp.float32, -s_f, s_f), 'sw1': jax.random.uniform(ks[6], (H, F), jnp.float32, -s_h, s_h), 'sb1': jax.random.uniform(ks[7], (F,), jnp.float32, -s_h, s_h), 'sw2': jax.random.uniform(ks[8], (F, H), jnp.float32, -s_f, s_f), 'sb2': jax.random.uniform(ks[9], (H,), jnp.float32, -s_f, s_f)}
    _L0_ffn_all = _L0_ffn_setup()
    _L0_ffn_in = {k: v for k, v in _L0_ffn_all.items() if k in ('router_w', 'w1', 'b1', 'w2', 'b2', 'sw1', 'sb1', 'sw2', 'sb2')}
    del _L0_ffn_all

    def _L1_xattn_setup():
        import jax, jax.numpy as jnp
        import numpy as np
        EMBED = 128
        HEADS = 16
        HEAD_DIM = EMBED // HEADS
        key = jax.random.key(seed)
        ks = jax.random.split(key, 8)
        B, S = (2, 256)
        return {'values': jax.random.normal(ks[0], (B, S, EMBED), jnp.float32), 'keys': jax.random.normal(ks[1], (B, S, EMBED), jnp.float32), 'query': jax.random.normal(ks[2], (B, S, EMBED), jnp.float32), 'Wv': jax.random.normal(ks[3], (EMBED, EMBED), jnp.float32) * EMBED ** (-0.5), 'Wk': jax.random.normal(ks[4], (EMBED, EMBED), jnp.float32) * EMBED ** (-0.5), 'Wq': jax.random.normal(ks[5], (EMBED, EMBED), jnp.float32) * EMBED ** (-0.5), 'Wo': jax.random.normal(ks[6], (EMBED, EMBED), jnp.float32) * EMBED ** (-0.5), 'bo': jnp.zeros((EMBED,), jnp.float32)}
    _L1_xattn_all = _L1_xattn_setup()
    _L1_xattn_in = {k: v for k, v in _L1_xattn_all.items() if k in ('Wv', 'Wk', 'Wq', 'Wo', 'bo')}
    del _L1_xattn_all

    def _L1_ffn_setup():
        import jax, jax.numpy as jnp
        import numpy as np
        B, T, D, E, H = (4, 256, 128, 4, 8)
        EPS = 1e-05

        def _uniform(k, shape, bound):
            return jax.random.uniform(k, shape, jnp.float32, -bound, bound)

        def _layernorm(x, w, b):
            mu = jnp.mean(x, axis=-1, keepdims=True)
            var = jnp.mean(jnp.square(x - mu), axis=-1, keepdims=True)
            return (x - mu) * jax.lax.rsqrt(var + EPS) * w + b
        key = jax.random.key(seed)
        ks = jax.random.split(key, 12)
        wb = np.sqrt(6.0 / D) / np.sqrt(6.0)
        wb = 1.0 / np.sqrt(D)
        return {'x': jax.random.normal(ks[0], (B, T, D), jnp.float32), 'router_prob': jax.random.uniform(ks[1], (B, T, E), jnp.float32), 'norm_w': jnp.ones((D,), jnp.float32), 'norm_b': jnp.zeros((D,), jnp.float32), 'q_w': _uniform(ks[2], (D, D), wb), 'q_b': _uniform(ks[3], (D,), wb), 'k_w': _uniform(ks[4], (D, D), wb), 'k_b': _uniform(ks[5], (D,), wb), 'v_w': _uniform(ks[6], (D, D), wb), 'v_b': _uniform(ks[7], (D,), wb), 'o_w': _uniform(ks[8], (D, D), wb), 'o_b': _uniform(ks[9], (D,), wb)}
    _L1_ffn_all = _L1_ffn_setup()
    _L1_ffn_in = {k: v for k, v in _L1_ffn_all.items() if k in ('router_prob', 'norm_w', 'norm_b', 'q_w', 'q_b', 'k_w', 'k_b', 'v_w', 'v_b', 'o_w', 'o_b')}
    del _L1_ffn_all
    return {'x': x, 'ctx_1024': ctx_1024, 'mask_Bx1xSxS2_ik1': mask_Bx1xSxS2_ik1, 'g_xattn': g_xattn, 'g_ffn': g_ffn, 'L0_xattn_Wq': _L0_xattn_in['Wq'], 'L0_xattn_bq': _L0_xattn_in['bq'], 'L0_xattn_Wk': _L0_xattn_in['Wk'], 'L0_xattn_bk': _L0_xattn_in['bk'], 'L0_xattn_Wv': _L0_xattn_in['Wv'], 'L0_xattn_bv': _L0_xattn_in['bv'], 'L0_xattn_Wo': _L0_xattn_in['Wo'], 'L0_xattn_bo': _L0_xattn_in['bo'], 'L0_ffn_router_w': _L0_ffn_in['router_w'], 'L0_ffn_w1': _L0_ffn_in['w1'], 'L0_ffn_b1': _L0_ffn_in['b1'], 'L0_ffn_w2': _L0_ffn_in['w2'], 'L0_ffn_b2': _L0_ffn_in['b2'], 'L0_ffn_sw1': _L0_ffn_in['sw1'], 'L0_ffn_sb1': _L0_ffn_in['sb1'], 'L0_ffn_sw2': _L0_ffn_in['sw2'], 'L0_ffn_sb2': _L0_ffn_in['sb2'], 'L1_xattn_Wv': _L1_xattn_in['Wv'], 'L1_xattn_Wk': _L1_xattn_in['Wk'], 'L1_xattn_Wq': _L1_xattn_in['Wq'], 'L1_xattn_Wo': _L1_xattn_in['Wo'], 'L1_xattn_bo': _L1_xattn_in['bo'], 'L1_ffn_router_prob': _L1_ffn_in['router_prob'], 'L1_ffn_norm_w': _L1_ffn_in['norm_w'], 'L1_ffn_norm_b': _L1_ffn_in['norm_b'], 'L1_ffn_q_w': _L1_ffn_in['q_w'], 'L1_ffn_q_b': _L1_ffn_in['q_b'], 'L1_ffn_k_w': _L1_ffn_in['k_w'], 'L1_ffn_k_b': _L1_ffn_in['k_b'], 'L1_ffn_v_w': _L1_ffn_in['v_w'], 'L1_ffn_v_b': _L1_ffn_in['v_b'], 'L1_ffn_o_w': _L1_ffn_in['o_w'], 'L1_ffn_o_b': _L1_ffn_in['o_b']}

def reference(x, ctx_1024, mask_Bx1xSxS2_ik1, g_xattn, g_ffn, L0_xattn_Wq, L0_xattn_bq, L0_xattn_Wk, L0_xattn_bk, L0_xattn_Wv, L0_xattn_bv, L0_xattn_Wo, L0_xattn_bo, L0_ffn_router_w, L0_ffn_w1, L0_ffn_b1, L0_ffn_w2, L0_ffn_b2, L0_ffn_sw1, L0_ffn_sb1, L0_ffn_sw2, L0_ffn_sb2, L1_xattn_Wv, L1_xattn_Wk, L1_xattn_Wq, L1_xattn_Wo, L1_xattn_bo, L1_ffn_router_prob, L1_ffn_norm_w, L1_ffn_norm_b, L1_ffn_q_w, L1_ffn_q_b, L1_ffn_k_w, L1_ffn_k_b, L1_ffn_v_w, L1_ffn_v_b, L1_ffn_o_w, L1_ffn_o_b):
    import jax
    import jax.numpy as jnp

    def _L0_xattn_ref(q, k, v, mask, Wq, bq, Wk, bk, Wv, bv, Wo, bo):
        import jax, jax.numpy as jnp
        import numpy as np
        import math
        D_MODEL = 128
        N_HEAD = 16
        D_HEAD = D_MODEL // N_HEAD
        B, TQ, TK = (2, 256, 256)

        def proj(x, W, b, T):
            return (x @ W.T + b).reshape(x.shape[0], T, N_HEAD, D_HEAD).transpose(0, 2, 1, 3)
        Q = proj(q, Wq, bq, q.shape[1])
        K = proj(k, Wk, bk, k.shape[1])
        V = proj(v, Wv, bv, v.shape[1])
        scores = jnp.einsum('bhqd,bhkd->bhqk', Q, K) / math.sqrt(D_HEAD)
        neg = jnp.finfo(scores.dtype).min
        scores = jnp.where(mask == 0, neg, scores)
        attn = jax.nn.softmax(scores, axis=-1)
        out = jnp.einsum('bhqk,bhkd->bhqd', attn, V)
        out = out.transpose(0, 2, 1, 3).reshape(q.shape[0], q.shape[1], D_MODEL)
        return out @ Wo.T + bo

    def _L0_ffn_ref(hidden_states, router_w, w1, b1, w2, b2, sw1, sb1, sw2, sb2):
        import math
        import jax, jax.numpy as jnp
        import numpy as np
        H = 128
        F = 512
        E = 8
        TOP_K = 2
        CAP_FACTOR = 1.25
        MIN_CAP = 4
        SHARED_SCALE = 0.1

        def _top2_gating(logits, capacity):
            N, nE = logits.shape
            gates = jax.nn.softmax(logits, axis=-1)
            idx1 = jnp.argmax(gates, axis=-1)
            mask1 = jax.nn.one_hot(idx1, nE, dtype=gates.dtype)
            idx2 = jnp.argmax(gates * (1.0 - mask1), axis=-1)
            mask2 = jax.nn.one_hot(idx2, nE, dtype=gates.dtype)
            pos1 = jnp.cumsum(mask1, axis=0) - mask1
            mask1 = mask1 * (pos1 < capacity)
            pos2 = jnp.cumsum(mask2, axis=0) - mask2 + jnp.sum(mask1, axis=0, keepdims=True)
            mask2 = mask2 * (pos2 < capacity)
            g1 = jnp.sum(gates * mask1, axis=-1)
            g2 = jnp.sum(gates * mask2, axis=-1)
            denom = jnp.maximum(g1 + g2, jnp.finfo(gates.dtype).eps)
            g1, g2 = (g1 / denom, g2 / denom)
            loc1 = jnp.sum(pos1 * mask1, axis=-1).astype(jnp.int32)
            loc2 = jnp.sum(pos2 * mask2, axis=-1).astype(jnp.int32)
            oh1 = jax.nn.one_hot(loc1, capacity, dtype=gates.dtype)
            oh2 = jax.nn.one_hot(loc2, capacity, dtype=gates.dtype)
            combine = (g1[:, None] * mask1)[:, :, None] * oh1[:, None, :] + (g2[:, None] * mask2)[:, :, None] * oh2[:, None, :]
            dispatch = (combine > 0).astype(gates.dtype)
            return (combine, dispatch)
        B, S, h = hidden_states.shape
        x = hidden_states.reshape(-1, h)
        N = x.shape[0]
        capacity = min(max(MIN_CAP, math.ceil(TOP_K * CAP_FACTOR * N / E)), N)
        logits = x @ router_w
        combine, dispatch = _top2_gating(logits, capacity)
        expert_in = jnp.einsum('nec,nh->ech', dispatch, x)
        hmid = jax.nn.silu(jnp.einsum('ech,ehf->ecf', expert_in, w1) + b1[:, None, :])
        expert_out = jnp.einsum('ecf,efh->ech', hmid, w2) + b2[:, None, :]
        y = jnp.einsum('nec,ech->nh', combine, expert_out)
        shared = jax.nn.silu(x @ sw1 + sb1) @ sw2 + sb2
        out = y + SHARED_SCALE * shared
        return out.reshape(B, S, h)

    def _L1_xattn_ref(values, keys, query, Wv, Wk, Wq, Wo, bo):
        import jax, jax.numpy as jnp
        import numpy as np
        EMBED = 128
        HEADS = 16
        HEAD_DIM = EMBED // HEADS
        N, Q, _ = query.shape
        v = (values @ Wv.T).reshape(N, -1, HEADS, HEAD_DIM)
        k = (keys @ Wk.T).reshape(N, -1, HEADS, HEAD_DIM)
        q = (query @ Wq.T).reshape(N, -1, HEADS, HEAD_DIM)
        energy = jnp.einsum('nqhd,nkhd->nhqk', q, k)
        attn = jax.nn.softmax(energy / HEAD_DIM ** 0.5, axis=-1)
        out = jnp.einsum('nhqk,nkhd->nqhd', attn, v).reshape(N, Q, EMBED)
        return out @ Wo.T + bo

    def _L1_ffn_ref(x, router_prob, norm_w, norm_b, q_w, q_b, k_w, k_b, v_w, v_b, o_w, o_b):
        import jax, jax.numpy as jnp
        import numpy as np
        B, T, D, E, H = (4, 256, 128, 4, 8)
        EPS = 1e-05

        def _uniform(k, shape, bound):
            return jax.random.uniform(k, shape, jnp.float32, -bound, bound)

        def _layernorm(x, w, b):
            mu = jnp.mean(x, axis=-1, keepdims=True)
            var = jnp.mean(jnp.square(x - mu), axis=-1, keepdims=True)
            return (x - mu) * jax.lax.rsqrt(var + EPS) * w + b
        e_cnt = router_prob.shape[2]
        b, t, d = x.shape
        n = t // e_cnt
        h = H
        scale = d ** (-0.5)
        qs, ks_, vs = ([], [], [])
        for e in range(e_cnt):
            xe = x[:, e * n:(e + 1) * n, :]
            xn = _layernorm(xe, norm_w, norm_b)
            m = d // 2 ** e
            xm = xn[..., :m]
            qs.append(jnp.einsum('bnm,dm->bnd', xm, q_w[:, :m]) + q_b)
            ks_.append(jnp.einsum('bnm,dm->bnd', xm, k_w[:, :m]) + k_b)
            vs.append(jnp.einsum('bnm,dm->bnd', xm, v_w[:, :m]) + v_b)
        q = jnp.concatenate(qs, axis=1)
        k = jnp.concatenate(ks_, axis=1)
        v = jnp.concatenate(vs, axis=1)
        dh = d // h
        q = q.reshape(b, t, h, dh).transpose(0, 2, 1, 3)
        k = k.reshape(b, t, h, dh).transpose(0, 2, 1, 3)
        v = v.reshape(b, t, h, dh).transpose(0, 2, 1, 3)
        attn = jnp.einsum('bhqd,bhkd->bhqk', q, k) * scale
        attn = jax.nn.softmax(attn, axis=-1)
        attn_out = jnp.einsum('bhqk,bhkd->bhqd', attn, v)
        attn_out = attn_out.transpose(0, 2, 1, 3).reshape(b, t, d)
        outs = []
        for e in range(e_cnt):
            sl = slice(e * n, (e + 1) * n)
            m = d // 2 ** e
            xm = attn_out[:, sl, :m]
            out = jnp.einsum('bnm,om->bno', xm, o_w[:m, :m]) + o_b[:m]
            pad = d - m
            if pad:
                out = jnp.pad(out, ((0, 0), (0, 0), (0, pad)))
            outs.append(out + x[:, sl, :])
        return jnp.concatenate(outs, axis=1)
    x = x + jnp.tanh(g_xattn[0]) * _L0_xattn_ref(_layernorm(x, axis=-1), ctx_1024, ctx_1024, mask_Bx1xSxS2_ik1, L0_xattn_Wq, L0_xattn_bq, L0_xattn_Wk, L0_xattn_bk, L0_xattn_Wv, L0_xattn_bv, L0_xattn_Wo, L0_xattn_bo)
    x = x + jnp.tanh(g_ffn[0]) * _L0_ffn_ref(_layernorm(x, axis=-1), L0_ffn_router_w, L0_ffn_w1, L0_ffn_b1, L0_ffn_w2, L0_ffn_b2, L0_ffn_sw1, L0_ffn_sb1, L0_ffn_sw2, L0_ffn_sb2)
    x = x + jnp.tanh(g_xattn[1]) * _L1_xattn_ref(ctx_1024, ctx_1024, _layernorm(x, axis=-1), L1_xattn_Wv, L1_xattn_Wk, L1_xattn_Wq, L1_xattn_Wo, L1_xattn_bo)
    x = x + jnp.tanh(g_ffn[1]) * _L1_ffn_ref(_layernorm(x, axis=-1), L1_ffn_router_prob, L1_ffn_norm_w, L1_ffn_norm_b, L1_ffn_q_w, L1_ffn_q_b, L1_ffn_k_w, L1_ffn_k_b, L1_ffn_v_w, L1_ffn_v_b, L1_ffn_o_w, L1_ffn_o_b)
    return x

_drawn_inputs = setup_inputs


def setup_inputs(seed=0):
    import zlib

    import numpy as np

    out = dict(_drawn_inputs(seed))
    spreads = {'g_ffn': (-1.0, 0.2),
     'L0_xattn_bq': (0.0, 0.314),
     'L0_xattn_bk': (0.0, 2.0),
     'L0_xattn_bv': (0.0, 0.1),
     'L0_xattn_bo': (0.0, 0.1),
     'L1_xattn_bo': (0.0, 0.1),
     'L1_ffn_norm_w': (1.0, 0.6),
     'L1_ffn_norm_b': (0.0, 0.366)}
    factors = {'L0_ffn_b1': 6.693,
     'L0_ffn_b2': 4.387,
     'L0_ffn_sw1': 4.818,
     'L0_ffn_sb1': 8.0,
     'L0_ffn_sw2': 4.754,
     'L0_ffn_sb2': 23.498,
     'L1_ffn_q_w': 8.0,
     'L1_ffn_q_b': 8.0,
     'L1_ffn_k_w': 8.0,
     'L1_ffn_k_b': 64.0}
    for name, (base, spread) in spreads.items():
        noise = np.random.default_rng([zlib.crc32(name.encode()), seed]).standard_normal(out[name].shape)
        drawn = base * np.exp(spread * noise) if base else spread * noise
        out[name] = jnp.asarray(drawn.astype(out[name].dtype))
    for name, factor in factors.items():
        out[name] = (out[name] * factor).astype(out[name].dtype)
    return out
```

```python
from contextlib import ExitStack

import numpy as np

import concourse.bass as bass
from concourse import mybir

F32 = mybir.dt.float32
BF16 = mybir.dt.bfloat16
I32 = mybir.dt.int32
U32 = mybir.dt.uint32
ALU = mybir.AluOpType
ACT = mybir.ActivationFunctionType
AX = mybir.AxisListType

P = 128
B = 2
S = 512
D = 128
NT = B * S // P
TB = S // P
H = 16
DH = D // H
NK = 77
E = 8
F = 512
FC = F // P
CAP = 320
SLOTS = E * CAP
ST = SLOTS // P
NTOK = B * S
ROW = D + 1
H2 = 8
DH2 = D // H2
EPS = 1e-5
SHARED_SCALE = 0.1
BIG = float(2.0 ** 100)
NONE = 4096.0
FEPS = float(np.finfo(np.float32).eps)

QROW = NK
MROW = QROW + 6 * DH
MROW2 = 6 * DH2
QPART = (0, 0, 0, 1, 1, 2)
KPART = (0, 1, 2, 0, 1, 0)

HEADS_OF = [H2 >> e for e in range(TB)]
NQ = [P * sum(h < n for n in HEADS_OF) for h in range(H2)]
PACKS = [[(0, 0), (1, 512), (4, 896)], [(2, 0), (3, 256), (5, 512), (6, 640), (7, 768)]]
PACK_W = [1024, 896]
PACK_AT = [0, 1024]
P2W = sum(PACK_W)
P2AT = {h: PACK_AT[k] + at for k in range(2) for h, at in PACKS[k]}
QM2 = [(e, h) for e in range(TB) for h in range(HEADS_OF[e])]
BLOCKS = [(e, h) for e in range(TB) for h in range(HEADS_OF[e])]

WEIGHTS = ["L0_xattn_Wq", "L0_xattn_Wk", "L0_xattn_Wv", "L0_xattn_Wo",
           "L1_xattn_Wq", "L1_xattn_Wk", "L1_xattn_Wv", "L1_xattn_Wo",
           "L1_ffn_q_w", "L1_ffn_k_w", "L1_ffn_v_w", "L1_ffn_o_w"]
ROWS = [("L0_ffn_b1", E * FC), ("L0_ffn_sb1", FC), ("L0_xattn_bq", 1), ("L0_xattn_bk", 1),
        ("L1_ffn_q_b", 1), ("L1_ffn_k_b", 1), ("L1_ffn_norm_w", 1), ("L1_ffn_norm_b", 1)]
ROW_AT = {}
_n = 0
for _name, _k in ROWS:
    ROW_AT[_name] = _n
    _n += _k
NROWS = _n
BC = ["L0_xattn_bv", "L0_xattn_bo", "L0_ffn_sb2", "L1_xattn_bo", "L1_ffn_v_b", "L1_ffn_o_b"]
BC_AT = {name: i for i, name in enumerate(BC)}


def work_jobs():
    jobs = []

    def prologue(L, b):
        jobs.append((("xT", L, b), "act"))
        if L != "B":
            jobs.append((("q", L, b), "dve"))
        if L == "D":
            jobs.append((("k", L, b), "dve"))
            jobs.append((("v", L, b), "dve"))

    def epilogue(L, b):
        if L == "D":
            jobs.append((("oT", L, b, 0), "dve"))
        else:
            for g in range(4):
                jobs.append((("oT", L, b, g), "dve"))
        jobs.append((("onT", L, b), "act"))
        jobs.append((("y", L, b), "dve"))

    def attention(L):
        for b in range(B):
            prologue(L, b)
        jobs.append((("nT", L, 0), "dve"))
        n_pv = 2 if L == "D" else 4
        for g in range(n_pv):
            jobs.append((("pv", L, 0, g), "dve"))
        jobs.append((("nT", L, 1), "dve"))
        epilogue(L, 0)
        for g in range(n_pv):
            jobs.append((("pv", L, 1, g), "dve"))
        epilogue(L, 1)

    attention("A")
    for b in range(B):
        prologue("B", b)
    jobs.append((("logits",), "dve"))
    jobs.append((("pos",), "dve"))
    for n in range(ST // 4):
        jobs.append((("xg", n), "act"))
    attention("C")
    attention("D")
    return jobs


JOBS = work_jobs()
JOB = {name: n for n, (name, _) in enumerate(JOBS)}


def taken(n):
    who = JOBS[n][1]
    return who, sum(1 for _, w in JOBS[:n + 1] if w == who)


LN = {(L, b): 2 * i + b for i, L in enumerate("ABCD") for b in range(B)}
XI = {("A", 0): 0, ("A", 1): 1, ("C", 0): 2, ("C", 1): 3, ("D", 0): 4, ("D", 1): 5}
QM_UNITS = {"A": 16, "C": 16, "D": len(QM2)}
T_UNITS = 8


def qm_index(L, b, u):
    before = {"A": 0, "C": 32, "D": 64}[L]
    return before + b * QM_UNITS[L] + u


def t_index(L, b, u):
    return ({"A": 0, "C": 2, "D": 4}[L] + b) * T_UNITS + u


def build(nc, a, out):
    with ExitStack() as ctx:
        def sb(name, shape, dt=F32):
            return ctx.enter_context(nc.sbuf_tensor(name, shape, dt))

        def sem(name):
            return ctx.enter_context(nc.semaphore(name))

        def dram(name, shape, dt):
            return nc.dram_tensor(name, shape, dt, kind="Internal").ap()

        qm = ctx.enter_context(nc.psum_tensor("qm", [P, 2, 512], F32))
        ts = ctx.enter_context(nc.psum_tensor("ts", [P, 4, 512], F32))
        wk = ctx.enter_context(nc.psum_tensor("wk", [P, 2, 512], F32))

        x = sb("x", [P, NT, D])
        xn = sb("xn", [P, NT, ROW])
        xb = sb("xb", [P, NT, D])
        xT = sb("xT", [P, NTOK])
        ctx_sb = sb("ctx_sb", [NK, B, D])
        ctxT = sb("ctxT", [P, B * NK])
        early = sb("early", [P, ST * ROW])
        mask_i = early[:, 0:NT * NK].bitcast(I32).rearrange("p (t k) -> p t k", k=NK)
        keep = early[:, NT * NK:2 * NT * NK].rearrange("p (t k) -> p t k", k=NK)
        someB = early[:, 2 * NT * NK:2 * NT * NK + NTOK]
        xg = early[:, :].rearrange("p (i r) -> p i r", r=ROW)
        fill = sb("fill", [P, ROW])
        some = sb("some", [P, NT])
        some_b = sb("some_b", [P, NT], BF16)
        none = sb("none", [P, NT])
        mneg = sb("mneg", [P, NT, NK], BF16)
        mnegT = sb("mnegT", [NK, NTOK], BF16)
        y12 = sb("y12", [P, 2, NT, D])
        wn = y12[:, :, :, :].rearrange("p c t d -> p (c t) d")[:, 0:12, :]
        wT = sb("wT", [P, 12, D])
        rows = sb("rows", [NROWS, D])
        col = sb("col", [P, NROWS])
        bc = sb("bc", [P, len(BC), D])
        gates_in = sb("gates_in", [P, 4])
        tg = sb("tg", [P, 4])
        tgs = sb("tgs", [P, 1])
        rw = sb("rw", [P, E])
        w1 = sb("w1", [P, E, F])
        w2 = sb("w2", [P, E, FC, D])
        b2 = sb("b2", [P, E, D])
        sw1 = sb("sw1", [P, F])
        sw2 = sb("sw2", [P, FC, D])
        ident = sb("ident", [P, P])
        identb = sb("identb", [P, P], BF16)
        onesb = sb("onesb", [P, P], BF16)
        trib = sb("trib", [P, P], BF16)
        half = sb("half", [P, 8])
        stats = sb("stats", [P, TB, 6])
        mv = sb("mv", [P, B, TB, 2])
        ve = sb("ve", [P, B, 2, TB])
        rstd = sb("rstd", [P, B, 2, TB])
        rtg = sb("rtg", [P, B, TB])
        qf = sb("qf", [P, S])
        qr = sb("qr", [P, S])
        parts = sb("parts", [P, 3, S], BF16)
        kf = sb("kf", [P, B * NK])
        kr = sb("kr", [P, B * NK])
        kparts = [sb(f"kparts{i}", [P, 3, B, P], BF16) for i in range(2)]
        qst = sb("qst", [P, H, NTOK], BF16)
        kst = sb("kst", [P, 2, H, B, P], BF16)
        kst2 = w1[:, :, :].rearrange("p e f -> p (e f)").bitcast(BF16).rearrange("p (h n) -> p h n", h=H2)
        vst = [sb(f"vst{i}", [P, B, H, 32]) for i in range(2)]
        vst2 = w2[:, :, :, :].rearrange("p e c h -> p (e c h)")[:, 0:B * TB * H2 * 32].rearrange(
            "p (b t h r) -> p b t h r", b=B, t=TB, h=H2)
        nmx = sb("nmx", [P, TB, H])
        nmr = sb("nmr", [P, TB, H])
        nsp = sb("nsp", [P, TB, 3, H], BF16)
        nsT = sb("nsT", [3 * H, S], BF16)
        pr = sb("pr", [P, H, S])
        oo = sb("oo", [P, 4 * S + TB * D])
        oT = oo[:, 0:4 * S].rearrange("p (g n) -> p g n", g=4)
        on = oo[:, 4 * S:4 * S + TB * D].rearrange("p (t d) -> p t d", d=D)
        rden = sb("rden", [P, 16])
        onT = sb("onT", [P, S])

        pr_flat = pr[:, :, :].rearrange("p a b -> p (a b)")
        pr2 = pr_flat[:, 0:TB * P2W].rearrange("p (k c) -> p k c", k=TB)
        hs = pr_flat[:, 0:FC * NTOK].rearrange("p (c n) -> p c n", c=FC)
        he = pr_flat[:, FC * NTOK:FC * NTOK + 3 * FC * CAP].rearrange("p (r c n) -> p r c n", r=3, c=FC)
        xgT = oo[:, :]
        ostage = onT[:, :].rearrange("p (i d) -> p i d", d=D)
        sums = sb("sums", [P, NT])
        lg, gates, gates2, cand = (qf[:, NT * E * i:NT * E * i + NT * E].rearrange("p (t e) -> p t e", e=E) for i in range(4))
        hot, posn, kept, rt = (qr[:, 2 * NT * E * i:2 * NT * E * (i + 1)].rearrange("p (c t e) -> p c t e", c=2, e=E) for i in range(4))
        best = sb("best", [P, NT])
        first = sb("first", [P, NT])
        iota8 = sb("iota8", [P, NT, E])
        iota8i = sb("iota8i", [P, NT, E], I32)
        base320 = sb("base320", [P, E])
        toki = sb("toki", [P, NT], I32)
        hotb = sb("hotb", [P, 2, NT, E], BF16)
        n1 = sb("n1", [P, 2, E])
        g12 = sb("g12", [P, 2, NT])
        k12 = sb("k12", [P, 2, NT])
        s12 = sb("s12", [P, 2, NT])
        den = sb("den", [P, NT])
        slot_i = sb("slot_i", [P, 2, NT], I32)
        sidx_i = sb("sidx_i", [P, ST], I32)
        sidx = sb("sidx", [P, ST])
        sidx_t = sb("sidx_t", [P, ST])
        n1s = sb("n1s", [P, ST])
        dst_i = sb("dst_i", [P, ST], I32)

        kd = dram("kd", [2, 3, D, B * P], BF16)
        qd = dram("qd", [6, 3, D, S], BF16)
        kd2 = dram("kd2", [2, 3, D, S], BF16)
        nd = dram("nd", [6, 3 * H, S], BF16)
        xs_d = dram("xs_d", [SLOTS, ROW], F32)
        y_d = dram("y_d", [2 * NTOK, D], F32)

        x_in = [sem(f"x_in{b}") for b in range(B)]
        ctx_in, mask_in, rows_in, gate_in, bc_in = (sem(n) for n in ("ctx_in", "mask_in", "rows_in", "gate_in", "bc_in"))
        w_in = [sem(f"w_in{i}") for i in range(3)]
        moe_in = [sem(f"moe_in{i}") for i in range(3)]
        const = sem("const")
        dve = sem("dve_chain")
        pol = sem("pool_chain")
        mneg_ready, some_ready = sem("mneg_ready"), sem("some_ready")
        setup_mm, setup_ev = sem("setup_mm"), sem("setup_ev")
        tg_ready, tgs_ready, bias_ready = sem("tg_ready"), sem("tgs_ready"), sem("bias_ready")
        kv_mm, kparts_ready, vst_ready = sem("kv_mm"), sem("kparts_ready"), sem("vst_ready")
        kd_out = [sem(f"kd_out{i}") for i in range(2)]
        kst_in = [sem(f"kst_in{i}") for i in range(2)]
        mask_rows_in = sem("mask_rows_in")
        var_ready, rstd_ready, xn_ready, xb_ready = sem("var_ready"), sem("rstd_ready"), sem("xn_ready"), sem("xb_ready")
        job_mm, job_dve, job_act = sem("job_mm"), sem("job_dve"), sem("job_act")
        qparts_ready, k2parts_ready, kpad = sem("qparts_ready"), sem("k2parts_ready"), sem("kpad")
        qd_out = [sem(f"qd_out{i}") for i in range(6)]
        qst_in = [sem(f"qst_in{i}") for i in range(6)]
        k2d_out = [sem(f"k2d_out{i}") for i in range(2)]
        k2st_in = [sem(f"k2st_in{i}") for i in range(2)]
        nd_out = [sem(f"nd_out{i}") for i in range(6)]
        nst_in = [sem(f"nst_in{i}") for i in range(6)]
        qm_mm, qm_max, nsp_ready = sem("qm_mm"), sem("qm_max"), sem("nsp_ready")
        t_mm, t_exp = sem("t_mm"), sem("t_exp")
        x_moe = sem("x_moe")
        ex_ready, hot_ready, slot_ready, dst_ready = (sem(n) for n in ("ex_ready", "hot_ready", "slot_ready", "dst_ready"))
        hid_mm, hid_act, out_mm, out_ev = sem("hid_mm"), sem("hid_act"), sem("out_mm"), sem("out_ev")
        fill_src, fill_xs, fill_y, scat, xg_in, y_in = (sem(n) for n in ("fill_src", "fill_xs", "fill_y", "scat", "xg_in", "y_in"))
        y_scats = [sem(f"y_scat{i}") for i in range(4)]
        out_sem = sem("out_sem")

        def done(*name):
            who, value = taken(JOB[name])
            return (job_dve if who == "dve" else job_act), value

        C_IDENT, C_IDENTB, C_ONES, C_TRI, C_HALF, C_KST, C_KID, C_VST, C_N1, C_IOTA, C_SIDX, C_KST2 = range(2, 14)

        x_dram = a["x"].rearrange("b (t p) d -> p b t d", p=P)
        out_dram = out.rearrange("b (t p) d -> p b t d", p=P)

        block = ctx.enter_context(nc.Block())

        @block.sync
        def _(sp):
            def bcast(name):
                return a[name].partition_broadcast(P)

            for b in range(B):
                sp.dma_start(x[:, TB * b:TB * b + TB, :], x_dram[:, b]).then_inc(x_in[b], 16)
            sp.dma_start(mask_i[:, :, :], a["mask_Bx1xSxS2_ik1"].rearrange("b o (t p) k -> p (b o t) k", p=P)).then_inc(mask_in, 16)
            sp.dma_start(ctx_sb[:, :, :], a["ctx_1024"].rearrange("b k d -> k b d")).then_inc(ctx_in, 16)
            sp.dma_start(gates_in[:, 0:2], bcast("g_xattn")).then_inc(gate_in, 16)
            sp.dma_start(gates_in[:, 2:4], bcast("g_ffn")).then_inc(gate_in, 16)
            for name, k in ROWS:
                src = a[name]
                src = src.rearrange("e (c p) -> (e c) p", p=D) if len(src.shape) == 2 else src.rearrange("(c p) -> c p", p=D)
                sp.dma_start(rows[ROW_AT[name]:ROW_AT[name] + k, :], src).then_inc(rows_in, 16)
            for i, name in enumerate(WEIGHTS):
                sp.dma_start(wn[:, i, :], a[name]).then_inc(w_in[i // 4], 16)
            for name in BC:
                sp.dma_start(bc[:, BC_AT[name], :], bcast(name)).then_inc(bc_in, 16)

            sp.wait_ge(const, C_KST)
            for L in range(2):
                for b in range(B):
                    sp.dma_start(kst[MROW:MROW + 3, L, :, b, 0:NK], onesb[0:3, 0:NK].unsqueeze(1).broadcast_to([3, H, NK])).then_inc(kst_in[L], 16)

            sp.wait_ge(setup_ev, 1)
            sp.dma_start(qst[0:NK, :, :], mnegT[:, :].unsqueeze(1).broadcast_to([NK, H, NTOK])).then_inc(mask_rows_in, 16)

            for L in range(2):
                sp.wait_ge(kparts_ready, L + 1)
                sp.dma_start(kd[L].rearrange("s p n -> p s n"), kparts[L][:, :, :, :].rearrange("p s b k -> p s (b k)")).then_inc(kd_out[L], 16)

            def k_stack(L):
                sp.wait_ge(kd_out[L], 16)
                for j, part in enumerate(KPART):
                    sp.dma_start(kst[QROW + DH * j:QROW + DH * j + DH, L, :, :, :].rearrange("p h b k -> p h (b k)"),
                                 kd[L, part].rearrange("(h d) n -> d h n", d=DH)).then_inc(kst_in[L], 16)

            k_stack(0)

            sp.dma_start(rw[:, :], a["L0_ffn_router_w"]).then_inc(moe_in[0], 16)
            sp.dma_start(sw1[:, :], a["L0_ffn_sw1"]).then_inc(moe_in[0], 16)
            sp.dma_start(sw2[:, :, :], a["L0_ffn_sw2"].rearrange("(c p) h -> p c h", p=P)).then_inc(moe_in[0], 16)

            def q_store(L, b):
                i = XI[L, b]
                sp.wait_ge(qparts_ready, i + 1)
                sp.dma_start(qd[i].rearrange("s p n -> p s n"), parts[:, :, :]).then_inc(qd_out[i], 16)

            def q_load(L, b):
                i = XI[L, b]
                dh = DH2 if L == "D" else DH
                nh = H2 if L == "D" else H
                row = 0 if L == "D" else QROW
                sp.wait_ge(qd_out[i], 16)
                for j, part in enumerate(QPART):
                    sp.dma_start(qst[row + dh * j:row + dh * j + dh, 0:nh, S * b:S * b + S],
                                 qd[i, part].rearrange("(h d) n -> d h n", d=dh)).then_inc(qst_in[i], 16)

            def k2_store(b):
                sp.wait_ge(k2parts_ready, b + 1)
                sp.dma_start(kd2[b].rearrange("s p n -> p s n"), parts[:, :, :]).then_inc(k2d_out[b], 16)

            def k2_load(b):
                sp.wait_ge(k2d_out[b], 16)
                for j, part in enumerate(KPART):
                    sp.dma_start(kst2[DH2 * j:DH2 * j + DH2, :, S * b:S * b + S],
                                 kd2[b, part].rearrange("(h d) n -> d h n", d=DH2)).then_inc(k2st_in[b], 16)

            def max_rows(L, b):
                i = XI[L, b]
                nh = H2 if L == "D" else H
                row = MROW2 if L == "D" else MROW
                sp.wait_ge(*done("nT", L, b))
                sp.dma_start(nd[i, 0:3 * nh], nsT[0:3 * nh, :]).then_inc(nd_out[i], 16)
                sp.wait_ge(nd_out[i], 16)
                sp.dma_start(qst[row:row + 3, 0:nh, S * b:S * b + S],
                             nd[i, 0:3 * nh].rearrange("(s h) n -> s h n", s=3)).then_inc(nst_in[i], 16)

            for b in range(B):
                q_store("A", b)
                q_load("A", b)
            k_stack(1)
            for b in range(B):
                max_rows("A", b)
            for e in range(E):
                sp.dma_start(w1[:, e, :], a["L0_ffn_w1"][e]).then_inc(moe_in[1], 16)
                sp.dma_start(w2[:, e, :, :], a["L0_ffn_w2"][e].rearrange("(c p) h -> p c h", p=P)).then_inc(moe_in[2], 16)
            sp.dma_start(b2[:, :, :], bcast("L0_ffn_b2")).then_inc(moe_in[2], 16)

            sp.wait_ge(fill_src, 1)
            sp.dma_start(xs_d.rearrange("(i p) r -> p i r", p=P), fill[:, :].unsqueeze(1).broadcast_to([P, ST, ROW])).then_inc(fill_xs, 16)
            sp.dma_start(y_d.rearrange("(c t p) d -> p (c t) d", p=P, t=NT), fill[:, 0:D].unsqueeze(1).broadcast_to([P, 2 * NT, D])).then_inc(fill_y, 16)

            sp.wait_ge(scat, 16 * 2 * NT)
            sp.dma_start(xg[:, :, :], xs_d.rearrange("(i p) r -> p i r", p=P)).then_inc(xg_in, 16)
            for i in range(4):
                sp.wait_ge(y_scats[i], 16 * (ST // 4))
            sp.dma_start(y12[:, :, :, :].rearrange("p c t d -> p (c t) d"), y_d.rearrange("(c t p) d -> p (c t) d", p=P, t=NT)).then_inc(y_in, 16)

            for b in range(B):
                q_store("C", b)
                q_load("C", b)
            for b in range(B):
                max_rows("C", b)
            for b in range(B):
                q_store("D", b)
                q_load("D", b)
                k2_store(b)
                k2_load(b)
            for b in range(B):
                max_rows("D", b)
            for b in range(B):
                sp.wait_ge(*done("y", "D", b))
                sp.dma_start(out_dram[:, b], xb[:, TB * b:TB * b + TB, :]).then_inc(out_sem, 16)
            sp.wait_ge(out_sem, 32)

        @block.gpsimd
        def _(pool):
            n_own = [0]

            def own(ins):
                n_own[0] += 1
                ins.then_inc(pol, 1)
                pool.wait_ge(pol, n_own[0])

            pool.memset(ident[:, :], 0.0).then_inc(const, 1)
            pool.wait_ge(const, 1)
            pool.affine_select(out=ident[:, :], in_=ident[:, :], compare_op=ALU.not_equal, fill=1.0, base=0,
                               pattern=[[-1, P]], channel_multiplier=1).then_inc(const, 1)
            pool.wait_ge(const, C_IDENT)
            pool.tensor_copy(identb[:, :], ident[:, :]).then_inc(const, 1)
            pool.memset(onesb[:, :], 1.0).then_inc(const, 1)
            pool.wait_ge(const, C_ONES)
            pool.affine_select(out=trib[:, :], in_=onesb[:, :], compare_op=ALU.is_gt, fill=0.0, base=0,
                               pattern=[[1, P]], channel_multiplier=-1).then_inc(const, 1)
            pool.memset(half[:, :], -0.5).then_inc(const, 1)
            pool.memset(kst[:, :, :, :, :].rearrange("p l h b k -> p (l h b k)").bitcast(U32), 0).then_inc(const, 1)

            def pow_rstd(L, b):
                n = 2 if L == "D" else 1
                pool.wait_ge(var_ready, LN[L, b] + 1)
                pool.tensor_tensor(rstd[:, b, 0:n, :], ve[:, b, 0:n, :],
                                   half[:, 0:n * TB].rearrange("p (n t) -> p n t", n=n), ALU.pow).then_inc(rstd_ready, 1)

            pool.wait_ge(const, C_HALF)
            pow_rstd("A", 0)
            pow_rstd("A", 1)
            pool.wait_ge(const, C_KST)
            kid = kst[0:NK, 0, :, :, 0:NK].rearrange("p h b k -> p (h b) k")
            pool.affine_select(out=kid, in_=kid, compare_op=ALU.not_equal, fill=BIG, base=0,
                               pattern=[[0, H * B], [-1, NK]], channel_multiplier=1).then_inc(const, 1)
            for L in range(2):
                own(pool.memset(vst[L][:, :, :, :], 0.0))
            for L in range(2):
                m = pool.memset(vst[L][0:NK, :, :, DH:DH + 1], 1.0)
                if L == 0:
                    own(m)
            m.then_inc(const, 1)
            pool.memset(n1[:, :, :], 0.0).then_inc(const, 1)
            pool.memset(fill[:, 0:D], 0.0)
            pool.memset(fill[:, D:ROW], NONE).then_inc(fill_src, 1)
            own(pool.iota(iota8i[:, :, :], pattern=[[0, NT], [1, E]], base=-E, channel_multiplier=0))
            own(pool.tensor_copy(iota8[:, :, :], iota8i[:, :, :]))
            own(pool.tensor_scalar(base320[:, :], iota8[:, 0, :], float(CAP), float(CAP * E), ALU.mult, ALU.add))
            own(pool.iota(toki[:, :], pattern=[[P, NT]], base=0, channel_multiplier=1))
            pool.tensor_copy(xn[:, :, D], toki[:, :]).then_inc(const, 1)
            own(pool.iota(sidx_i[:, :], pattern=[[0, ST // 5], [P, 5]], base=0, channel_multiplier=1))
            own(pool.tensor_copy(sidx[:, :], sidx_i[:, :]))
            own(pool.tensor_scalar(sidx_t[:, :], sidx[:, :], float(CAP), float(-CAP), ALU.is_ge, ALU.mult))
            pool.tensor_tensor(sidx[:, :], sidx[:, :], sidx_t[:, :], ALU.add).then_inc(const, 1)

            def x_bias(L, b, row, x_ready, value):
                pool.wait_ge(x_ready, value)
                t = slice(TB * b, TB * b + TB)
                pool.tensor_tensor(xb[:, t, :], x[:, t, :], bc[:, row, :].unsqueeze(1).broadcast_to([P, TB, D]),
                                   ALU.add).then_inc(xb_ready, 1)

            pool.wait_ge(bc_in, 16 * len(BC))
            pool.wait_ge(tg_ready, 1)
            pool.wait_ge(tgs_ready, 1)
            pool.tensor_scalar(bc[:, BC_AT["L0_xattn_bo"], :], bc[:, BC_AT["L0_xattn_bo"], :], tg[:, 0:1], None, ALU.mult).then_inc(bias_ready, 1)
            pool.tensor_scalar(bc[:, BC_AT["L1_xattn_bo"], :], bc[:, BC_AT["L1_xattn_bo"], :], tg[:, 1:2], None, ALU.mult).then_inc(bias_ready, 1)
            pool.tensor_scalar(bc[:, BC_AT["L0_ffn_sb2"], :], bc[:, BC_AT["L0_ffn_sb2"], :], tgs[:, 0:1], None, ALU.mult).then_inc(bias_ready, 1)
            pool.tensor_scalar(bc[:, BC_AT["L1_ffn_o_b"], :], bc[:, BC_AT["L1_ffn_o_b"], :], tg[:, 3:4], None, ALU.mult).then_inc(bias_ready, 1)
            pool.wait_ge(bias_ready, 4)
            for b in range(B):
                x_bias("A", b, BC_AT["L0_xattn_bo"], x_in[b], 16)

            for b in range(B):
                pow_rstd("B", b)
                x_bias("B", b, BC_AT["L0_ffn_sb2"], *done("y", "A", b))
            pool.wait_ge(slot_ready, 1)
            pool.wait_ge(fill_xs, 16)
            for c in range(2):
                for t in range(NT):
                    pool.indirect_dma_start(xs_d, bass.IndirectOffsetOnAxis(ap=slot_i[:, c, t:t + 1], axis=0),
                                            xn[:, t, :], None, bounds_check=SLOTS - 1, oob_is_err=False).then_inc(scat, 16)
            pool.wait_ge(dst_ready, 1)
            pool.wait_ge(fill_y, 16)
            for i in range(ST):
                pool.wait_ge(out_ev, 2 + i + 1)
                pool.indirect_dma_start(y_d, bass.IndirectOffsetOnAxis(ap=dst_i[:, i:i + 1], axis=0),
                                        ostage[:, i % 4, :], None, bounds_check=2 * NTOK - 1, oob_is_err=False).then_inc(y_scats[i % 4], 16)

            pool.wait_ge(out_mm, 2 + ST)
            own(pool.memset(vst2, 0.0))
            own(pool.memset(vst2[:, :, :, :, DH2:DH2 + 1], 1.0))
            pool.memset(kst2[MROW2:MROW2 + 3, :, :], 1.0).then_inc(const, 1)
            pool.wait_ge(const, C_KST2)

            for b in range(B):
                pow_rstd("C", b)
                x_bias("C", b, BC_AT["L1_xattn_bo"], x_moe, b + 1)
            for b in range(B):
                pow_rstd("D", b)
                pool.wait_ge(rstd_ready, LN["D", b] + 1)
                own(pool.tensor_scalar(rtg[:, b, :], rstd[:, b, 0, :], tg[:, 3:4], None, ALU.mult))
                for t in range(TB):
                    m = pool.tensor_scalar(xb[:, TB * b + t, :], x[:, TB * b + t, :], mv[:, b, t, 0:1], rtg[:, b, t:t + 1],
                                           ALU.subtract, ALU.mult)
                own(m)
                own(pool.tensor_tensor(xb[:, TB * b:TB * b + TB, :], xb[:, TB * b:TB * b + TB, :], x[:, TB * b:TB * b + TB, :], ALU.add))
                for t in range(TB):
                    k = D >> t
                    m = pool.tensor_tensor(xb[:, TB * b + t, 0:k], xb[:, TB * b + t, 0:k], bc[:, BC_AT["L1_ffn_o_b"], 0:k], ALU.add)
                m.then_inc(xb_ready, 1)

        @block.tensor
        def _(pe):
            def wait_bank(n):
                if n >= 2:
                    who, value = taken(n - 2)
                    pe.wait_ge(job_dve if who == "dve" else job_act, value)
                return wk[:, n % 2, :]

            def transposes_x(L, b):
                w = wait_bank(JOB["xT", L, b])
                for t in range(TB):
                    pe.wait_ge(xn_ready, TB * LN[L, b] + t + 1)
                    m = pe.transpose(w[:, P * t:P * t + P], xn[:, TB * b + t, 0:D], ident[:, :])
                m.then_inc(job_mm, 1)

            def x_cols(b, t=None):
                return xT[:, S * b:S * b + S] if t is None else xT[:, S * b + P * t:S * b + P * t + P]

            def wait_taken(name):
                pe.wait_ge(*done(*name))

            def project_q(L, b):
                w = wait_bank(JOB["q", L, b])
                wait_taken(("xT", L, b))
                pe.matmul(w, wT[:, 0 if L == "A" else 4, :], x_cols(b), start=True, stop=True).then_inc(job_mm, 1)

            def project_d(b):
                for name, i in (("q", 8), ("k", 9)):
                    w = wait_bank(JOB[name, "D", b])
                    wait_taken(("xT", "D", b))
                    for t in range(TB):
                        k = D >> t
                        m = pe.matmul(w[:, P * t:P * t + P], wT[0:k, i, :], x_cols(b, t)[0:k], start=True, stop=True)
                    m.then_inc(job_mm, 1)
                w = wait_bank(JOB["v", "D", b])
                for t in range(TB):
                    k = D >> t
                    m = pe.matmul(w[:, P * t:P * t + P], x_cols(b, t)[0:k], wT[0:k, 10, :], start=True, stop=True)
                m.then_inc(job_mm, 1)

            def scores_q(L, b, u):
                n = qm_index(L, b, u)
                if n >= 2:
                    pe.wait_ge(qm_max, n - 1)
                if u == 0:
                    pe.wait_ge(qst_in[XI[L, b]], 16 * 6)
                    if L == "A" and b == 0:
                        pe.wait_ge(mask_rows_in, 16)
                    if L == "A":
                        pe.wait_ge(kst_in[0], 16 * 8)
                        pe.wait_ge(const, C_KID)
                    if L == "C":
                        pe.wait_ge(kst_in[1], 16 * 8)
                    if L == "D":
                        pe.wait_ge(k2st_in[b], 16 * 6)
                        pe.wait_ge(const, C_KST2)
                if L == "D":
                    e, h = QM2[u]
                    m = pe.matmul(qm[:, n % 2, :], qst[0:MROW2, h, S * b + P * e:S * b + P * e + P],
                                  kst2[0:MROW2, h, S * b:S * b + S], start=True, stop=True)
                else:
                    t, g = u // 4, u % 4
                    for j in range(4):
                        h = 4 * g + j
                        m = pe.matmul(qm[:, n % 2, NK * j:NK * j + NK], qst[0:MROW, h, S * b + P * t:S * b + P * t + P],
                                      kst[0:MROW, 0 if L == "A" else 1, h, b, 0:NK], start=True, stop=True)
                m.then_inc(qm_mm, 1)

            def transposes_max(L, b):
                nh = 3 * (H2 if L == "D" else H)
                w = wait_bank(JOB["nT", L, b])
                pe.wait_ge(nsp_ready, XI[L, b] + 1)
                wb = w.bitcast(BF16)
                src = nsp[:, :, :, :].rearrange("p t s h -> p (t s h)")
                for t in range(TB):
                    m = pe.transpose(wb[0:nh, P * t:P * t + P], src[:, nh * t:nh * t + nh], identb[:, :])
                m.then_inc(job_mm, 1)

            def scores_t(L, b, u):
                n = t_index(L, b, u)
                if u == 0:
                    pe.wait_ge(nst_in[XI[L, b]], 16)
                if n >= 2:
                    pe.wait_ge(t_exp, n - 1)
                dst = ts[:, 2 * (n % 2):2 * (n % 2) + 2, :].rearrange("p a b -> p (a b)")
                if L == "D":
                    kt, k = u // 2, u % 2
                    for h, at in PACKS[k]:
                        m = pe.matmul(dst[:, at:at + NQ[h]], kst2[0:MROW2 + 3, h, S * b + P * kt:S * b + P * kt + P],
                                      qst[0:MROW2 + 3, h, S * b:S * b + NQ[h]], start=True, stop=True)
                else:
                    for j in range(2):
                        h = 2 * u + j
                        m = pe.matmul(dst[:, S * j:S * j + S], kst[:, 0 if L == "A" else 1, h, b, :],
                                      qst[:, h, S * b:S * b + S], start=True, stop=True)
                m.then_inc(t_mm, 1)

            def values(L, b, g):
                w = wait_bank(JOB["pv", L, b, g])
                if b == 0 and g == 0:
                    pe.wait_ge(vst_ready, 4)
                pe.wait_ge(t_exp, t_index(L, b, 2 * g + 1) + 1)
                for j in range(4):
                    h = 4 * g + j
                    m = pe.matmul(w[32 * j:32 * j + 32, :], vst[0 if L == "A" else 1][:, b, h, :], pr[:, h, :],
                                  start=True, stop=True)
                m.then_inc(job_mm, 1)

            def values_d(b, kt):
                ws = [wk[:, JOB["pv", "D", b, g] % 2, :] for g in range(2)]
                if kt == 0:
                    wait_bank(JOB["pv", "D", b, 0])
                    wait_bank(JOB["pv", "D", b, 1])
                    wait_taken(("v", "D", b))
                pe.wait_ge(t_exp, t_index("D", b, 2 * kt + 1) + 1)
                for g in range(2):
                    for j in range(4):
                        h = 4 * g + j
                        m = pe.matmul(ws[g][32 * j:32 * j + 32, 0:NQ[h]], vst2[:, b, kt, h, :],
                                      pr2[:, kt, P2AT[h]:P2AT[h] + NQ[h]], start=(kt == 0), stop=(kt == TB - 1))
                    if kt == TB - 1:
                        m.then_inc(job_mm, 1)

            def epilogue(L, b):
                for g in range(4):
                    w = wait_bank(JOB["oT", L, b, g])
                    wait_taken(("pv", L, b, g))
                    for t in range(TB):
                        m = pe.transpose(w[:, P * t:P * t + P], oT[:, g, P * t:P * t + P], ident[:, :])
                    m.then_inc(job_mm, 1)
                w = wait_bank(JOB["onT", L, b])
                wait_taken(("oT", L, b, 3))
                for t in range(TB):
                    m = pe.transpose(w[:, P * t:P * t + P], on[:, t, :], ident[:, :])
                m.then_inc(job_mm, 1)
                w = wait_bank(JOB["y", L, b])
                wait_taken(("onT", L, b))
                for t in range(TB):
                    m = pe.matmul(w[:, P * t:P * t + P], onT[:, P * t:P * t + P], wT[:, 3 if L == "A" else 7, :],
                                  start=True, stop=True)
                m.then_inc(job_mm, 1)

            def epilogue_d(b):
                w = wait_bank(JOB["oT", "D", b, 0])
                wait_taken(("pv", "D", b, 1))
                at = 0
                for e in range(TB):
                    for g in range(max(1, HEADS_OF[e] // 4)):
                        n = 32 * min(4, HEADS_OF[e])
                        m = pe.transpose(w[:, at:at + n], oT[0:n, g, P * e:P * e + P], ident[0:n, 0:n])
                        at += n
                m.then_inc(job_mm, 1)
                w = wait_bank(JOB["onT", "D", b])
                wait_taken(("oT", "D", b, 0))
                onf = on[:, :, :].rearrange("p t d -> p (t d)")
                at = 0
                for e in range(TB):
                    n = D >> e
                    m = pe.transpose(w[0:n, P * e:P * e + P], onf[:, at:at + n], ident[:, :])
                    at += n
                m.then_inc(job_mm, 1)
                w = wait_bank(JOB["y", "D", b])
                wait_taken(("onT", "D", b))
                for e in range(TB):
                    n = D >> e
                    m = pe.matmul(w[:, P * e:P * e + n], onT[0:n, P * e:P * e + P], wT[0:n, 11, 0:n], start=True, stop=True)
                m.then_inc(job_mm, 1)

            pe.wait_ge(const, C_IDENTB)
            pe.wait_ge(mneg_ready, 1)
            for t in range(NT):
                m = pe.transpose(qm[:, 0, :].bitcast(BF16)[0:NK, P * t:P * t + P], mneg[:, t, :], identb[:, :])
            m.then_inc(setup_mm, 1)
            pe.wait_ge(some_ready, 1)
            for t in range(TB):
                m = pe.matmul(qm[:, 1, P * t:P * t + P], some_b[:, t:t + 1].broadcast_to([P, P]), identb[:, :], start=True, stop=True)
            m.then_inc(setup_mm, 1)
            pe.wait_ge(w_in[0], 64)
            for i in range(4):
                m = pe.transpose(ts[:, 0, P * i:P * i + P], wn[:, i, :], ident[:, :])
            m.then_inc(setup_mm, 1)
            pe.wait_ge(rows_in, 16 * len(ROWS))
            pe.wait_ge(ctx_in, 16)
            pe.transpose(ts[:, 1, 0:NROWS], rows[:, :], ident[0:NROWS, 0:NROWS])
            for b in range(B):
                m = pe.transpose(ts[:, 1, P + NK * b:P + NK * b + NK], ctx_sb[:, b, :], ident[0:NK, 0:NK])
            m.then_inc(setup_mm, 1)
            for g in (1, 2):
                pe.wait_ge(w_in[g], 64)
                for i in range(4):
                    m = pe.transpose(ts[:, 1 + g, P * i:P * i + P], wn[:, 4 * g + i, :], ident[:, :])
                m.then_inc(setup_mm, 1)
            pe.wait_ge(setup_ev, 1)
            for t in range(TB):
                m = pe.matmul(qm[:, 0, P * t:P * t + P], some_b[:, TB + t:TB + t + 1].broadcast_to([P, P]), identb[:, :], start=True, stop=True)
            m.then_inc(setup_mm, 1)

            transposes_x("A", 0)
            pe.wait_ge(setup_ev, 3)
            project_q("A", 0)
            pe.wait_ge(setup_ev, 5)
            pe.matmul(ts[:, 0, 0:B * NK], wT[:, 1, :], ctxT[:, :], start=True, stop=True).then_inc(kv_mm, 1)
            pe.matmul(ts[:, 1, 0:B * NK], wT[:, 5, :], ctxT[:, :], start=True, stop=True).then_inc(kv_mm, 1)
            for L in range(2):
                for b in range(B):
                    m = pe.matmul(ts[0:NK, 2, P * (2 * L + b):P * (2 * L + b) + P], ctxT[:, NK * b:NK * b + NK], wT[:, 4 * L + 2, :],
                                  start=True, stop=True)
            m.then_inc(kv_mm, 1)
            transposes_x("A", 1)
            project_q("A", 1)

            def attention(L):
                nq = QM_UNITS[L]
                for u in range(nq):
                    scores_q(L, 0, u)
                transposes_max(L, 0)
                lead = nq - T_UNITS
                for u in range(lead):
                    scores_q(L, 1, u)
                for u in range(T_UNITS):
                    scores_q(L, 1, lead + u)
                    scores_t(L, 0, u)
                    if L != "D" and u >= 2 and u % 2 == 0:
                        values(L, 0, u // 2 - 1)
                    if L == "D" and u >= 2 and u % 2 == 0:
                        values_d(0, u // 2 - 1)
                if L == "D":
                    values_d(0, 3)
                else:
                    values(L, 0, 3)
                transposes_max(L, 1)
                (epilogue_d(0) if L == "D" else epilogue(L, 0))
                for u in range(T_UNITS):
                    scores_t(L, 1, u)
                    if u >= 2 and u % 2 == 0:
                        (values_d(1, u // 2 - 1) if L == "D" else values(L, 1, u // 2 - 1))
                if L == "D":
                    values_d(1, 3)
                    epilogue_d(1)
                else:
                    values(L, 1, 3)
                    epilogue(L, 1)

            pe.wait_ge(setup_ev, 7)
            pe.wait_ge(vst_ready, 4)
            pe.wait_ge(kparts_ready, 2)
            attention("A")

            for b in range(B):
                transposes_x("B", b)
            w = wait_bank(JOB["logits",])
            wait_taken(("xT", "B", 1))
            pe.wait_ge(moe_in[0], 48)
            for t in range(NT):
                m = pe.matmul(w[:, E * t:E * t + E], xT[:, P * t:P * t + P], rw[:, :], start=True, stop=True)
            m.then_inc(job_mm, 1)

            def hidden(n, lhs, rhs, width):
                if n >= 4:
                    pe.wait_ge(hid_act, n - 3)
                elif n == 0:
                    pe.wait_ge(t_exp, t_index("A", 1, T_UNITS - 1) + 1)
                pe.matmul(ts[:, n % 4, 0:width], lhs, rhs, start=True, stop=True).then_inc(hid_mm, 1)

            for c in range(FC):
                for b in range(B):
                    hidden(2 * c + b, sw1[:, P * c:P * c + P], x_cols(b), S)
                if c == 0:
                    w = wait_bank(JOB["pos",])
                    pe.wait_ge(hot_ready, 1)
                    wv = w[:, 0:2 * NT * E].rearrange("p (c t e) -> p c t e", c=2, t=NT)
                    pe.matmul(w[:, 2 * NT * E:3 * NT * E], onesb[:, :], hotb[:, 0, :, :].rearrange("p t e -> p (t e)"),
                              start=True, stop=True)
                    for t in range(NT - 1):
                        for ch in range(2):
                            pe.matmul(wv[:, ch, t + 1:, :], onesb[:, :],
                                      hotb[:, ch, t, :].unsqueeze(1).broadcast_to([P, NT - 1 - t, E]),
                                      start=False, stop=False, skip_group_check=True)
                    pe.matmul(w[:, 0:2 * NT * E], trib[:, :], hotb[:, :, :, :].rearrange("p c t e -> p (c t e)"),
                              start=False, stop=True, skip_group_check=True).then_inc(job_mm, 1)
            for b in range(B):
                pe.wait_ge(hid_act, 2 * FC)
                if b == 0:
                    pe.wait_ge(qm_max, qm_index("A", 1, 15) + 1)
                for t in range(TB):
                    for c in range(FC):
                        m = pe.matmul(qm[:, b, P * t:P * t + P], hs[:, c, S * b + P * t:S * b + P * t + P], sw2[:, c, :],
                                      start=(c == 0), stop=(c == FC - 1))
                m.then_inc(out_mm, 1)
            pe.wait_ge(xg_in, 16)
            for n in range(ST // 4):
                w = wait_bank(JOB["xg", n])
                for j in range(4):
                    m = pe.transpose(w[:, P * j:P * j + P], xg[:, 4 * n + j, 0:D], ident[:, :])
                m.then_inc(job_mm, 1)

            def expert_hidden(e):
                if e == 0:
                    pe.wait_ge(moe_in[1], 16 * E)
                who, value = taken(JOB["xg", (CAP * (e + 1) - 1) // 512])
                pe.wait_ge(job_act, value)
                for c in range(FC):
                    hidden(2 * FC + FC * e + c, w1[:, e, P * c:P * c + P], xgT[:, CAP * e:CAP * e + CAP], CAP)

            def expert_out(i):
                n = 2 + i
                pe.wait_ge(out_ev, n - 1)
                k, r = 2 * (i // 5), i % 5
                pieces = {0: [(k, 0, P, 0)], 1: [(k, P, P, 0)], 2: [(k, 2 * P, 64, 0), (k + 1, 0, 64, 64)],
                          3: [(k + 1, 64, P, 0)], 4: [(k + 1, 64 + P, P, 0)]}[r]
                for e, s0, m_, p0 in pieces:
                    pe.wait_ge(hid_act, 2 * FC + FC * e + FC)
                    for c in range(FC):
                        m = pe.matmul(qm[p0:p0 + m_, n % 2, 0:D], he[:, e % 3, c, s0:s0 + m_], w2[:, e, c, :],
                                      start=(c == 0), stop=(c == FC - 1))
                m.then_inc(out_mm, 1)

            expert_hidden(0)
            pe.wait_ge(moe_in[2], 16 * (E + 1))
            for e in range(E):
                if e + 1 < E:
                    expert_hidden(e + 1)
                for i in ((5 * (e // 2), 5 * (e // 2) + 1) if e % 2 == 0 else (5 * (e // 2) + 2, 5 * (e // 2) + 3, 5 * (e // 2) + 4)):
                    expert_out(i)

            transposes_x("C", 0)
            project_q("C", 0)
            transposes_x("C", 1)
            project_q("C", 1)
            pe.wait_ge(out_ev, 2 + ST)
            pe.wait_ge(hid_act, 2 * FC + FC * E)
            attention("C")
            for b in range(B):
                transposes_x("D", b)
                project_d(b)
            attention("D")

        @block.scalar
        def _(act):
            def job(name):
                n = JOB[name]
                act.wait_ge(job_mm, n + 1)
                return wk[:, n % 2, :]

            def take_xT(L, b):
                w = job(("xT", L, b))
                dst = xT[:, S * b:S * b + S]
                if L == "D":
                    act.activation(dst, w, ACT.Identity, scale=col[:, ROW_AT["L1_ffn_norm_w"]:ROW_AT["L1_ffn_norm_w"] + 1],
                                   bias=col[:, ROW_AT["L1_ffn_norm_b"]:ROW_AT["L1_ffn_norm_b"] + 1]).then_inc(job_act, 1)
                else:
                    act.activation(dst, w, ACT.Copy).then_inc(job_act, 1)

            def exps(L, b, u):
                n = t_index(L, b, u)
                act.wait_ge(t_mm, n + 1)
                src = ts[:, 2 * (n % 2):2 * (n % 2) + 2, :].rearrange("p a b -> p (a b)")
                if L == "D":
                    kt, k = u // 2, u % 2
                    if b == 1 and u == 0:
                        act.wait_ge(job_mm, JOB["pv", L, 0, 1] + 1)
                    act.activation(pr2[:, kt, PACK_AT[k]:PACK_AT[k] + PACK_W[k]], src[:, 0:PACK_W[k]], ACT.Exp).then_inc(t_exp, 1)
                else:
                    if b == 1 and u % 2 == 0:
                        act.wait_ge(job_mm, JOB["pv", L, 0, u // 2] + 1)
                    act.activation(pr[:, 2 * u:2 * u + 2, :].rearrange("p h n -> p (h n)"), src, ACT.Exp).then_inc(t_exp, 1)

            def take_onT(L, b):
                w = job(("onT", L, b))
                if L == "D":
                    for e in range(TB):
                        n = D >> e
                        m = act.activation(onT[0:n, P * e:P * e + P], w[0:n, P * e:P * e + P], ACT.Copy)
                    m.then_inc(job_act, 1)
                else:
                    act.activation(onT[:, :], w, ACT.Copy).then_inc(job_act, 1)

            act.wait_ge(gate_in, 32)
            act.activation(tg[:, :], gates_in[:, :], ACT.Tanh).then_inc(tg_ready, 1)
            act.wait_ge(setup_mm, 1)
            act.activation(mnegT[:, :], qm[:, 0, :].bitcast(BF16)[0:NK, :], ACT.Copy).then_inc(setup_ev, 1)
            act.wait_ge(setup_mm, 2)
            act.activation(someB[:, 0:S], qm[:, 1, :], ACT.Copy).then_inc(setup_ev, 1)
            act.wait_ge(setup_mm, 3)
            act.activation(wT[:, 0:4, :].rearrange("p i d -> p (i d)"), ts[:, 0, :], ACT.Copy).then_inc(setup_ev, 1)
            act.wait_ge(setup_mm, 4)
            act.activation(ctxT[:, :], ts[:, 1, P:P + B * NK], ACT.Copy)
            act.activation(col[:, :], ts[:, 1, 0:NROWS], ACT.Copy).then_inc(setup_ev, 1)
            act.wait_ge(setup_mm, 5)
            act.activation(wT[:, 4:8, :].rearrange("p i d -> p (i d)"), ts[:, 2, :], ACT.Copy).then_inc(setup_ev, 1)
            act.wait_ge(setup_mm, 6)
            act.activation(wT[:, 8:12, :].rearrange("p i d -> p (i d)"), ts[:, 3, :], ACT.Copy).then_inc(setup_ev, 1)
            act.wait_ge(setup_mm, 7)
            act.activation(someB[:, S:2 * S], qm[:, 0, :], ACT.Copy).then_inc(setup_ev, 1)

            def attention(L):
                for u in range(T_UNITS):
                    exps(L, 0, u)
                take_onT(L, 0)
                for u in range(T_UNITS):
                    exps(L, 1, u)
                take_onT(L, 1)

            for b in range(B):
                take_xT("A", b)
            attention("A")

            for b in range(B):
                take_xT("B", b)
            act.wait_ge(*done("logits"))
            act.activation(gates[:, :, :], lg[:, :, :], ACT.Exp).then_inc(ex_ready, 1)
            for n in range(2 * FC):
                c, b = n // 2, n % 2
                act.wait_ge(hid_mm, n + 1)
                k = ROW_AT["L0_ffn_sb1"] + c
                act.activation(hs[:, c, S * b:S * b + S], ts[:, n % 4, :], ACT.Silu, bias=col[:, k:k + 1]).then_inc(hid_act, 1)
            for n in range(ST // 4):
                w = job(("xg", n))
                act.activation(xgT[:, 512 * n:512 * n + 512], w, ACT.Copy).then_inc(job_act, 1)
            for e in range(E):
                if e >= 3:
                    last = 5 * ((e - 3) // 2) + (2 if (e - 3) % 2 == 0 else 4)
                    act.wait_ge(out_mm, 2 + last + 1)
                for c in range(FC):
                    n = 2 * FC + FC * e + c
                    act.wait_ge(hid_mm, n + 1)
                    k = ROW_AT["L0_ffn_b1"] + FC * e + c
                    act.activation(he[:, e % 3, c, :], ts[:, n % 4, 0:CAP], ACT.Silu, bias=col[:, k:k + 1]).then_inc(hid_act, 1)

            for b in range(B):
                take_xT("C", b)
            attention("C")
            for b in range(B):
                take_xT("D", b)
            attention("D")

        @block.vector
        def _(v):
            n_own = [0]

            def own(ins):
                n_own[0] += 1
                ins.then_inc(dve, 1)
                v.wait_ge(dve, n_own[0])

            def job(name):
                n = JOB[name]
                v.wait_ge(job_mm, n + 1)
                return wk[:, n % 2, :]

            def norm_stats(L, b):
                for t in range(TB):
                    m = v.bn_stats(stats[:, t, :], x[:, TB * b + t, :])
                own(m)
                for t in range(TB):
                    m = v.bn_aggr(mv[:, b, t, :], stats[:, t, :])
                own(m)
                if L == "D":
                    v.tensor_scalar(ve[:, b, 1, :], mv[:, b, :, 1], 1.0 + EPS, EPS * EPS, ALU.mult, ALU.add)
                v.tensor_scalar(ve[:, b, 0, :], mv[:, b, :, 1], EPS, None, ALU.add).then_inc(var_ready, 1)

            def norm(L, b):
                v.wait_ge(rstd_ready, LN[L, b] + 1)
                for t in range(TB):
                    v.tensor_scalar(xn[:, TB * b + t, 0:D], x[:, TB * b + t, :], mv[:, b, t, 0:1],
                                    rstd[:, b, 1 if L == "D" else 0, t:t + 1], ALU.subtract, ALU.mult).then_inc(xn_ready, 1)

            def split3(src, rest, dst, last_inc):
                own(v.tensor_copy(dst[0], src))
                own(v.tensor_tensor(rest, src, dst[0], ALU.subtract))
                own(v.tensor_copy(dst[1], rest))
                v.tensor_tensor(dst[2], rest, dst[1], ALU.subtract).then_inc(*last_inc)

            def take_q(L, b):
                i = XI[L, b]
                if i >= 1:
                    if L == "D" and b == 1:
                        v.wait_ge(k2d_out[0], 16)
                    else:
                        v.wait_ge(qd_out[i - 1], 16)
                w = job(("q", L, b))
                if L == "A":
                    v.wait_ge(setup_ev, 2 if b == 0 else 7)
                    if b == 0:
                        v.wait_ge(setup_ev, 4)
                    k = ROW_AT["L0_xattn_bq"]
                    m = v.scalar_tensor_tensor(qf[:, :], w, col[:, k:k + 1], someB[:, S * b:S * b + S], ALU.add, ALU.mult)
                elif L == "C":
                    m = v.tensor_copy(qf[:, :], w)
                else:
                    k = ROW_AT["L1_ffn_q_b"]
                    m = v.tensor_scalar(qf[:, :], w, col[:, k:k + 1], None, ALU.add)
                m.then_inc(job_dve, 1)
                v.wait_ge(*done("q", L, b))
                split3(qf[:, :], qr[:, :], [parts[:, s, :] for s in range(3)], (qparts_ready, 1))

            def take_k2(b):
                v.wait_ge(qd_out[XI["D", b]], 16)
                w = job(("k", "D", b))
                k = ROW_AT["L1_ffn_k_b"]
                v.tensor_scalar(qf[:, :], w, col[:, k:k + 1], float(D) ** -0.5, ALU.add, ALU.mult).then_inc(job_dve, 1)
                v.wait_ge(*done("k", "D", b))
                split3(qf[:, :], qr[:, :], [parts[:, s, :] for s in range(3)], (k2parts_ready, 1))

            def take_v2(b):
                w = job(("v", "D", b))
                v.tensor_tensor(vst2[:, b, :, :, 0:DH2], w.rearrange("p (t h d) -> p t h d", t=TB, d=DH2),
                                bc[:, BC_AT["L1_ffn_v_b"], :].rearrange("p (h d) -> p h d", d=DH2).unsqueeze(1).broadcast_to([P, TB, H2, DH2]),
                                ALU.add).then_inc(job_dve, 1)

            def take_max(L, b, u):
                n = qm_index(L, b, u)
                v.wait_ge(qm_mm, n + 1)
                if L == "D":
                    e, h = QM2[u]
                    dst = nmx[:, :, :].rearrange("p t h -> p (t h)")[:, H2 * e + h:H2 * e + h + 1]
                    v.tensor_reduce(dst, qm[:, n % 2, :], AX.X, ALU.max, negate=True).then_inc(qm_max, 1)
                else:
                    t, g = u // 4, u % 4
                    v.tensor_reduce(nmx[:, t, 4 * g:4 * g + 4], qm[:, n % 2, 0:4 * NK].rearrange("p (h k) -> p h k", k=NK),
                                    AX.X, ALU.max, negate=True).then_inc(qm_max, 1)

            def split_max(L, b):
                i = XI[L, b]
                nh = H2 if L == "D" else H
                v.wait_ge(qm_max, qm_index(L, b, QM_UNITS[L] - 1) + 1)
                if L == "D":
                    src = nmx[:, :, :].rearrange("p t h -> p (t h)")[:, 0:TB * nh].rearrange("p (t h) -> p t h", h=nh)
                    rest = nmr[:, :, :].rearrange("p t h -> p (t h)")[:, 0:TB * nh].rearrange("p (t h) -> p t h", h=nh)
                    sp_ = nsp[:, :, :, :].rearrange("p t s h -> p (t s h)")[:, 0:TB * 3 * nh].rearrange("p (t s h) -> p t s h", s=3, h=nh)
                else:
                    src, rest, sp_ = nmx[:, :, :], nmr[:, :, :], nsp[:, :, :, :]
                split3(src, rest, [sp_[:, :, s, :] for s in range(3)], (nsp_ready, 1))
                if i >= 1:
                    v.wait_ge(nd_out[i - 1], 16)
                w = job(("nT", L, b))
                v.tensor_copy(nsT[0:3 * nh, :], w.bitcast(BF16)[0:3 * nh, 0:S]).then_inc(job_dve, 1)

            def take_pv(L, b, g):
                w = job(("pv", L, b, g))
                if L == "D":
                    if g == 0:
                        v.tensor_copy(oT[:, 0, 0:2 * P], w[:, 0:2 * P])
                        v.tensor_copy(oT[0:64, 0, 2 * P:3 * P], w[0:64, 2 * P:3 * P])
                        v.tensor_copy(oT[0:32, 0, 3 * P:4 * P], w[0:32, 3 * P:4 * P]).then_inc(job_dve, 1)
                    else:
                        v.tensor_copy(oT[:, 1, 0:P], w[:, 0:P]).then_inc(job_dve, 1)
                else:
                    v.tensor_copy(oT[:, g, :], w).then_inc(job_dve, 1)

            def divide(L, b):
                for g in range(4):
                    w = job(("oT", L, b, g))
                    wv = w.rearrange("p (t j r) -> p t j r", t=TB, r=32)
                    own(v.reciprocal(rden[:, :].rearrange("p (t j) -> p t j", t=TB), wv[:, :, :, DH]))
                    v.tensor_tensor(on[:, :, 32 * g:32 * g + 32].rearrange("p t (j d) -> p t j d", d=DH),
                                    wv[:, :, :, 0:DH],
                                    rden[:, :].rearrange("p (t j) -> p t j", t=TB).unsqueeze(3).broadcast_to([P, TB, 4, DH]),
                                    ALU.mult).then_inc(job_dve, 1)
                    v.wait_ge(*done("oT", L, b, g))

            def divide_d(b):
                w = job(("oT", "D", b, 0))
                nb = len(BLOCKS)
                wv = w[:, 0:32 * nb].rearrange("p (n r) -> p n r", r=32)
                own(v.reciprocal(rden[:, 0:nb], wv[:, :, DH2]))
                v.tensor_tensor(on[:, :, :].rearrange("p t d -> p (t d)")[:, 0:DH2 * nb].rearrange("p (n d) -> p n d", d=DH2),
                                wv[:, :, 0:DH2], rden[:, 0:nb].unsqueeze(2).broadcast_to([P, nb, DH2]), ALU.mult).then_inc(job_dve, 1)

            def residual(L, b):
                w = job(("y", L, b))
                v.wait_ge(xb_ready, {"A": 0, "B": 2, "C": 4, "D": 6}[L] + b + 1)
                if L == "D":
                    for e in range(TB):
                        k = D >> e
                        o = xb[:, TB * b + e, 0:k]
                        m = v.scalar_tensor_tensor(o, w[:, P * e:P * e + k], tg[:, 3:4], o, ALU.mult, ALU.add)
                else:
                    g = 0 if L == "A" else 1
                    t = slice(TB * b, TB * b + TB)
                    m = v.scalar_tensor_tensor(x[:, t, :].rearrange("p t d -> p (t d)"), w, tg[:, g:g + 1],
                                               xb[:, t, :].rearrange("p t d -> p (t d)"), ALU.mult, ALU.add)
                m.then_inc(job_dve, 1)
                v.wait_ge(*done("y", L, b))

            def take_kv():
                v.wait_ge(kpad, 2)
                for L in range(2):
                    v.wait_ge(kv_mm, L + 1)
                    k = ROW_AT["L0_xattn_bk"]
                    if L == 0:
                        own(v.tensor_scalar(kf[:, :], ts[:, 0, 0:B * NK], col[:, k:k + 1], float(DH) ** -0.5, ALU.add, ALU.mult))
                    else:
                        own(v.tensor_scalar(kf[:, :], ts[:, 1, 0:B * NK], float(DH) ** -0.5, None, ALU.mult))
                    split3(kf[:, :].rearrange("p (b k) -> p b k", b=B), kr[:, :].rearrange("p (b k) -> p b k", b=B),
                           [kparts[L][:, s, :, 0:NK] for s in range(3)], (kparts_ready, 1))
                v.wait_ge(kv_mm, 3)
                v.wait_ge(const, C_VST)
                v.wait_ge(bc_in, 16 * len(BC))
                for L in range(2):
                    for b in range(B):
                        src = ts[0:NK, 2, P * (2 * L + b):P * (2 * L + b) + P].rearrange("p (h d) -> p h d", d=DH)
                        dst = vst[L][0:NK, b, :, 0:DH]
                        if L == 0:
                            bv = bc[0:NK, BC_AT["L0_xattn_bv"], :].rearrange("p (h d) -> p h d", d=DH)
                            v.tensor_tensor(dst, src, bv, ALU.add).then_inc(vst_ready, 1)
                        else:
                            v.tensor_copy(dst, src).then_inc(vst_ready, 1)

            def attention(L, after0, after1):
                nq = QM_UNITS[L]
                n_pv = 2 if L == "D" else 4
                for u in range(nq):
                    take_max(L, 0, u)
                split_max(L, 0)
                lead = nq - T_UNITS
                for u in range(lead):
                    take_max(L, 1, u)
                for u in range(T_UNITS):
                    take_max(L, 1, lead + u)
                    if L != "D" and u >= 2 and u % 2 == 0:
                        take_pv(L, 0, u // 2 - 1)
                if L == "D":
                    take_pv(L, 0, 0)
                    take_pv(L, 0, 1)
                else:
                    take_pv(L, 0, 3)
                split_max(L, 1)
                (divide_d(0) if L == "D" else divide(L, 0))
                residual(L, 0)
                after0()
                for g in range(n_pv):
                    take_pv(L, 1, g)
                (divide_d(1) if L == "D" else divide(L, 1))
                residual(L, 1)
                after1()

            def then_norm(L, b):
                def run():
                    norm_stats(L, b)
                    norm(L, b)
                return run

            v.memset(kparts[0][:, :, :, NK:P], 0.0).then_inc(kpad, 1)
            v.memset(kparts[1][:, :, :, NK:P], 0.0).then_inc(kpad, 1)
            own(v.memset(nmx[:, :, :], 0.0))
            for b in range(B):
                v.wait_ge(x_in[b], 16)
                norm_stats("A", b)
            v.wait_ge(mask_in, 16)
            own(v.tensor_scalar(keep[:, :, :], mask_i[:, :, :], 0.0, None, ALU.not_equal))
            own(v.tensor_reduce(some[:, :], keep[:, :, :], AX.X, ALU.max))
            v.tensor_copy(some_b[:, :], some[:, :]).then_inc(some_ready, 1)
            own(v.tensor_scalar(none[:, :], some[:, :], -1.0, 1.0, ALU.mult, ALU.add))
            own(v.tensor_tensor(keep[:, :, :], keep[:, :, :], none[:, :].unsqueeze(2).broadcast_to([P, NT, NK]), ALU.max))
            v.tensor_scalar(mneg[:, :, :], keep[:, :, :], -1.0, None, ALU.add).then_inc(mneg_ready, 1)
            for b in range(B):
                norm("A", b)
            v.wait_ge(tg_ready, 1)
            v.tensor_scalar(tgs[:, :], tg[:, 2:3], SHARED_SCALE, None, ALU.mult).then_inc(tgs_ready, 1)
            take_q("A", 0)
            take_kv()
            take_q("A", 1)
            attention("A", then_norm("B", 0), then_norm("B", 1))

            flat = lambda t: t[:, :, :, :].rearrange("p c t e -> p (c t e)")
            both = lambda t: t[:, :, :].unsqueeze(1).broadcast_to([P, 2, NT, E])
            wide = lambda t: t[:, :].unsqueeze(2).broadcast_to([P, NT, E])
            v.wait_ge(const, C_SIDX)
            w = job(("logits",))
            lv = w[:, 0:NT * E].rearrange("p (t e) -> p t e", e=E)
            own(v.tensor_reduce(best[:, :], lv, AX.X, ALU.max))
            v.tensor_tensor(lg[:, :, :], lv, wide(best), ALU.subtract).then_inc(job_dve, 1)
            v.wait_ge(ex_ready, 1)
            own(v.tensor_reduce(sums[:, :], gates[:, :, :], AX.X, ALU.add))
            own(v.reciprocal(sums[:, :], sums[:, :]))
            own(v.tensor_tensor(gates[:, :, :], gates[:, :, :], wide(sums), ALU.mult))

            def choose(src, c):
                own(v.tensor_reduce(best[:, :], src, AX.X, ALU.max))
                own(v.tensor_tensor(cand[:, :, :], src, wide(best), ALU.is_equal))
                own(v.tensor_tensor(cand[:, :, :], cand[:, :, :], iota8[:, :, :], ALU.mult))
                own(v.tensor_reduce(first[:, :], cand[:, :, :], AX.X, ALU.min))
                own(v.tensor_tensor(hot[:, c, :, :], iota8[:, :, :], wide(first), ALU.is_equal))

            choose(gates[:, :, :], 0)
            own(v.tensor_tensor(cand[:, :, :], iota8[:, :, :], wide(first), ALU.not_equal))
            own(v.tensor_tensor(gates2[:, :, :], gates[:, :, :], cand[:, :, :], ALU.mult))
            choose(gates2[:, :, :], 1)
            v.tensor_copy(flat(hotb), flat(hot)).then_inc(hot_ready, 1)
            w = job(("pos",))
            n = 2 * NT * E
            own(v.tensor_reduce(n1[:, 1, :], w[:, n:n + NT * E].rearrange("p (t e) -> p e t", e=E), AX.X, ALU.add))
            own(v.tensor_scalar(n1[:, 1, :], n1[:, 1, :], float(CAP), None, ALU.min))
            v.tensor_tensor(posn[:, :, :, :], w[:, 0:n].rearrange("p (c t e) -> p c t e", c=2, t=NT),
                            n1[:, :, :].unsqueeze(2).broadcast_to([P, 2, NT, E]), ALU.add).then_inc(job_dve, 1)
            v.wait_ge(*done("pos"))
            v.scalar_tensor_tensor(flat(kept), flat(posn), float(CAP), flat(hot), ALU.is_lt, ALU.mult)
            own(v.tensor_tensor(rt[:, :, :, :], posn[:, :, :, :],
                                base320[:, :].unsqueeze(1).unsqueeze(1).broadcast_to([P, 2, NT, E]), ALU.add))
            own(v.tensor_tensor(flat(rt), flat(rt), flat(hot), ALU.mult))
            v.tensor_reduce(s12[:, :, :], rt[:, :, :, :], AX.X, ALU.add)
            own(v.tensor_reduce(k12[:, :, :], kept[:, :, :, :], AX.X, ALU.add))
            own(v.tensor_scalar(k12[:, :, :], k12[:, :, :], -NONE, NONE, ALU.mult, ALU.add))
            v.tensor_tensor(slot_i[:, :, :], s12[:, :, :], k12[:, :, :], ALU.add).then_inc(slot_ready, 1)
            own(v.tensor_tensor(rt[:, :, :, :], kept[:, :, :, :], both(gates), ALU.mult))
            own(v.tensor_reduce(g12[:, :, :], rt[:, :, :, :], AX.X, ALU.add))
            own(v.tensor_tensor(den[:, :], g12[:, 0, :], g12[:, 1, :], ALU.add))
            own(v.tensor_scalar(den[:, :], den[:, :], FEPS, None, ALU.max))
            own(v.reciprocal(den[:, :], den[:, :]))
            own(v.tensor_scalar(den[:, :], den[:, :], tg[:, 2:3], None, ALU.mult))
            own(v.tensor_tensor(g12[:, :, :], g12[:, :, :], den[:, :].unsqueeze(1).broadcast_to([P, 2, NT]), ALU.mult))
            nv = n1s[:, :].rearrange("p (k r) -> p k r", r=5)
            pair = n1[:, 1, :].rearrange("p (k r) -> p k r", r=2)
            v.tensor_copy(nv[:, :, 0:2], pair[:, :, 0:1].broadcast_to([P, ST // 5, 2]))
            v.tensor_copy(nv[:, :, 3:5], pair[:, :, 1:2].broadcast_to([P, ST // 5, 2]))
            v.tensor_copy(nv[0:64, :, 2:3], pair[0:64, :, 0:1])
            own(v.tensor_copy(nv[64:P, :, 2:3], pair[64:P, :, 1:2]))
            own(v.tensor_tensor(n1s[:, :], sidx[:, :], n1s[:, :], ALU.is_ge))
            for b in range(B):
                v.wait_ge(xb_ready, 2 + b + 1)
                v.wait_ge(out_mm, b + 1)
                xv = xb[:, TB * b:TB * b + TB, :].rearrange("p t d -> p (t d)")
                v.scalar_tensor_tensor(xv, qm[:, b, :], tgs[:, 0:1], xv, ALU.mult, ALU.add).then_inc(out_ev, 1)
            v.wait_ge(xg_in, 16)
            v.scalar_tensor_tensor(dst_i[:, :], n1s[:, :], float(NTOK), xg[:, :, D], ALU.mult, ALU.add).then_inc(dst_ready, 1)
            v.wait_ge(moe_in[2], 16 * (E + 1))
            for i in range(ST):
                v.wait_ge(out_mm, 2 + i + 1)
                if i >= 4:
                    v.wait_ge(y_scats[i % 4], 16 * (i // 4))
                k, r = 2 * (i // 5), i % 5
                src = qm[:, (2 + i) % 2, 0:D]
                if r == 2:
                    v.tensor_tensor(ostage[0:64, i % 4, :], src[0:64], b2[0:64, k, :], ALU.add)
                    m = v.tensor_tensor(ostage[64:P, i % 4, :], src[64:P], b2[64:P, k + 1, :], ALU.add)
                else:
                    m = v.tensor_tensor(ostage[:, i % 4, :], src, b2[:, k + (r > 2), :], ALU.add)
                m.then_inc(out_ev, 1)
            v.wait_ge(y_in, 16)
            v.wait_ge(out_ev, 2)
            for b in range(B):
                for t in range(TB * b, TB * b + TB):
                    m = v.scalar_tensor_tensor(xb[:, t, :], y12[:, 0, t, :], g12[:, 0, t:t + 1], xb[:, t, :], ALU.mult, ALU.add)
                own(m)
                for t in range(TB * b, TB * b + TB):
                    m = v.scalar_tensor_tensor(x[:, t, :], y12[:, 1, t, :], g12[:, 1, t:t + 1], xb[:, t, :], ALU.mult, ALU.add)
                m.then_inc(x_moe, 1)
                v.wait_ge(x_moe, b + 1)
                norm_stats("C", b)
                norm("C", b)

            take_q("C", 0)
            take_q("C", 1)
            attention("C", then_norm("D", 0), then_norm("D", 1))
            for b in range(B):
                take_q("D", b)
                take_k2(b)
                take_v2(b)
            attention("D", lambda: None, lambda: None)


INS = ["x", "ctx_1024", "mask_Bx1xSxS2_ik1", "g_xattn", "g_ffn", "L0_xattn_Wq", "L0_xattn_bq", "L0_xattn_Wk",
       "L0_xattn_bk", "L0_xattn_Wv", "L0_xattn_bv", "L0_xattn_Wo", "L0_xattn_bo", "L0_ffn_router_w", "L0_ffn_w1",
       "L0_ffn_b1", "L0_ffn_w2", "L0_ffn_b2", "L0_ffn_sw1", "L0_ffn_sb1", "L0_ffn_sw2", "L0_ffn_sb2", "L1_xattn_Wv",
       "L1_xattn_Wk", "L1_xattn_Wq", "L1_xattn_Wo", "L1_xattn_bo", "L1_ffn_norm_w", "L1_ffn_norm_b", "L1_ffn_q_w",
       "L1_ffn_q_b", "L1_ffn_k_w", "L1_ffn_k_b", "L1_ffn_v_w", "L1_ffn_v_b", "L1_ffn_o_w", "L1_ffn_o_b"]


def kernel(**inputs):
    import concourse.bacc as bacc
    from concourse.bass_utils import run_bass_kernel_spmd

    nc = bacc.Bacc("TRN2", target_bir_lowering=False, num_devices=1)
    arrays, args = {}, {}
    for name in INS:
        arr = np.ascontiguousarray(inputs[name])
        arrays[f"in_{name}"] = arr
        args[name] = nc.dram_tensor(f"in_{name}", arr.shape, mybir.dt.from_np(arr.dtype), kind="ExternalInput").ap()
    out = nc.dram_tensor("out_x", (B, S, D), F32, kind="ExternalOutput").ap()
    build(nc, args, out)
    r = run_bass_kernel_spmd(nc, [arrays], core_ids=[0])
    return r.results[0]["out_x"]
```

```python
from contextlib import ExitStack

import numpy as np

import concourse.bass as bass
from concourse import mybir

F32 = mybir.dt.float32
BF16 = mybir.dt.bfloat16
I32 = mybir.dt.int32
U32 = mybir.dt.uint32
ALU = mybir.AluOpType
ACT = mybir.ActivationFunctionType
AX = mybir.AxisListType

P = 128
B = 2
S = 512
D = 128
NT = B * S // P
TB = S // P
H = 16
DH = D // H
NK = 77
E = 8
F = 512
FC = F // P
CAP = 320
SLOTS = E * CAP
ST = SLOTS // P
NTOK = B * S
ROW = D + 1
H2 = 8
DH2 = D // H2
EPS = 1e-5
SHARED_SCALE = 0.1
BIG = float(2.0 ** 100)
NONE = 4096.0
FEPS = float(np.finfo(np.float32).eps)

QROW = NK
MROW = QROW + 6 * DH
MROW2 = 6 * DH2
QPART = (0, 0, 0, 1, 1, 2)
KPART = (0, 1, 2, 0, 1, 0)

HEADS_OF = [H2 >> e for e in range(TB)]
NQ = [P * sum(h < n for n in HEADS_OF) for h in range(H2)]
PACKS = [[(0, 0), (1, 512), (4, 896)], [(2, 0), (3, 256), (5, 512), (6, 640), (7, 768)]]
PACK_W = [1024, 896]
PACK_AT = [0, 1024]
P2W = sum(PACK_W)
P2AT = {h: PACK_AT[k] + at for k in range(2) for h, at in PACKS[k]}
QM2 = [(e, h) for e in range(TB) for h in range(HEADS_OF[e])]
BLOCKS = [(e, h) for e in range(TB) for h in range(HEADS_OF[e])]

WEIGHTS = ["L0_xattn_Wq", "L0_xattn_Wk", "L0_xattn_Wv", "L0_xattn_Wo",
           "L1_xattn_Wq", "L1_xattn_Wk", "L1_xattn_Wv", "L1_xattn_Wo",
           "L1_ffn_q_w", "L1_ffn_k_w", "L1_ffn_v_w", "L1_ffn_o_w"]
ROWS = [("L0_xattn_bq", 1), ("L0_xattn_bk", 1), ("L0_ffn_b1", E * FC), ("L0_ffn_sb1", FC),
        ("L1_ffn_q_b", 1), ("L1_ffn_k_b", 1), ("L1_ffn_norm_w", 1), ("L1_ffn_norm_b", 1)]
ROW_AT = {}
_n = 0
for _name, _k in ROWS:
    ROW_AT[_name] = _n
    _n += _k
NROWS = _n
AROWS = 2
BC = ["L0_xattn_bv", "L0_xattn_bo", "L0_ffn_sb2", "L1_xattn_bo", "L1_ffn_v_b", "L1_ffn_o_b"]
BC_AT = {name: i for i, name in enumerate(BC)}


def work_jobs():
    jobs = []

    def add(who, *names):
        jobs.extend((name, who) for name in names)

    def cross_attention(L):
        add("dve", ("nT", L, 0))
        if L == "A":
            add("act", ("weights", 1), ("weights", 2), ("columns",))
        add("dve", ("nT", L, 1))
        if L == "A":
            add("dve", ("kv", "C"))
        add("dve", ("pv", L, 0, 0), ("pv", L, 0, 1), ("oT", L, 0, 0), ("pv", L, 0, 2), ("oT", L, 0, 1), ("pv", L, 0, 3),
            ("oT", L, 0, 2), ("oT", L, 0, 3), ("pv", L, 1, 0), ("onT", L, 0), ("pv", L, 1, 1), ("y", L, 0),
            ("pv", L, 1, 2), ("pv", L, 1, 3))
        add("dve", *[("oT", L, 1, g) for g in range(4)])

    for b in range(B):
        add("act", ("xT", "A", b))
        add("dve", ("q", "A", b))
    cross_attention("A")
    add("dve", ("xT", "B", 0), ("onT", "A", 1), ("y", "A", 1))
    add("act", ("xT", "B", 1))
    add("dve", ("logits",), ("pos",))
    add("act", *[("xg", n) for n in range(ST // 4)])
    for b in range(B):
        add("act", ("xT", "C", b))
        add("dve", ("q", "C", b))
    cross_attention("C")
    add("dve", ("xT", "D", 0), ("onT", "C", 1), ("q", "D", 0), ("y", "C", 1), ("k", "D", 0), ("v", "D", 0))
    add("act", ("xT", "D", 1))
    add("dve", ("q", "D", 1), ("k", "D", 1), ("v", "D", 1))
    add("dve", ("nT", "D", 0), ("nT", "D", 1), ("pv", "D", 0, 0), ("pv", "D", 0, 1))
    for b in range(B):
        add("dve", ("oT", "D", b, 0), ("onT", "D", b), ("y", "D", b))
    return jobs


JOBS = work_jobs()
JOB = {name: n for n, (name, _) in enumerate(JOBS)}


def taken(n):
    who = JOBS[n][1]
    return who, sum(1 for _, w in JOBS[:n + 1] if w == who)


LN = {(L, b): 2 * i + b for i, L in enumerate("ABCD") for b in range(B)}
XI = {("A", 0): 0, ("A", 1): 1, ("C", 0): 2, ("C", 1): 3, ("D", 0): 4, ("D", 1): 5}
QM_UNITS = {"A": 16, "C": 16, "D": len(QM2)}
T_UNITS = 8


def qm_index(L, b, u):
    before = {"A": 0, "C": 32, "D": 64}[L]
    return before + b * QM_UNITS[L] + u


def t_index(L, b, u):
    return ({"A": 0, "C": 2, "D": 4}[L] + b) * T_UNITS + u


def build(nc, a, out):
    with ExitStack() as ctx:
        def sb(name, shape, dt=F32):
            return ctx.enter_context(nc.sbuf_tensor(name, shape, dt))

        def sem(name):
            return ctx.enter_context(nc.semaphore(name))

        def dram(name, shape, dt):
            return nc.dram_tensor(name, shape, dt, kind="Internal").ap()

        qm = ctx.enter_context(nc.psum_tensor("qm", [P, 2, 512], F32))
        ts = ctx.enter_context(nc.psum_tensor("ts", [P, 4, 512], F32))
        wk = ctx.enter_context(nc.psum_tensor("wk", [P, 2, 512], F32))

        x = sb("x", [P, NT, D])
        xn = sb("xn", [P, NT, ROW])
        xb = sb("xb", [P, NT, D])
        xT = sb("xT", [P, NTOK])
        ctx_sb = sb("ctx_sb", [NK, B, D])
        ctxT = sb("ctxT", [P, B * NK])
        early = sb("early", [P, ST * ROW])
        mask_i = early[:, 0:NT * NK].bitcast(I32).rearrange("p (t k) -> p t k", k=NK)
        keep = early[:, NT * NK:2 * NT * NK].rearrange("p (t k) -> p t k", k=NK)
        someB = early[:, 2 * NT * NK:2 * NT * NK + NTOK]
        xg = early[:, :].rearrange("p (i r) -> p i r", r=ROW)
        fill = sb("fill", [P, ROW])
        some = sb("some", [P, NT])
        some_b = sb("some_b", [P, NT], BF16)
        none = sb("none", [P, NT])
        mneg = sb("mneg", [P, NT, NK], BF16)
        mnegT = sb("mnegT", [NK, NTOK], BF16)
        y12 = sb("y12", [P, 2, NT, D])
        wn = y12[:, :, :, :].rearrange("p c t d -> p (c t) d")[:, 0:12, :]
        wT = sb("wT", [P, 12, D])
        rows = sb("rows", [NROWS, D])
        col = sb("col", [P, NROWS])
        bc = sb("bc", [P, len(BC), D])
        gates_in = sb("gates_in", [P, 4])
        tg = sb("tg", [P, 4])
        tgs = sb("tgs", [P, 1])
        rw = sb("rw", [P, E])
        w1 = sb("w1", [P, E, F])
        w2 = sb("w2", [P, E, FC, D])
        b2 = sb("b2", [P, E, D])
        sw1 = sb("sw1", [P, F])
        sw2 = sb("sw2", [P, FC, D])
        ident = sb("ident", [P, P])
        identb = sb("identb", [P, P], BF16)
        onesb = sb("onesb", [P, P], BF16)
        trib = sb("trib", [P, P], BF16)
        half = sb("half", [P, 8])
        stats = sb("stats", [P, TB, 6])
        mv = sb("mv", [P, B, TB, 2])
        ve = sb("ve", [P, B, 2, TB])
        rstd = sb("rstd", [P, B, 2, TB])
        rtg = sb("rtg", [P, B, TB])
        qf = sb("qf", [P, S])
        qr = sb("qr", [P, S])
        kf = sb("kf", [P, B * NK])
        kr = sb("kr", [P, B * NK])
        parts = [sb(f"parts{i}", [P, 3 * S], BF16)[:, :].rearrange("p (s n) -> p s n", s=3) for i in range(2)]
        kparts = [parts[1].rearrange("p s n -> p (s n)")[:, 3 * B * P * i:3 * B * P * (i + 1)].rearrange(
            "p (s b k) -> p s b k", s=3, b=B) for i in range(2)]
        qst = sb("qst", [P, H, NTOK], BF16)
        kst = sb("kst", [P, 2, H, B, P], BF16)
        kst2 = w1[:, :, :].rearrange("p e f -> p (e f)").bitcast(BF16).rearrange("p (h n) -> p h n", h=H2)
        vst = [sb(f"vst{i}", [P, B, H, 32]) for i in range(2)]
        vst2 = w2[:, :, :, :].rearrange("p e c h -> p (e c h)")[:, 0:B * TB * H2 * 32].rearrange(
            "p (b t h r) -> p b t h r", b=B, t=TB, h=H2)
        nmx = sb("nmx", [P, TB, H])
        nmr = sb("nmr", [P, TB, H])
        nsp = sb("nsp", [P, TB, 3, H], BF16)
        nsT = sb("nsT", [3 * H, S], BF16)
        pr = sb("pr", [P, H, S])
        oo = sb("oo", [P, 4 * S + TB * D])
        oT = oo[:, 0:4 * S].rearrange("p (g n) -> p g n", g=4)
        on = oo[:, 4 * S:4 * S + TB * D].rearrange("p (t d) -> p t d", d=D)
        rden = sb("rden", [P, 16])
        onT = sb("onT", [P, S])

        pr_flat = pr[:, :, :].rearrange("p a b -> p (a b)")
        pr2 = pr_flat[:, 0:TB * P2W].rearrange("p (k c) -> p k c", k=TB)
        hs = pr_flat[:, 0:FC * NTOK].rearrange("p (c n) -> p c n", c=FC)
        he = pr_flat[:, FC * NTOK:FC * NTOK + 3 * FC * CAP].rearrange("p (r c n) -> p r c n", r=3, c=FC)
        xgT = oo[:, :]
        ostage = onT[:, :].rearrange("p (i d) -> p i d", d=D)
        sums = sb("sums", [P, NT])
        lg, gates, gates2, cand = (qf[:, NT * E * i:NT * E * i + NT * E].rearrange("p (t e) -> p t e", e=E) for i in range(4))
        hot, posn, kept, rt = (qr[:, 2 * NT * E * i:2 * NT * E * (i + 1)].rearrange("p (c t e) -> p c t e", c=2, e=E) for i in range(4))
        best = sb("best", [P, NT])
        first = sb("first", [P, NT])
        iota8 = sb("iota8", [P, NT, E])
        iota8i = sb("iota8i", [P, NT, E], I32)
        base320 = sb("base320", [P, E])
        toki = sb("toki", [P, NT], I32)
        hotb = sb("hotb", [P, 2, NT, E], BF16)
        n1 = sb("n1", [P, 2, E])
        g12 = sb("g12", [P, 2, NT])
        k12 = sb("k12", [P, 2, NT])
        s12 = sb("s12", [P, 2, NT])
        den = sb("den", [P, NT])
        slot_i = sb("slot_i", [P, 2, NT], I32)
        sidx_i = sb("sidx_i", [P, ST], I32)
        sidx = sb("sidx", [P, ST])
        sidx_t = sb("sidx_t", [P, ST])
        n1s = sb("n1s", [P, ST])
        dst_i = sb("dst_i", [P, ST], I32)

        kd = dram("kd", [2, 3, D, B * P], BF16)
        qd = dram("qd", [6, 3, D, S], BF16)
        kd2 = dram("kd2", [2, 3, D, S], BF16)
        nd = dram("nd", [6, 3 * H, S], BF16)
        xs_d = dram("xs_d", [SLOTS, ROW], F32)
        y_d = dram("y_d", [2 * NTOK, D], F32)

        x_in = [sem(f"x_in{b}") for b in range(B)]
        ctx_in, mask_in, rows_in, rows2_in, gate_in, bc_in = (
            sem(n) for n in ("ctx_in", "mask_in", "rows_in", "rows2_in", "gate_in", "bc_in"))
        bc2_in = sem("bc2_in")
        w_in = [sem(f"w_in{i}") for i in range(3)]
        moe_in = [sem(f"moe_in{i}") for i in range(3)]
        const = sem("const")
        dve = sem("dve_chain")
        pol = sem("pool_chain")
        mneg_ready, some_ready = sem("mneg_ready"), sem("some_ready")
        setup_mm, setup_ev = sem("setup_mm"), sem("setup_ev")
        tg_ready, tgs_ready, bias_ready = sem("tg_ready"), sem("tgs_ready"), sem("bias_ready")
        kv_mm, kparts_ready, vst_ready = sem("kv_mm"), sem("kparts_ready"), sem("vst_ready")
        kd_out = [sem(f"kd_out{i}") for i in range(2)]
        kst_in = [sem(f"kst_in{i}") for i in range(2)]
        mask_rows_in = [sem(f"mask_rows_in{b}") for b in range(B)]
        var_ready, rstd_ready, xn_ready, xb_ready = sem("var_ready"), sem("rstd_ready"), sem("xn_ready"), sem("xb_ready")
        job_mm, job_dve, job_act = sem("job_mm"), sem("job_dve"), sem("job_act")
        qparts_ready, k2parts_ready, kpad = sem("qparts_ready"), sem("k2parts_ready"), sem("kpad")
        qd_out = [[sem(f"qd_out{i}_{s}") for s in range(3)] for i in range(6)]
        qst_in = [sem(f"qst_in{i}") for i in range(6)]
        k2d_out = [[sem(f"k2d_out{i}_{s}") for s in range(3)] for i in range(2)]
        k2st_in = [sem(f"k2st_in{i}") for i in range(2)]
        nd_out = [sem(f"nd_out{i}") for i in range(6)]
        nst_in = [sem(f"nst_in{i}") for i in range(6)]
        qm_mm, qm_max, nsp_ready = sem("qm_mm"), sem("qm_max"), sem("nsp_ready")
        t_mm, t_exp = sem("t_mm"), sem("t_exp")
        pr_used = sem("pr_used")
        pv1_mm, pv1_taken = sem("pv1_mm"), sem("pv1_taken")
        x_moe = sem("x_moe")
        ex_ready, hot_ready, slot_ready, dst_ready = (sem(n) for n in ("ex_ready", "hot_ready", "slot_ready", "dst_ready"))
        hid_mm, hid_act, out_mm, out_ev = sem("hid_mm"), sem("hid_act"), sem("out_mm"), sem("out_ev")
        fill_src, fill_xs, fill_y, scat = (sem(n) for n in ("fill_src", "fill_xs", "fill_y", "scat"))
        xg_in = [sem(f"xg_in{n}") for n in range(ST // 4)]
        y_in = [sem(f"y_in{b}") for b in range(B)]
        y_scats = [sem(f"y_scat{i}") for i in range(4)]
        out_sem = sem("out_sem")

        def done(*name):
            who, value = taken(JOB[name])
            return (job_dve if who == "dve" else job_act), value

        norm_w, norm_b = (col[:, ROW_AT[n]:ROW_AT[n] + 1] for n in ("L1_ffn_norm_w", "L1_ffn_norm_b"))

        EV_WEIGHTS, EV_CONTEXT, EV_MASK, EV_SOME = 1, 2, 3, 4

        def q_bank(n):
            return (qm if n % 4 < 2 else ts)[:, n % 4, :]

        def q_parts(L, b):
            return parts[1 if (L, b) == ("C", 1) else 0]

        C_IDENT, C_HALF, C_IDENTB, C_ONES, C_KST, C_KID, C_TRI, C_VST, C_N1, C_IOTA, C_SIDX, C_KST2 = range(2, 14)

        x_dram = a["x"].rearrange("b (t p) d -> p b t d", p=P)
        out_dram = out.rearrange("b (t p) d -> p b t d", p=P)

        block = ctx.enter_context(nc.Block())

        @block.sync
        def _(sp):
            def bcast(name):
                return a[name].partition_broadcast(P)

            def row(name):
                src = a[name]
                src = src.rearrange("e (c p) -> (e c) p", p=D) if len(src.shape) == 2 else src.rearrange("(c p) -> c p", p=D)
                return rows[ROW_AT[name]:ROW_AT[name] + dict(ROWS)[name], :], src

            def weights(g):
                for i in range(4 * g, 4 * g + 4):
                    sp.dma_start(wn[:, i, :], a[WEIGHTS[i]]).then_inc(w_in[g], 16)

            def k_ones(L):
                for b in range(B):
                    sp.dma_start(kst[MROW:MROW + 3, L, :, b, 0:NK], onesb[0:3, 0:NK].unsqueeze(1).broadcast_to([3, H, NK])).then_inc(kst_in[L], 16)

            def mask_rows(b):
                c = slice(S * b, S * b + S)
                sp.dma_start(qst[0:NK, :, c], mnegT[:, c].unsqueeze(1).broadcast_to([NK, H, S])).then_inc(mask_rows_in[b], 16)

            def k_store(L):
                sp.wait_ge(kparts_ready, L + 1)
                sp.dma_start(kd[L].rearrange("s p n -> p s n"), kparts[L][:, :, :, :].rearrange("p s b k -> p s (b k)")).then_inc(kd_out[L], 16)

            def k_stack(L):
                sp.wait_ge(kd_out[L], 16)
                for j, part in enumerate(KPART):
                    sp.dma_start(kst[QROW + DH * j:QROW + DH * j + DH, L, :, :, :].rearrange("p h b k -> p h (b k)"),
                                 kd[L, part].rearrange("(h d) n -> d h n", d=DH)).then_inc(kst_in[L], 16)

            def q_store(L, b):
                i = XI[L, b]
                for s in range(3):
                    sp.wait_ge(qparts_ready, 3 * i + s + 1)
                    sp.dma_start(qd[i, s], q_parts(L, b)[:, s, :]).then_inc(qd_out[i][s], 16)

            def q_load(L, b):
                i = XI[L, b]
                dh = DH2 if L == "D" else DH
                nh = H2 if L == "D" else H
                row0 = 0 if L == "D" else QROW
                for part in range(3):
                    sp.wait_ge(qd_out[i][part], 16)
                    for j in (j for j in range(6) if QPART[j] == part):
                        sp.dma_start(qst[row0 + dh * j:row0 + dh * j + dh, 0:nh, S * b:S * b + S],
                                     qd[i, part].rearrange("(h d) n -> d h n", d=dh)).then_inc(qst_in[i], 16)

            def k2_store(b):
                for s in range(3):
                    sp.wait_ge(k2parts_ready, 3 * b + s + 1)
                    sp.dma_start(kd2[b, s], parts[1][:, s, :]).then_inc(k2d_out[b][s], 16)

            def k2_load(b):
                for part in range(3):
                    sp.wait_ge(k2d_out[b][part], 16)
                    for j in (j for j in range(6) if KPART[j] == part):
                        sp.dma_start(kst2[DH2 * j:DH2 * j + DH2, :, S * b:S * b + S],
                                     kd2[b, part].rearrange("(h d) n -> d h n", d=DH2)).then_inc(k2st_in[b], 16)

            def max_rows(L, b):
                i = XI[L, b]
                nh = H2 if L == "D" else H
                row = MROW2 if L == "D" else MROW
                sp.wait_ge(*done("nT", L, b))
                sp.dma_start(nd[i, 0:3 * nh], nsT[0:3 * nh, :]).then_inc(nd_out[i], 16)
                sp.wait_ge(nd_out[i], 16)
                sp.dma_start(qst[row:row + 3, 0:nh, S * b:S * b + S],
                             nd[i, 0:3 * nh].rearrange("(s h) n -> s h n", s=3)).then_inc(nst_in[i], 16)

            sp.dma_start(x[:, 0:TB, :], x_dram[:, 0]).then_inc(x_in[0], 16)
            sp.dma_start(mask_i[:, :, :], a["mask_Bx1xSxS2_ik1"].rearrange("b o (t p) k -> p (b o t) k", p=P)).then_inc(mask_in, 16)
            weights(0)
            sp.dma_start(ctx_sb[:, :, :], a["ctx_1024"].rearrange("b k d -> k b d")).then_inc(ctx_in, 16)
            for name, _ in ROWS[:AROWS]:
                sp.dma_start(*row(name)).then_inc(rows_in, 16)
            sp.dma_start(x[:, TB:NT, :], x_dram[:, 1]).then_inc(x_in[1], 16)
            for i, name in enumerate(BC[:2]):
                sp.dma_start(bc[:, BC_AT[name], :], bcast(name)).then_inc(bc_in, 16)
            sp.wait_ge(const, C_KST)
            k_ones(0)
            sp.wait_ge(setup_ev, EV_MASK)
            mask_rows(0)
            q_store("A", 0)
            k_store(0)
            q_load("A", 0)
            k_stack(0)
            q_store("A", 1)
            q_load("A", 1)
            mask_rows(1)
            sp.dma_start(gates_in[:, 0:2], bcast("g_xattn")).then_inc(gate_in, 16)
            sp.dma_start(gates_in[:, 2:4], bcast("g_ffn")).then_inc(gate_in, 16)
            weights(1)
            weights(2)
            for name, _ in ROWS[AROWS:]:
                sp.dma_start(*row(name)).then_inc(rows2_in, 16)
            for name in BC[2:]:
                sp.dma_start(bc[:, BC_AT[name], :], bcast(name)).then_inc(bc2_in, 16)
            k_ones(1)
            max_rows("A", 0)
            sp.dma_start(rw[:, :], a["L0_ffn_router_w"]).then_inc(moe_in[0], 16)
            sp.dma_start(sw1[:, :], a["L0_ffn_sw1"]).then_inc(moe_in[0], 16)
            sp.dma_start(sw2[:, :, :], a["L0_ffn_sw2"].rearrange("(c p) h -> p c h", p=P)).then_inc(moe_in[0], 16)
            max_rows("A", 1)
            k_store(1)
            k_stack(1)
            for e in range(E):
                sp.dma_start(w1[:, e, :], a["L0_ffn_w1"][e]).then_inc(moe_in[1], 16)
                sp.dma_start(w2[:, e, :, :], a["L0_ffn_w2"][e].rearrange("(c p) h -> p c h", p=P)).then_inc(moe_in[2], 16)
            sp.dma_start(b2[:, :, :], bcast("L0_ffn_b2")).then_inc(moe_in[2], 16)

            sp.wait_ge(fill_src, 1)
            sp.dma_start(xs_d.rearrange("(i p) r -> p i r", p=P), fill[:, :].unsqueeze(1).broadcast_to([P, ST, ROW])).then_inc(fill_xs, 16)
            sp.dma_start(y_d.rearrange("(c t p) d -> p (c t) d", p=P, t=NT), fill[:, 0:D].unsqueeze(1).broadcast_to([P, 2 * NT, D])).then_inc(fill_y, 16)

            sp.wait_ge(scat, 16 * 2 * NT)
            xs_v = xs_d.rearrange("(i p) r -> p i r", p=P)
            for n in range(ST // 4):
                sp.dma_start(xg[:, 4 * n:4 * n + 4, :], xs_v[:, 4 * n:4 * n + 4, :]).then_inc(xg_in[n], 16)
            for i in range(4):
                sp.wait_ge(y_scats[i], 16 * (ST // 4))
            y_v = y_d.rearrange("(c t p) d -> p c t d", p=P, t=NT)
            for b in range(B):
                for c in range(2):
                    t = slice(TB * b, TB * b + TB)
                    sp.dma_start(y12[:, c, t, :], y_v[:, c, t, :]).then_inc(y_in[b], 16)

            for b in range(B):
                q_store("C", b)
                q_load("C", b)
            for b in range(B):
                max_rows("C", b)
            for b in range(B):
                q_store("D", b)
                q_load("D", b)
                k2_store(b)
                k2_load(b)
            for b in range(B):
                max_rows("D", b)
            for b in range(B):
                sp.wait_ge(*done("y", "D", b))
                sp.dma_start(out_dram[:, b], xb[:, TB * b:TB * b + TB, :]).then_inc(out_sem, 16)
            sp.wait_ge(out_sem, 32)

        @block.gpsimd
        def _(pool):
            n_own = [0]

            def own(ins):
                n_own[0] += 1
                ins.then_inc(pol, 1)
                pool.wait_ge(pol, n_own[0])

            pool.memset(ident[:, :], 0.0).then_inc(const, 1)
            pool.wait_ge(const, 1)
            pool.affine_select(out=ident[:, :], in_=ident[:, :], compare_op=ALU.not_equal, fill=1.0, base=0,
                               pattern=[[-1, P]], channel_multiplier=1).then_inc(const, 1)
            pool.memset(half[:, :], -0.5).then_inc(const, 1)
            pool.wait_ge(const, C_IDENT)
            pool.tensor_copy(identb[:, :], ident[:, :]).then_inc(const, 1)
            pool.memset(onesb[:, :], 1.0).then_inc(const, 1)

            def pow_rstd(L, b):
                n = 2 if L == "D" else 1
                pool.wait_ge(var_ready, LN[L, b] + 1)
                pool.tensor_tensor(rstd[:, b, 0:n, :], ve[:, b, 0:n, :],
                                   half[:, 0:n * TB].rearrange("p (n t) -> p n t", n=n), ALU.pow).then_inc(rstd_ready, 1)

            pool.wait_ge(const, C_HALF)
            pow_rstd("A", 0)
            pool.memset(kst[:, :, :, :, :].rearrange("p l h b k -> p (l h b k)").bitcast(U32), 0).then_inc(const, 1)
            pool.wait_ge(const, C_KST)
            kid = kst[0:NK, 0, :, :, 0:NK].rearrange("p h b k -> p (h b) k")
            pool.affine_select(out=kid, in_=kid, compare_op=ALU.not_equal, fill=BIG, base=0,
                               pattern=[[0, H * B], [-1, NK]], channel_multiplier=1).then_inc(const, 1)
            pow_rstd("A", 1)
            pool.affine_select(out=trib[:, :], in_=onesb[:, :], compare_op=ALU.is_gt, fill=0.0, base=0,
                               pattern=[[1, P]], channel_multiplier=-1).then_inc(const, 1)
            for L in range(2):
                own(pool.memset(vst[L][:, :, :, :], 0.0))
            for L in range(2):
                m = pool.memset(vst[L][0:NK, :, :, DH:DH + 1], 1.0)
                if L == 0:
                    own(m)
            m.then_inc(const, 1)
            pool.memset(n1[:, :, :], 0.0).then_inc(const, 1)
            pool.memset(fill[:, 0:D], 0.0)
            pool.memset(fill[:, D:ROW], NONE).then_inc(fill_src, 1)
            own(pool.iota(iota8i[:, :, :], pattern=[[0, NT], [1, E]], base=-E, channel_multiplier=0))
            own(pool.tensor_copy(iota8[:, :, :], iota8i[:, :, :]))
            own(pool.tensor_scalar(base320[:, :], iota8[:, 0, :], float(CAP), float(CAP * E), ALU.mult, ALU.add))
            own(pool.iota(toki[:, :], pattern=[[P, NT]], base=0, channel_multiplier=1))
            pool.tensor_copy(xn[:, :, D], toki[:, :]).then_inc(const, 1)
            own(pool.iota(sidx_i[:, :], pattern=[[0, ST // 5], [P, 5]], base=0, channel_multiplier=1))
            own(pool.tensor_copy(sidx[:, :], sidx_i[:, :]))
            own(pool.tensor_scalar(sidx_t[:, :], sidx[:, :], float(CAP), float(-CAP), ALU.is_ge, ALU.mult))
            pool.tensor_tensor(sidx[:, :], sidx[:, :], sidx_t[:, :], ALU.add).then_inc(const, 1)

            def x_bias(L, b, row, x_ready, value):
                pool.wait_ge(x_ready, value)
                t = slice(TB * b, TB * b + TB)
                pool.tensor_tensor(xb[:, t, :], x[:, t, :], bc[:, row, :].unsqueeze(1).broadcast_to([P, TB, D]),
                                   ALU.add).then_inc(xb_ready, 1)

            pool.wait_ge(bc_in, 32)
            pool.wait_ge(bc2_in, 16 * (len(BC) - 2))
            pool.wait_ge(tg_ready, 1)
            pool.wait_ge(tgs_ready, 1)
            pool.tensor_scalar(bc[:, BC_AT["L0_xattn_bo"], :], bc[:, BC_AT["L0_xattn_bo"], :], tg[:, 0:1], None, ALU.mult).then_inc(bias_ready, 1)
            pool.tensor_scalar(bc[:, BC_AT["L1_xattn_bo"], :], bc[:, BC_AT["L1_xattn_bo"], :], tg[:, 1:2], None, ALU.mult).then_inc(bias_ready, 1)
            pool.tensor_scalar(bc[:, BC_AT["L0_ffn_sb2"], :], bc[:, BC_AT["L0_ffn_sb2"], :], tgs[:, 0:1], None, ALU.mult).then_inc(bias_ready, 1)
            pool.tensor_scalar(bc[:, BC_AT["L1_ffn_o_b"], :], bc[:, BC_AT["L1_ffn_o_b"], :], tg[:, 3:4], None, ALU.mult).then_inc(bias_ready, 1)
            pool.wait_ge(bias_ready, 4)
            for b in range(B):
                x_bias("A", b, BC_AT["L0_xattn_bo"], x_in[b], 16)

            for b in range(B):
                pow_rstd("B", b)
            for b in range(B):
                x_bias("B", b, BC_AT["L0_ffn_sb2"], *done("y", "A", b))
            pool.wait_ge(slot_ready, 1)
            pool.wait_ge(fill_xs, 16)
            for c in range(2):
                for t in range(NT):
                    pool.indirect_dma_start(xs_d, bass.IndirectOffsetOnAxis(ap=slot_i[:, c, t:t + 1], axis=0),
                                            xn[:, t, :], None, bounds_check=SLOTS - 1, oob_is_err=False).then_inc(scat, 16)
            pool.wait_ge(dst_ready, 1)
            pool.wait_ge(fill_y, 16)
            for i in range(ST):
                pool.wait_ge(out_ev, 2 + i + 1)
                pool.indirect_dma_start(y_d, bass.IndirectOffsetOnAxis(ap=dst_i[:, i:i + 1], axis=0),
                                        ostage[:, i % 4, :], None, bounds_check=2 * NTOK - 1, oob_is_err=False).then_inc(y_scats[i % 4], 16)

            for b in range(B):
                pow_rstd("C", b)
            for b in range(B):
                x_bias("C", b, BC_AT["L1_xattn_bo"], x_moe, b + 1)

            pool.wait_ge(out_mm, 2 + ST)
            own(pool.memset(vst2, 0.0))
            own(pool.memset(vst2[:, :, :, :, DH2:DH2 + 1], 1.0))
            pool.memset(kst2[MROW2:MROW2 + 3, :, :], 1.0).then_inc(const, 1)
            pool.wait_ge(const, C_KST2)

            for b in range(B):
                pow_rstd("D", b)
            for b in range(B):
                pool.wait_ge(rstd_ready, LN["D", b] + 1)
                own(pool.tensor_scalar(rtg[:, b, :], rstd[:, b, 0, :], tg[:, 3:4], None, ALU.mult))
                for t in range(TB):
                    m = pool.tensor_scalar(xb[:, TB * b + t, :], x[:, TB * b + t, :], mv[:, b, t, 0:1], rtg[:, b, t:t + 1],
                                           ALU.subtract, ALU.mult)
                own(m)
                own(pool.tensor_tensor(xb[:, TB * b:TB * b + TB, :], xb[:, TB * b:TB * b + TB, :], x[:, TB * b:TB * b + TB, :], ALU.add))
                for t in range(TB):
                    k = D >> t
                    m = pool.tensor_tensor(xb[:, TB * b + t, 0:k], xb[:, TB * b + t, 0:k], bc[:, BC_AT["L1_ffn_o_b"], 0:k], ALU.add)
                m.then_inc(xb_ready, 1)

        @block.tensor
        def _(pe):
            def wait_bank(n):
                if n >= 2:
                    who, value = taken(n - 2)
                    pe.wait_ge(job_dve if who == "dve" else job_act, value)
                return wk[:, n % 2, :]

            def transposes_x(L, b):
                w = wait_bank(JOB["xT", L, b])
                for t in range(TB):
                    pe.wait_ge(xn_ready, TB * LN[L, b] + t + 1)
                    m = pe.transpose(w[:, P * t:P * t + P], xn[:, TB * b + t, 0:D], ident[:, :])
                m.then_inc(job_mm, 1)

            def x_cols(b, t=None):
                return xT[:, S * b:S * b + S] if t is None else xT[:, S * b + P * t:S * b + P * t + P]

            def wait_taken(name):
                pe.wait_ge(*done(*name))

            def project_q(L, b):
                w = wait_bank(JOB["q", L, b])
                wait_taken(("xT", L, b))
                pe.matmul(w, wT[:, 0 if L == "A" else 4, :], x_cols(b), start=True, stop=True).then_inc(job_mm, 1)

            def project_d(b, *names):
                wait_taken(("xT", "D", b))
                for name in names:
                    w = wait_bank(JOB[name, "D", b])
                    for t in range(TB):
                        k = D >> t
                        xt, wt = x_cols(b, t)[0:k], wT[0:k, {"q": 8, "k": 9, "v": 10}[name], :]
                        if name == "v":
                            m = pe.matmul(w[:, P * t:P * t + P], xt, wt, start=True, stop=True)
                        else:
                            m = pe.matmul(w[:, P * t:P * t + P], wt, xt, start=True, stop=True)
                    m.then_inc(job_mm, 1)

            def scores_q(L, b, u):
                n = qm_index(L, b, u)
                bank = q_bank(n)
                if n >= 4:
                    pe.wait_ge(qm_max, n - 3)
                if u == 0:
                    pe.wait_ge(qst_in[XI[L, b]], 16 * 6)
                    if L == "A":
                        pe.wait_ge(mask_rows_in[b], 16)
                        pe.wait_ge(kst_in[0], 16 * 8)
                        pe.wait_ge(const, C_KID)
                    if L == "C":
                        pe.wait_ge(kst_in[1], 16 * 8)
                    if L == "D":
                        pe.wait_ge(k2st_in[b], 16 * 6)
                        pe.wait_ge(const, C_KST2)
                if L == "D":
                    e, h = QM2[u]
                    m = pe.matmul(bank, qst[0:MROW2, h, S * b + P * e:S * b + P * e + P],
                                  kst2[0:MROW2, h, S * b:S * b + S], start=True, stop=True)
                else:
                    t, g = u // 4, u % 4
                    for j in range(4):
                        h = 4 * g + j
                        m = pe.matmul(bank[:, NK * j:NK * j + NK], qst[0:MROW, h, S * b + P * t:S * b + P * t + P],
                                      kst[0:MROW, 0 if L == "A" else 1, h, b, 0:NK], start=True, stop=True)
                m.then_inc(qm_mm, 1)

            def transposes_max(L, b):
                nh = 3 * (H2 if L == "D" else H)
                w = wait_bank(JOB["nT", L, b])
                pe.wait_ge(nsp_ready, XI[L, b] + 1)
                wb = w.bitcast(BF16)
                src = nsp[:, :, :, :].rearrange("p t s h -> p (t s h)")
                for t in range(TB):
                    m = pe.transpose(wb[0:nh, P * t:P * t + P], src[:, nh * t:nh * t + nh], identb[:, :])
                m.then_inc(job_mm, 1)

            def scores_t(L, b, u):
                n = t_index(L, b, u)
                if u == 0:
                    pe.wait_ge(nst_in[XI[L, b]], 16)
                if b == 0 and u == 1:
                    pe.wait_ge(qm_max, qm_index(L, 1, QM_UNITS[L] - 1) + 1)
                if n >= 2:
                    pe.wait_ge(t_exp, n - 1)
                dst = ts[:, 2 * (n % 2):2 * (n % 2) + 2, :].rearrange("p a b -> p (a b)")
                if L == "D":
                    kt, k = u // 2, u % 2
                    for h, at in PACKS[k]:
                        m = pe.matmul(dst[:, at:at + NQ[h]], kst2[0:MROW2 + 3, h, S * b + P * kt:S * b + P * kt + P],
                                      qst[0:MROW2 + 3, h, S * b:S * b + NQ[h]], start=True, stop=True)
                else:
                    for j in range(2):
                        h = 2 * u + j
                        m = pe.matmul(dst[:, S * j:S * j + S], kst[:, 0 if L == "A" else 1, h, b, :],
                                      qst[:, h, S * b:S * b + S], start=True, stop=True)
                m.then_inc(t_mm, 1)

            def values(L, b, g):
                w = wait_bank(JOB["pv", L, b, g])
                if b == 0 and g == 0:
                    pe.wait_ge(vst_ready, 2)
                pe.wait_ge(t_exp, t_index(L, b, 2 * g + 1) + 1)
                for j in range(4):
                    h = 4 * g + j
                    m = pe.matmul(w[32 * j:32 * j + 32, :], vst[0 if L == "A" else 1][:, b, h, :], pr[:, h, :],
                                  start=True, stop=True)
                m.then_inc(job_mm, 1)

            def values_d(b, kt):
                if b == 0:
                    ws = [wk[:, JOB["pv", "D", 0, g] % 2, :] for g in range(2)]
                else:
                    ws = [qm[:, g, :] for g in range(2)]
                if kt == 0:
                    if b == 0:
                        wait_bank(JOB["pv", "D", 0, 0])
                        wait_bank(JOB["pv", "D", 0, 1])
                    wait_taken(("v", "D", b))
                pe.wait_ge(t_exp, t_index("D", b, 2 * kt + 1) + 1)
                for g in range(2):
                    for j in range(4):
                        h = 4 * g + j
                        m = pe.matmul(ws[g][32 * j:32 * j + 32, 0:NQ[h]], vst2[:, b, kt, h, :],
                                      pr2[:, kt, P2AT[h]:P2AT[h] + NQ[h]], start=(kt == 0), stop=(kt == TB - 1))
                    if kt == TB - 1:
                        m.then_inc(job_mm if b == 0 else pv1_mm, 1)
                if kt < TB - 1 and b == 0:
                    m.then_inc(pr_used, 1)

            def token_major(L, b, g):
                w = wait_bank(JOB["oT", L, b, g])
                wait_taken(("pv", L, b, g))
                for t in range(TB):
                    m = pe.transpose(w[:, P * t:P * t + P], oT[:, g, P * t:P * t + P], ident[:, :])
                m.then_inc(job_mm, 1)

            def channel_major(L, b):
                w = wait_bank(JOB["onT", L, b])
                wait_taken(("oT", L, b, 3))
                for t in range(TB):
                    m = pe.transpose(w[:, P * t:P * t + P], on[:, t, :], ident[:, :])
                m.then_inc(job_mm, 1)

            def project_out(L, b):
                w = wait_bank(JOB["y", L, b])
                wait_taken(("onT", L, b))
                for t in range(TB):
                    m = pe.matmul(w[:, P * t:P * t + P], onT[:, P * t:P * t + P], wT[:, 3 if L == "A" else 7, :],
                                  start=True, stop=True)
                m.then_inc(job_mm, 1)

            def token_major_d(b):
                w = wait_bank(JOB["oT", "D", b, 0])
                if b == 0:
                    wait_taken(("pv", "D", 0, 1))
                else:
                    pe.wait_ge(pv1_taken, 2)
                at = 0
                for e in range(TB):
                    for g in range(max(1, HEADS_OF[e] // 4)):
                        n = 32 * min(4, HEADS_OF[e])
                        m = pe.transpose(w[:, at:at + n], oT[0:n, g, P * e:P * e + P], ident[0:n, 0:n])
                        at += n
                m.then_inc(job_mm, 1)

            def channel_major_d(b):
                w = wait_bank(JOB["onT", "D", b])
                wait_taken(("oT", "D", b, 0))
                onf = on[:, :, :].rearrange("p t d -> p (t d)")
                at = 0
                for e in range(TB):
                    n = D >> e
                    m = pe.transpose(w[0:n, P * e:P * e + P], onf[:, at:at + n], ident[:, :])
                    at += n
                m.then_inc(job_mm, 1)

            def project_out_d(b):
                w = wait_bank(JOB["y", "D", b])
                wait_taken(("onT", "D", b))
                for e in range(TB):
                    n = D >> e
                    m = pe.matmul(w[:, P * e:P * e + n], onT[0:n, P * e:P * e + P], wT[0:n, 11, 0:n], start=True, stop=True)
                m.then_inc(job_mm, 1)

            def later_weights():
                for g in (1, 2):
                    w = wait_bank(JOB["weights", g])
                    pe.wait_ge(w_in[g], 64)
                    for i in range(4):
                        m = pe.transpose(w[:, P * i:P * i + P], wn[:, 4 * g + i, :], ident[:, :])
                    m.then_inc(job_mm, 1)
                w = wait_bank(JOB["columns",])
                pe.wait_ge(rows2_in, 16 * (len(ROWS) - AROWS))
                pe.transpose(w[:, 0:NROWS], rows[:, :], ident[0:NROWS, 0:NROWS]).then_inc(job_mm, 1)

            def context_products(k_out, v_out, layer):
                pe.matmul(k_out, wT[:, 4 * layer + 1, :], ctxT[:, :], start=True, stop=True)
                for b in range(B):
                    m = pe.matmul(v_out[:, P * b:P * b + P], ctxT[:, NK * b:NK * b + NK], wT[:, 4 * layer + 2, :],
                                  start=True, stop=True)
                return m

            def keys_and_values_c():
                w = wait_bank(JOB["kv", "C"])
                wait_taken(("weights", 1))
                context_products(w[:, 0:B * NK], w[0:NK, 2 * P:4 * P], 1).then_inc(job_mm, 1)

            LEAD = 4

            def scores_and_maxima(L):
                for u in range(QM_UNITS[L]):
                    scores_q(L, 0, u)
                for u in range(LEAD):
                    scores_q(L, 1, u)
                transposes_max(L, 0)
                if L == "A":
                    later_weights()
                for u in range(LEAD, QM_UNITS[L]):
                    scores_q(L, 1, u)
                for u in range(2):
                    scores_t(L, 0, u)
                transposes_max(L, 1)
                if L == "A":
                    keys_and_values_c()

            def cross_attention(L):
                scores_and_maxima(L)
                for k in range(1, 4):
                    scores_t(L, 0, 2 * k)
                    scores_t(L, 0, 2 * k + 1)
                    values(L, 0, k - 1)
                    if k > 1:
                        token_major(L, 0, k - 2)
                scores_t(L, 1, 0)
                scores_t(L, 1, 1)
                values(L, 0, 3)
                token_major(L, 0, 2)
                scores_t(L, 1, 2)
                token_major(L, 0, 3)
                scores_t(L, 1, 3)
                values(L, 1, 0)
                channel_major(L, 0)
                scores_t(L, 1, 4)
                scores_t(L, 1, 5)
                values(L, 1, 1)
                project_out(L, 0)
                scores_t(L, 1, 6)
                scores_t(L, 1, 7)
                values(L, 1, 2)
                values(L, 1, 3)
                for g in range(4):
                    token_major(L, 1, g)

            pe.wait_ge(const, C_IDENT)
            pe.wait_ge(w_in[0], 64)
            for i in range(4):
                m = pe.transpose(ts[:, 0, P * i:P * i + P], wn[:, i, :], ident[:, :])
            m.then_inc(setup_mm, 1)
            pe.wait_ge(rows_in, 16 * AROWS)
            pe.wait_ge(ctx_in, 16)
            pe.transpose(ts[:, 1, 0:AROWS], rows[0:AROWS, :], ident[0:AROWS, 0:AROWS])
            for b in range(B):
                m = pe.transpose(ts[:, 1, P + NK * b:P + NK * b + NK], ctx_sb[:, b, :], ident[0:NK, 0:NK])
            m.then_inc(setup_mm, 1)
            pe.wait_ge(const, C_IDENTB)
            pe.wait_ge(mneg_ready, 1)
            for t in range(NT):
                m = pe.transpose(qm[:, 0, :].bitcast(BF16)[0:NK, P * t:P * t + P], mneg[:, t, :], identb[:, :])
            m.then_inc(setup_mm, 1)
            pe.wait_ge(some_ready, 1)
            for b in range(B):
                for t in range(TB):
                    tt = TB * b + t
                    bank = qm[:, 1, :] if b == 0 else ts[:, 3, :]
                    m = pe.matmul(bank[:, P * t:P * t + P], some_b[:, tt:tt + 1].broadcast_to([P, P]), identb[:, :], start=True, stop=True)
                m.then_inc(setup_mm, 1)
            transposes_x("A", 0)
            pe.wait_ge(setup_ev, EV_WEIGHTS)
            project_q("A", 0)
            pe.wait_ge(setup_ev, EV_CONTEXT)
            context_products(ts[:, 2, 0:B * NK], ts[0:NK, 2, 2 * P:4 * P], 0).then_inc(kv_mm, 1)
            transposes_x("A", 1)
            project_q("A", 1)

            pe.wait_ge(setup_ev, EV_SOME + 1)
            pe.wait_ge(vst_ready, 2)
            pe.wait_ge(kparts_ready, 1)
            cross_attention("A")
            transposes_x("B", 0)
            channel_major("A", 1)
            project_out("A", 1)

            transposes_x("B", 1)
            w = wait_bank(JOB["logits",])
            wait_taken(("xT", "B", 1))
            pe.wait_ge(moe_in[0], 48)
            for t in range(NT):
                m = pe.matmul(w[:, E * t:E * t + E], xT[:, P * t:P * t + P], rw[:, :], start=True, stop=True)
            m.then_inc(job_mm, 1)

            def hidden(n, lhs, rhs, width):
                if n >= 4:
                    pe.wait_ge(hid_act, n - 3)
                elif n == 0:
                    pe.wait_ge(t_exp, t_index("A", 1, T_UNITS - 1) + 1)
                pe.matmul(ts[:, n % 4, 0:width], lhs, rhs, start=True, stop=True).then_inc(hid_mm, 1)

            for c in range(FC):
                for b in range(B):
                    hidden(2 * c + b, sw1[:, P * c:P * c + P], x_cols(b), S)
                if c == 0:
                    w = wait_bank(JOB["pos",])
                    pe.wait_ge(hot_ready, 1)
                    wv = w[:, 0:2 * NT * E].rearrange("p (c t e) -> p c t e", c=2, t=NT)
                    pe.matmul(w[:, 2 * NT * E:3 * NT * E], onesb[:, :], hotb[:, 0, :, :].rearrange("p t e -> p (t e)"),
                              start=True, stop=True)
                    for t in range(NT - 1):
                        for ch in range(2):
                            pe.matmul(wv[:, ch, t + 1:, :], onesb[:, :],
                                      hotb[:, ch, t, :].unsqueeze(1).broadcast_to([P, NT - 1 - t, E]),
                                      start=False, stop=False, skip_group_check=True)
                    pe.matmul(w[:, 0:2 * NT * E], trib[:, :], hotb[:, :, :, :].rearrange("p c t e -> p (c t e)"),
                              start=False, stop=True, skip_group_check=True).then_inc(job_mm, 1)
            for b in range(B):
                pe.wait_ge(hid_act, 2 * FC)
                if b == 0:
                    pe.wait_ge(qm_max, qm_index("A", 1, 15) + 1)
                for t in range(TB):
                    for c in range(FC):
                        m = pe.matmul(qm[:, b, P * t:P * t + P], hs[:, c, S * b + P * t:S * b + P * t + P], sw2[:, c, :],
                                      start=(c == 0), stop=(c == FC - 1))
                m.then_inc(out_mm, 1)
            for n in range(ST // 4):
                w = wait_bank(JOB["xg", n])
                pe.wait_ge(xg_in[n], 16)
                for j in range(4):
                    m = pe.transpose(w[:, P * j:P * j + P], xg[:, 4 * n + j, 0:D], ident[:, :])
                m.then_inc(job_mm, 1)

            def expert_hidden(e):
                if e == 0:
                    pe.wait_ge(moe_in[1], 16 * E)
                who, value = taken(JOB["xg", (CAP * (e + 1) - 1) // 512])
                pe.wait_ge(job_act, value)
                for c in range(FC):
                    hidden(2 * FC + FC * e + c, w1[:, e, P * c:P * c + P], xgT[:, CAP * e:CAP * e + CAP], CAP)

            def expert_out(i):
                n = 2 + i
                pe.wait_ge(out_ev, n - 1)
                k, r = 2 * (i // 5), i % 5
                pieces = {0: [(k, 0, P, 0)], 1: [(k, P, P, 0)], 2: [(k, 2 * P, 64, 0), (k + 1, 0, 64, 64)],
                          3: [(k + 1, 64, P, 0)], 4: [(k + 1, 64 + P, P, 0)]}[r]
                for e, s0, m_, p0 in pieces:
                    pe.wait_ge(hid_act, 2 * FC + FC * e + FC)
                    for c in range(FC):
                        m = pe.matmul(qm[p0:p0 + m_, n % 2, 0:D], he[:, e % 3, c, s0:s0 + m_], w2[:, e, c, :],
                                      start=(c == 0), stop=(c == FC - 1))
                m.then_inc(out_mm, 1)

            expert_hidden(0)
            pe.wait_ge(moe_in[2], 16 * (E + 1))
            for e in range(E):
                if e + 1 < E:
                    expert_hidden(e + 1)
                for i in ((5 * (e // 2), 5 * (e // 2) + 1) if e % 2 == 0 else (5 * (e // 2) + 2, 5 * (e // 2) + 3, 5 * (e // 2) + 4)):
                    expert_out(i)

            transposes_x("C", 0)
            project_q("C", 0)
            transposes_x("C", 1)
            project_q("C", 1)
            pe.wait_ge(out_ev, 2 + ST)
            pe.wait_ge(hid_act, 2 * FC + FC * E)
            cross_attention("C")
            transposes_x("D", 0)
            channel_major("C", 1)
            project_d(0, "q")
            project_out("C", 1)

            project_d(0, "k", "v")
            transposes_x("D", 1)
            project_d(1, "q", "k", "v")
            scores_and_maxima("D")
            for kt in range(1, 4):
                scores_t("D", 0, 2 * kt)
                scores_t("D", 0, 2 * kt + 1)
                values_d(0, kt - 1)
            scores_t("D", 1, 0)
            scores_t("D", 1, 1)
            values_d(0, 3)
            scores_t("D", 1, 2)
            scores_t("D", 1, 3)
            values_d(1, 0)
            token_major_d(0)
            scores_t("D", 1, 4)
            scores_t("D", 1, 5)
            values_d(1, 1)
            channel_major_d(0)
            scores_t("D", 1, 6)
            scores_t("D", 1, 7)
            values_d(1, 2)
            project_out_d(0)
            values_d(1, 3)
            token_major_d(1)
            channel_major_d(1)
            project_out_d(1)

        @block.scalar
        def _(act):
            def job(name):
                n = JOB[name]
                act.wait_ge(job_mm, n + 1)
                return wk[:, n % 2, :]

            def take_xT(L, b):
                w = job(("xT", L, b))
                dst = xT[:, S * b:S * b + S]
                if L == "D":
                    act.activation(dst, w, ACT.Identity, scale=norm_w, bias=norm_b).then_inc(job_act, 1)
                else:
                    act.activation(dst, w, ACT.Copy).then_inc(job_act, 1)

            def exps(L, b, u):
                n = t_index(L, b, u)
                act.wait_ge(t_mm, n + 1)
                src = ts[:, 2 * (n % 2):2 * (n % 2) + 2, :].rearrange("p a b -> p (a b)")
                if L == "D":
                    kt, k = u // 2, u % 2
                    if b == 1 and u % 2 == 0:
                        if kt < TB - 1:
                            act.wait_ge(pr_used, kt + 1)
                        else:
                            act.wait_ge(job_mm, JOB["pv", L, 0, 1] + 1)
                    act.activation(pr2[:, kt, PACK_AT[k]:PACK_AT[k] + PACK_W[k]], src[:, 0:PACK_W[k]], ACT.Exp).then_inc(t_exp, 1)
                else:
                    if b == 1 and u % 2 == 0:
                        act.wait_ge(job_mm, JOB["pv", L, 0, u // 2] + 1)
                    act.activation(pr[:, 2 * u:2 * u + 2, :].rearrange("p h n -> p (h n)"), src, ACT.Exp).then_inc(t_exp, 1)

            act.wait_ge(setup_mm, 1)
            act.activation(wT[:, 0:4, :].rearrange("p i d -> p (i d)"), ts[:, 0, :], ACT.Copy).then_inc(setup_ev, 1)
            act.wait_ge(setup_mm, 2)
            act.activation(ctxT[:, :], ts[:, 1, P:P + B * NK], ACT.Copy)
            act.activation(col[:, 0:AROWS], ts[:, 1, 0:AROWS], ACT.Copy).then_inc(setup_ev, 1)
            act.wait_ge(setup_mm, 3)
            act.activation(mnegT[:, :], qm[:, 0, :].bitcast(BF16)[0:NK, :], ACT.Copy).then_inc(setup_ev, 1)
            act.wait_ge(setup_mm, 4)
            act.activation(someB[:, 0:S], qm[:, 1, :], ACT.Copy).then_inc(setup_ev, 1)
            take_xT("A", 0)
            act.wait_ge(setup_mm, 5)
            act.activation(someB[:, S:2 * S], ts[:, 3, :], ACT.Copy).then_inc(setup_ev, 1)
            take_xT("A", 1)

            act.wait_ge(gate_in, 32)
            act.activation(tg[:, :], gates_in[:, :], ACT.Tanh).then_inc(tg_ready, 1)
            for g in (1, 2):
                act.activation(wT[:, 4 * g:4 * g + 4, :].rearrange("p i d -> p (i d)"), job(("weights", g)), ACT.Copy).then_inc(job_act, 1)
            act.activation(col[:, AROWS:NROWS], job(("columns",))[:, AROWS:NROWS], ACT.Copy).then_inc(job_act, 1)

            def attention(L):
                for b in range(B):
                    for u in range(T_UNITS):
                        exps(L, b, u)

            attention("A")

            take_xT("B", 1)
            act.wait_ge(*done("logits"))
            act.activation(gates[:, :, :], lg[:, :, :], ACT.Exp).then_inc(ex_ready, 1)
            for n in range(2 * FC):
                c, b = n // 2, n % 2
                act.wait_ge(hid_mm, n + 1)
                k = ROW_AT["L0_ffn_sb1"] + c
                act.activation(hs[:, c, S * b:S * b + S], ts[:, n % 4, :], ACT.Silu, bias=col[:, k:k + 1]).then_inc(hid_act, 1)
            for n in range(ST // 4):
                w = job(("xg", n))
                act.activation(xgT[:, 512 * n:512 * n + 512], w, ACT.Copy).then_inc(job_act, 1)
            for e in range(E):
                if e >= 3:
                    last = 5 * ((e - 3) // 2) + (2 if (e - 3) % 2 == 0 else 4)
                    act.wait_ge(out_mm, 2 + last + 1)
                for c in range(FC):
                    n = 2 * FC + FC * e + c
                    act.wait_ge(hid_mm, n + 1)
                    k = ROW_AT["L0_ffn_b1"] + FC * e + c
                    act.activation(he[:, e % 3, c, :], ts[:, n % 4, 0:CAP], ACT.Silu, bias=col[:, k:k + 1]).then_inc(hid_act, 1)

            for b in range(B):
                take_xT("C", b)
            attention("C")
            take_xT("D", 1)
            attention("D")

        @block.vector
        def _(v):
            n_own = [0]

            def own(ins):
                n_own[0] += 1
                ins.then_inc(dve, 1)
                v.wait_ge(dve, n_own[0])

            def job(name):
                n = JOB[name]
                v.wait_ge(job_mm, n + 1)
                return wk[:, n % 2, :]

            def norm_stats(L, b):
                for t in range(TB):
                    m = v.bn_stats(stats[:, t, :], x[:, TB * b + t, :])
                own(m)
                for t in range(TB):
                    m = v.bn_aggr(mv[:, b, t, :], stats[:, t, :])
                own(m)
                if L == "D":
                    v.tensor_scalar(ve[:, b, 1, :], mv[:, b, :, 1], 1.0 + EPS, EPS * EPS, ALU.mult, ALU.add)
                v.tensor_scalar(ve[:, b, 0, :], mv[:, b, :, 1], EPS, None, ALU.add).then_inc(var_ready, 1)

            def norm(L, b):
                v.wait_ge(rstd_ready, LN[L, b] + 1)
                for t in range(TB):
                    v.tensor_scalar(xn[:, TB * b + t, 0:D], x[:, TB * b + t, :], mv[:, b, t, 0:1],
                                    rstd[:, b, 1 if L == "D" else 0, t:t + 1], ALU.subtract, ALU.mult).then_inc(xn_ready, 1)

            def split3(src, rest, dst, ready, before=None):
                def part(ins, s):
                    if before is None:
                        own(ins)
                    else:
                        ins.then_inc(ready, 1)
                        v.wait_ge(ready, before + s + 1)

                part(v.tensor_copy(dst[0], src), 0)
                own(v.tensor_tensor(rest, src, dst[0], ALU.subtract))
                part(v.tensor_copy(dst[1], rest), 1)
                v.tensor_tensor(dst[2], rest, dst[1], ALU.subtract).then_inc(ready, 1)

            def take_q(L, b):
                i = XI[L, b]
                if (L, b) == ("C", 1):
                    for k in range(2):
                        v.wait_ge(kd_out[k], 16)
                elif i >= 1:
                    last = {("A", 1): ("A", 0), ("C", 0): ("A", 1), ("D", 0): ("C", 0), ("D", 1): ("D", 0)}[L, b]
                    for s in range(3):
                        v.wait_ge(qd_out[XI[last]][s], 16)
                w = job(("q", L, b))
                if L == "A":
                    v.wait_ge(setup_ev, EV_SOME + b)
                    k = ROW_AT["L0_xattn_bq"]
                    m = v.scalar_tensor_tensor(qf[:, :], w, col[:, k:k + 1], someB[:, S * b:S * b + S], ALU.add, ALU.mult)
                elif L == "C":
                    m = v.tensor_copy(qf[:, :], w)
                else:
                    k = ROW_AT["L1_ffn_q_b"]
                    m = v.tensor_scalar(qf[:, :], w, col[:, k:k + 1], None, ALU.add)
                m.then_inc(job_dve, 1)
                v.wait_ge(*done("q", L, b))
                split3(qf[:, :], qr[:, :], [q_parts(L, b)[:, s, :] for s in range(3)], qparts_ready, 3 * i)

            def take_k2(b):
                for s in range(3):
                    v.wait_ge(qd_out[XI["C", 1]][s] if b == 0 else k2d_out[0][s], 16)
                w = job(("k", "D", b))
                k = ROW_AT["L1_ffn_k_b"]
                v.tensor_scalar(qf[:, :], w, col[:, k:k + 1], float(D) ** -0.5, ALU.add, ALU.mult).then_inc(job_dve, 1)
                v.wait_ge(*done("k", "D", b))
                split3(qf[:, :], qr[:, :], [parts[1][:, s, :] for s in range(3)], k2parts_ready, 3 * b)

            def take_v2(b):
                w = job(("v", "D", b))
                v.tensor_tensor(vst2[:, b, :, :, 0:DH2], w.rearrange("p (t h d) -> p t h d", t=TB, d=DH2),
                                bc[:, BC_AT["L1_ffn_v_b"], :].rearrange("p (h d) -> p h d", d=DH2).unsqueeze(1).broadcast_to([P, TB, H2, DH2]),
                                ALU.add).then_inc(job_dve, 1)

            def take_max(L, b, u):
                n = qm_index(L, b, u)
                v.wait_ge(qm_mm, n + 1)
                if L == "D":
                    e, h = QM2[u]
                    dst = nmx[:, :, :].rearrange("p t h -> p (t h)")[:, H2 * e + h:H2 * e + h + 1]
                    v.tensor_reduce(dst, q_bank(n), AX.X, ALU.max, negate=True).then_inc(qm_max, 1)
                else:
                    t, g = u // 4, u % 4
                    v.tensor_reduce(nmx[:, t, 4 * g:4 * g + 4], q_bank(n)[:, 0:4 * NK].rearrange("p (h k) -> p h k", k=NK),
                                    AX.X, ALU.max, negate=True).then_inc(qm_max, 1)

            def split_max(L, b):
                i = XI[L, b]
                nh = H2 if L == "D" else H
                v.wait_ge(qm_max, qm_index(L, b, QM_UNITS[L] - 1) + 1)
                if L == "D":
                    src = nmx[:, :, :].rearrange("p t h -> p (t h)")[:, 0:TB * nh].rearrange("p (t h) -> p t h", h=nh)
                    rest = nmr[:, :, :].rearrange("p t h -> p (t h)")[:, 0:TB * nh].rearrange("p (t h) -> p t h", h=nh)
                    sp_ = nsp[:, :, :, :].rearrange("p t s h -> p (t s h)")[:, 0:TB * 3 * nh].rearrange("p (t s h) -> p t s h", s=3, h=nh)
                else:
                    src, rest, sp_ = nmx[:, :, :], nmr[:, :, :], nsp[:, :, :, :]
                split3(src, rest, [sp_[:, :, s, :] for s in range(3)], nsp_ready)

            def take_nT(L, b):
                i = XI[L, b]
                nh = H2 if L == "D" else H
                if i >= 1:
                    v.wait_ge(nd_out[i - 1], 16)
                w = job(("nT", L, b))
                v.tensor_copy(nsT[0:3 * nh, :], w.bitcast(BF16)[0:3 * nh, 0:S]).then_inc(job_dve, 1)

            def take_pv(L, b, g):
                if L == "D":
                    w, taken_sem = (job(("pv", L, b, g)), job_dve) if b == 0 else (qm[:, g, :], pv1_taken)
                    if b == 1:
                        v.wait_ge(pv1_mm, g + 1)
                    if g == 0:
                        v.tensor_copy(oT[:, 0, 0:2 * P], w[:, 0:2 * P])
                        v.tensor_copy(oT[0:64, 0, 2 * P:3 * P], w[0:64, 2 * P:3 * P])
                        v.tensor_copy(oT[0:32, 0, 3 * P:4 * P], w[0:32, 3 * P:4 * P]).then_inc(taken_sem, 1)
                    else:
                        v.tensor_copy(oT[:, 1, 0:P], w[:, 0:P]).then_inc(taken_sem, 1)
                else:
                    w = job(("pv", L, b, g))
                    v.tensor_copy(oT[:, g, :], w).then_inc(job_dve, 1)

            def take_xT(L, b):
                w = job(("xT", L, b))
                dst = xT[:, S * b:S * b + S]
                if L == "D":
                    v.tensor_scalar(dst, w, norm_w, norm_b, ALU.mult, ALU.add).then_inc(job_dve, 1)
                else:
                    v.tensor_copy(dst, w).then_inc(job_dve, 1)

            def take_onT(L, b):
                w = job(("onT", L, b))
                if L == "D":
                    for e in range(TB):
                        n = D >> e
                        m = v.tensor_copy(onT[0:n, P * e:P * e + P], w[0:n, P * e:P * e + P])
                    m.then_inc(job_dve, 1)
                else:
                    v.tensor_copy(onT[:, :], w).then_inc(job_dve, 1)

            def divide(L, b, g):
                w = job(("oT", L, b, g))
                wv = w.rearrange("p (t j r) -> p t j r", t=TB, r=32)
                own(v.reciprocal(rden[:, :].rearrange("p (t j) -> p t j", t=TB), wv[:, :, :, DH]))
                v.tensor_tensor(on[:, :, 32 * g:32 * g + 32].rearrange("p t (j d) -> p t j d", d=DH),
                                wv[:, :, :, 0:DH],
                                rden[:, :].rearrange("p (t j) -> p t j", t=TB).unsqueeze(3).broadcast_to([P, TB, 4, DH]),
                                ALU.mult).then_inc(job_dve, 1)
                v.wait_ge(*done("oT", L, b, g))

            def divide_d(b):
                w = job(("oT", "D", b, 0))
                nb = len(BLOCKS)
                wv = w[:, 0:32 * nb].rearrange("p (n r) -> p n r", r=32)
                own(v.reciprocal(rden[:, 0:nb], wv[:, :, DH2]))
                v.tensor_tensor(on[:, :, :].rearrange("p t d -> p (t d)")[:, 0:DH2 * nb].rearrange("p (n d) -> p n d", d=DH2),
                                wv[:, :, 0:DH2], rden[:, 0:nb].unsqueeze(2).broadcast_to([P, nb, DH2]), ALU.mult).then_inc(job_dve, 1)

            def residual(L, b):
                w = job(("y", L, b))
                v.wait_ge(xb_ready, {"A": 0, "B": 2, "C": 4, "D": 6}[L] + b + 1)
                if L == "D":
                    for e in range(TB):
                        k = D >> e
                        o = xb[:, TB * b + e, 0:k]
                        m = v.scalar_tensor_tensor(o, w[:, P * e:P * e + k], tg[:, 3:4], o, ALU.mult, ALU.add)
                else:
                    g = 0 if L == "A" else 1
                    t = slice(TB * b, TB * b + TB)
                    m = v.scalar_tensor_tensor(x[:, t, :].rearrange("p t d -> p (t d)"), w, tg[:, g:g + 1],
                                               xb[:, t, :].rearrange("p t d -> p (t d)"), ALU.mult, ALU.add)
                m.then_inc(job_dve, 1)
                v.wait_ge(*done("y", L, b))

            def take_kv(L):
                k_in = (ts[:, 2, :] if L == 0 else wk[:, JOB["kv", "C"] % 2, :])[:, 0:B * NK]
                v_in = (ts[0:NK, 2, :] if L == 0 else wk[0:NK, JOB["kv", "C"] % 2, :])[:, 2 * P:4 * P]
                k = ROW_AT["L0_xattn_bk"]
                v.wait_ge(kpad, 2)
                if L == 0:
                    v.wait_ge(kv_mm, 1)
                    own(v.tensor_scalar(kf[:, :], k_in, col[:, k:k + 1], float(DH) ** -0.5, ALU.add, ALU.mult))
                else:
                    v.wait_ge(job_mm, JOB["kv", "C"] + 1)
                    own(v.tensor_scalar(kf[:, :], k_in, float(DH) ** -0.5, None, ALU.mult))
                split3(kf[:, :].rearrange("p (b k) -> p b k", b=B), kr[:, :].rearrange("p (b k) -> p b k", b=B),
                       [kparts[L][:, s, :, 0:NK] for s in range(3)], kparts_ready)
                v.wait_ge(const, C_VST)
                if L == 0:
                    v.wait_ge(bc_in, 32)
                for b in range(B):
                    src = v_in[:, P * b:P * b + P].rearrange("p (h d) -> p h d", d=DH)
                    dst = vst[L][0:NK, b, :, 0:DH]
                    if L == 0:
                        bv = bc[0:NK, BC_AT["L0_xattn_bv"], :].rearrange("p (h d) -> p h d", d=DH)
                        m = v.tensor_tensor(dst, src, bv, ALU.add)
                        m.then_inc(vst_ready, 1)
                    elif b == 0:
                        v.tensor_copy(dst, src)
                    else:
                        v.tensor_copy(dst, src).then_inc(job_dve, 1)

            LEAD = 4

            def maxima(L):
                for u in range(QM_UNITS[L]):
                    take_max(L, 0, u)
                split_max(L, 0)
                for u in range(LEAD):
                    take_max(L, 1, u)
                take_nT(L, 0)
                for u in range(LEAD, QM_UNITS[L]):
                    take_max(L, 1, u)
                split_max(L, 1)
                take_nT(L, 1)
                if L == "A":
                    take_kv(1)

            def cross_attention(L, following):
                maxima(L)
                take_pv(L, 0, 0)
                take_pv(L, 0, 1)
                divide(L, 0, 0)
                take_pv(L, 0, 2)
                divide(L, 0, 1)
                take_pv(L, 0, 3)
                divide(L, 0, 2)
                divide(L, 0, 3)
                take_pv(L, 1, 0)
                take_onT(L, 0)
                take_pv(L, 1, 1)
                residual(L, 0)
                norm_stats(following, 0)
                take_pv(L, 1, 2)
                take_pv(L, 1, 3)
                divide(L, 1, 0)
                divide(L, 1, 1)
                divide(L, 1, 2)
                norm(following, 0)
                divide(L, 1, 3)
                take_xT(following, 0)
                take_onT(L, 1)

            v.memset(kparts[0][:, :, :, NK:P], 0.0).then_inc(kpad, 1)
            v.memset(kparts[1][:, :, :, NK:P], 0.0).then_inc(kpad, 1)
            own(v.memset(nmx[:, :, :], 0.0))
            v.wait_ge(x_in[0], 16)
            norm_stats("A", 0)
            v.wait_ge(mask_in, 16)
            own(v.tensor_scalar(keep[:, :, :], mask_i[:, :, :], 0.0, None, ALU.not_equal))
            own(v.tensor_reduce(some[:, :], keep[:, :, :], AX.X, ALU.max))
            v.tensor_copy(some_b[:, :], some[:, :]).then_inc(some_ready, 1)
            own(v.tensor_scalar(none[:, :], some[:, :], -1.0, 1.0, ALU.mult, ALU.add))
            own(v.tensor_tensor(keep[:, :, :], keep[:, :, :], none[:, :].unsqueeze(2).broadcast_to([P, NT, NK]), ALU.max))
            v.tensor_scalar(mneg[:, :, :], keep[:, :, :], -1.0, None, ALU.add).then_inc(mneg_ready, 1)
            norm("A", 0)
            v.wait_ge(x_in[1], 16)
            norm_stats("A", 1)
            take_q("A", 0)
            norm("A", 1)
            take_kv(0)
            take_q("A", 1)
            v.wait_ge(tg_ready, 1)
            v.tensor_scalar(tgs[:, :], tg[:, 2:3], SHARED_SCALE, None, ALU.mult).then_inc(tgs_ready, 1)
            cross_attention("A", "B")
            residual("A", 1)
            norm_stats("B", 1)
            norm("B", 1)

            flat = lambda t: t[:, :, :, :].rearrange("p c t e -> p (c t e)")
            both = lambda t: t[:, :, :].unsqueeze(1).broadcast_to([P, 2, NT, E])
            wide = lambda t: t[:, :].unsqueeze(2).broadcast_to([P, NT, E])
            v.wait_ge(const, C_SIDX)
            w = job(("logits",))
            lv = w[:, 0:NT * E].rearrange("p (t e) -> p t e", e=E)
            own(v.tensor_reduce(best[:, :], lv, AX.X, ALU.max))
            v.tensor_tensor(lg[:, :, :], lv, wide(best), ALU.subtract).then_inc(job_dve, 1)
            v.wait_ge(ex_ready, 1)
            own(v.tensor_reduce(sums[:, :], gates[:, :, :], AX.X, ALU.add))
            own(v.reciprocal(sums[:, :], sums[:, :]))
            own(v.tensor_tensor(gates[:, :, :], gates[:, :, :], wide(sums), ALU.mult))

            def choose(src, c):
                own(v.tensor_reduce(best[:, :], src, AX.X, ALU.max))
                own(v.tensor_tensor(cand[:, :, :], src, wide(best), ALU.is_equal))
                own(v.tensor_tensor(cand[:, :, :], cand[:, :, :], iota8[:, :, :], ALU.mult))
                own(v.tensor_reduce(first[:, :], cand[:, :, :], AX.X, ALU.min))
                own(v.tensor_tensor(hot[:, c, :, :], iota8[:, :, :], wide(first), ALU.is_equal))

            choose(gates[:, :, :], 0)
            own(v.tensor_tensor(cand[:, :, :], iota8[:, :, :], wide(first), ALU.not_equal))
            own(v.tensor_tensor(gates2[:, :, :], gates[:, :, :], cand[:, :, :], ALU.mult))
            choose(gates2[:, :, :], 1)
            v.tensor_copy(flat(hotb), flat(hot)).then_inc(hot_ready, 1)
            w = job(("pos",))
            n = 2 * NT * E
            own(v.tensor_reduce(n1[:, 1, :], w[:, n:n + NT * E].rearrange("p (t e) -> p e t", e=E), AX.X, ALU.add))
            own(v.tensor_scalar(n1[:, 1, :], n1[:, 1, :], float(CAP), None, ALU.min))
            v.tensor_tensor(posn[:, :, :, :], w[:, 0:n].rearrange("p (c t e) -> p c t e", c=2, t=NT),
                            n1[:, :, :].unsqueeze(2).broadcast_to([P, 2, NT, E]), ALU.add).then_inc(job_dve, 1)
            v.wait_ge(*done("pos"))
            v.scalar_tensor_tensor(flat(kept), flat(posn), float(CAP), flat(hot), ALU.is_lt, ALU.mult)
            own(v.tensor_tensor(rt[:, :, :, :], posn[:, :, :, :],
                                base320[:, :].unsqueeze(1).unsqueeze(1).broadcast_to([P, 2, NT, E]), ALU.add))
            own(v.tensor_tensor(flat(rt), flat(rt), flat(hot), ALU.mult))
            v.tensor_reduce(s12[:, :, :], rt[:, :, :, :], AX.X, ALU.add)
            own(v.tensor_reduce(k12[:, :, :], kept[:, :, :, :], AX.X, ALU.add))
            own(v.tensor_scalar(k12[:, :, :], k12[:, :, :], -NONE, NONE, ALU.mult, ALU.add))
            v.tensor_tensor(slot_i[:, :, :], s12[:, :, :], k12[:, :, :], ALU.add).then_inc(slot_ready, 1)
            own(v.tensor_tensor(rt[:, :, :, :], kept[:, :, :, :], both(gates), ALU.mult))
            own(v.tensor_reduce(g12[:, :, :], rt[:, :, :, :], AX.X, ALU.add))
            own(v.tensor_tensor(den[:, :], g12[:, 0, :], g12[:, 1, :], ALU.add))
            own(v.tensor_scalar(den[:, :], den[:, :], FEPS, None, ALU.max))
            own(v.reciprocal(den[:, :], den[:, :]))
            own(v.tensor_scalar(den[:, :], den[:, :], tg[:, 2:3], None, ALU.mult))
            own(v.tensor_tensor(g12[:, :, :], g12[:, :, :], den[:, :].unsqueeze(1).broadcast_to([P, 2, NT]), ALU.mult))
            nv = n1s[:, :].rearrange("p (k r) -> p k r", r=5)
            pair = n1[:, 1, :].rearrange("p (k r) -> p k r", r=2)
            v.tensor_copy(nv[:, :, 0:2], pair[:, :, 0:1].broadcast_to([P, ST // 5, 2]))
            v.tensor_copy(nv[:, :, 3:5], pair[:, :, 1:2].broadcast_to([P, ST // 5, 2]))
            v.tensor_copy(nv[0:64, :, 2:3], pair[0:64, :, 0:1])
            own(v.tensor_copy(nv[64:P, :, 2:3], pair[64:P, :, 1:2]))
            own(v.tensor_tensor(n1s[:, :], sidx[:, :], n1s[:, :], ALU.is_ge))
            for b in range(B):
                v.wait_ge(xb_ready, 2 + b + 1)
                v.wait_ge(out_mm, b + 1)
                xv = xb[:, TB * b:TB * b + TB, :].rearrange("p t d -> p (t d)")
                v.scalar_tensor_tensor(xv, qm[:, b, :], tgs[:, 0:1], xv, ALU.mult, ALU.add).then_inc(out_ev, 1)
            for n in range(ST // 4):
                v.wait_ge(xg_in[n], 16)
            v.scalar_tensor_tensor(dst_i[:, :], n1s[:, :], float(NTOK), xg[:, :, D], ALU.mult, ALU.add).then_inc(dst_ready, 1)
            v.wait_ge(moe_in[2], 16 * (E + 1))
            for i in range(ST):
                v.wait_ge(out_mm, 2 + i + 1)
                if i >= 4:
                    v.wait_ge(y_scats[i % 4], 16 * (i // 4))
                k, r = 2 * (i // 5), i % 5
                src = qm[:, (2 + i) % 2, 0:D]
                if r == 2:
                    v.tensor_tensor(ostage[0:64, i % 4, :], src[0:64], b2[0:64, k, :], ALU.add)
                    m = v.tensor_tensor(ostage[64:P, i % 4, :], src[64:P], b2[64:P, k + 1, :], ALU.add)
                else:
                    m = v.tensor_tensor(ostage[:, i % 4, :], src, b2[:, k + (r > 2), :], ALU.add)
                m.then_inc(out_ev, 1)
            v.wait_ge(out_ev, 2)
            for b in range(B):
                v.wait_ge(y_in[b], 32)
                for t in range(TB * b, TB * b + TB):
                    m = v.scalar_tensor_tensor(xb[:, t, :], y12[:, 0, t, :], g12[:, 0, t:t + 1], xb[:, t, :], ALU.mult, ALU.add)
                own(m)
                for t in range(TB * b, TB * b + TB):
                    m = v.scalar_tensor_tensor(x[:, t, :], y12[:, 1, t, :], g12[:, 1, t:t + 1], xb[:, t, :], ALU.mult, ALU.add)
                m.then_inc(x_moe, 1)
                v.wait_ge(x_moe, b + 1)
                norm_stats("C", b)
                norm("C", b)

            take_q("C", 0)
            take_q("C", 1)
            cross_attention("C", "D")
            take_q("D", 0)
            residual("C", 1)
            norm_stats("D", 1)
            take_k2(0)
            norm("D", 1)
            take_v2(0)
            take_q("D", 1)
            take_k2(1)
            take_v2(1)
            maxima("D")
            take_pv("D", 0, 0)
            take_pv("D", 0, 1)
            divide_d(0)
            take_onT("D", 0)
            residual("D", 0)
            take_pv("D", 1, 0)
            take_pv("D", 1, 1)
            divide_d(1)
            take_onT("D", 1)
            residual("D", 1)


INS = ["x", "ctx_1024", "mask_Bx1xSxS2_ik1", "g_xattn", "g_ffn", "L0_xattn_Wq", "L0_xattn_bq", "L0_xattn_Wk",
       "L0_xattn_bk", "L0_xattn_Wv", "L0_xattn_bv", "L0_xattn_Wo", "L0_xattn_bo", "L0_ffn_router_w", "L0_ffn_w1",
       "L0_ffn_b1", "L0_ffn_w2", "L0_ffn_b2", "L0_ffn_sw1", "L0_ffn_sb1", "L0_ffn_sw2", "L0_ffn_sb2", "L1_xattn_Wv",
       "L1_xattn_Wk", "L1_xattn_Wq", "L1_xattn_Wo", "L1_xattn_bo", "L1_ffn_norm_w", "L1_ffn_norm_b", "L1_ffn_q_w",
       "L1_ffn_q_b", "L1_ffn_k_w", "L1_ffn_k_b", "L1_ffn_v_w", "L1_ffn_v_b", "L1_ffn_o_w", "L1_ffn_o_b"]


def kernel(**inputs):
    import concourse.bacc as bacc
    from concourse.bass_utils import run_bass_kernel_spmd

    nc = bacc.Bacc("TRN2", target_bir_lowering=False, num_devices=1)
    arrays, args = {}, {}
    for name in INS:
        arr = np.ascontiguousarray(inputs[name])
        arrays[f"in_{name}"] = arr
        args[name] = nc.dram_tensor(f"in_{name}", arr.shape, mybir.dt.from_np(arr.dtype), kind="ExternalInput").ap()
    out = nc.dram_tensor("out_x", (B, S, D), F32, kind="ExternalOutput").ap()
    build(nc, args, out)
    r = run_bass_kernel_spmd(nc, [arrays], core_ids=[0])
    return r.results[0]["out_x"]
```

```python
from contextlib import ExitStack

import numpy as np

import concourse.bass as bass
from concourse import mybir

F32 = mybir.dt.float32
BF16 = mybir.dt.bfloat16
I32 = mybir.dt.int32
U32 = mybir.dt.uint32
ALU = mybir.AluOpType
ACT = mybir.ActivationFunctionType
AX = mybir.AxisListType

P = 128
B = 2
S = 512
D = 128
NT = B * S // P
TB = S // P
H = 16
DH = D // H
NK = 77
E = 8
F = 512
FC = F // P
CAP = 320
SLOTS = E * CAP
ST = SLOTS // P
NTOK = B * S
ROW = D + 1
H2 = 8
DH2 = D // H2
EPS = 1e-5
SHARED_SCALE = 0.1
BIG = float(2.0 ** 100)
NONE = 4096.0
FEPS = float(np.finfo(np.float32).eps)

QROW = NK
MROW = QROW + 6 * DH
MROW2 = 6 * DH2
QPART = (0, 0, 0, 1, 1, 2)
KPART = (0, 1, 2, 0, 1, 0)
HEADS_OF_WEIGHT = {"L0_xattn_Wq": H, "L0_xattn_Wk": H, "L1_xattn_Wq": H, "L1_xattn_Wk": H, "L1_ffn_q_w": 8, "L1_ffn_k_w": 8}

HEADS_OF = [H2 >> e for e in range(TB)]
NQ = [P * sum(h < n for n in HEADS_OF) for h in range(H2)]
PACKS = [[(0, 0), (1, 512), (4, 896)], [(2, 0), (3, 256), (5, 512), (6, 640), (7, 768)]]
PACK_W = [1024, 896]
PACK_AT = [0, 1024]
P2W = sum(PACK_W)
P2AT = {h: PACK_AT[k] + at for k in range(2) for h, at in PACKS[k]}
QM2 = [(e, h) for e in range(TB) for h in range(HEADS_OF[e])]
O_AT = [[(0, 0)], [(1, 0), (4, 3 * P)], [(2, 0), (5, 2 * P), (6, 3 * P)], [(3, 0), (7, 2 * P)]]

WEIGHTS = ["L0_xattn_Wq", "L0_xattn_Wk", "L0_xattn_Wv", "L0_xattn_Wo",
           "L1_xattn_Wq", "L1_xattn_Wk", "L1_xattn_Wv", "L1_xattn_Wo",
           "L1_ffn_q_w", "L1_ffn_k_w", "L1_ffn_v_w", "L1_ffn_o_w"]
QK_ROWS = [("L0_xattn_bq", "L0_xattn_bk"), ("L1_ffn_q_b", "L1_ffn_k_b")]
ROWS = [("L0_ffn_b1", E * FC), ("L0_ffn_sb1", FC), ("L1_ffn_norm_w", 1), ("L1_ffn_norm_b", 1)]
ROW_AT = {"L0_xattn_bq": 0, "L0_xattn_bk": 1}
_n = 2
for _name, _k in ROWS:
    ROW_AT[_name] = _n
    _n += _k
NROWS = _n - 2
ROW_AT["L1_ffn_q_b"], ROW_AT["L1_ffn_k_b"] = _n, _n + 1
NCOLS = _n + 2
BC = ["L0_xattn_bv", "L0_xattn_bo", "L0_ffn_sb2", "L1_xattn_bo", "L1_ffn_v_b", "L1_ffn_o_b"]
BC_AT = {name: i for i, name in enumerate(BC)}


def work_jobs():
    jobs = []

    def add(who, *names):
        jobs.extend((name, who) for name in names)

    def cross_attention(L):
        add("dve", ("nT", L, 0))
        if L == "A":
            add("act", ("weights", 1), ("weights", 2), ("columns",))
        add("dve", ("pv", L, 0, 0), ("nT", L, 1))
        if L == "A":
            add("dve", ("kv", "C"))
        add("dve", *[("pv", L, 0, g) for g in range(1, 4)])
        add("dve", ("pv", L, 1, 0), ("onT", L, 0), ("pv", L, 1, 1), ("y", L, 0), ("pv", L, 1, 2), ("pv", L, 1, 3))
        add("act", ("xT", "B" if L == "A" else "D", 0), ("onT", L, 1))

    for b in range(B):
        add("act", ("xT", "A", b))
        add("dve", ("q", "A", b))
    cross_attention("A")
    add("dve", ("y", "A", 1), ("logits", 0))
    add("act", ("xT", "B", 1))
    add("dve", ("logits", 1), ("pos", 0), ("pos", 1))
    add("act", *[("xg", n) for n in range(ST // 4)])
    for b in range(B):
        add("act", ("xT", "C", b), ("q", "C", b))
    cross_attention("C")
    add("dve", ("y", "C", 1))
    add("act", ("q", "D", 0), ("k", "D", 0))
    add("dve", ("v", "D", 0))
    add("act", ("xT", "D", 1), ("q", "D", 1), ("k", "D", 1))
    add("dve", ("v", "D", 1))
    add("dve", ("nT", "D", 0), ("nT", "D", 1), ("pv", "D", 0))
    for b in range(B):
        add("dve", ("oT", "D", b, 0), ("onT", "D", b), ("y", "D", b))
    return jobs


JOBS = work_jobs()
JOB = {name: n for n, (name, _) in enumerate(JOBS)}


def taken(n):
    who = JOBS[n][1]
    return who, sum(1 for _, w in JOBS[:n + 1] if w == who)


LN = {(L, b): 2 * i + b for i, L in enumerate("ABCD") for b in range(B)}
XI = {("A", 0): 0, ("A", 1): 1, ("C", 0): 2, ("C", 1): 3, ("D", 0): 4, ("D", 1): 5}
O_N = {(L, b, k): 4 * i + 2 * b + k + 1 for i, L in enumerate("AC") for b in range(B) for k in range(2)}
QM_UNITS = {"A": 16, "C": 16, "D": len(QM2)}
T_UNITS = 8
LEAD = 4
T_AFTER = {"A": (9, 11, 13, 15), "C": (9, 11, 13, 15), "D": (8, 10, 12, 14)}


def qm_index(L, b, u):
    before = {"A": 0, "C": 32, "D": 64}[L]
    return before + b * QM_UNITS[L] + u


def t_index(L, b, u):
    return ({"A": 0, "C": 2, "D": 4}[L] + b) * T_UNITS + u


def build(nc, a, out):
    with ExitStack() as ctx:
        def sb(name, shape, dt=F32):
            return ctx.enter_context(nc.sbuf_tensor(name, shape, dt))

        def sem(name):
            return ctx.enter_context(nc.semaphore(name))

        def dram(name, shape, dt):
            return nc.dram_tensor(name, shape, dt, kind="Internal").ap()

        qm = ctx.enter_context(nc.psum_tensor("qm", [P, 2, 512], F32))
        ts = ctx.enter_context(nc.psum_tensor("ts", [P, 4, 512], F32))
        wk = ctx.enter_context(nc.psum_tensor("wk", [P, 2, 512], F32))

        x = sb("x", [P, NT, D])
        xn = sb("xn", [P, NT, ROW])
        xb = sb("xb", [P, NT, D])
        xT = sb("xT", [P, NTOK])
        ctx_sb = sb("ctx_sb", [NK, B, D])
        ctxT = sb("ctxT", [P, B * NK])
        early = sb("early", [P, ST * ROW])
        mask_i = early[:, 0:NT * NK].bitcast(I32).rearrange("p (t k) -> p t k", k=NK)
        keep = early[:, NT * NK:2 * NT * NK].rearrange("p (t k) -> p t k", k=NK)
        someB = early[:, 2 * NT * NK:2 * NT * NK + NTOK]
        xg = early[:, :].rearrange("p (i r) -> p i r", r=ROW)
        fill = sb("fill", [P, ROW])
        some = sb("some", [P, NT])
        some_b = sb("some_b", [P, NT], BF16)
        none = sb("none", [P, NT])
        mneg = sb("mneg", [P, NT, NK], BF16)
        mnegT = sb("mnegT", [NK, NTOK], BF16)
        y12 = sb("y12", [P, 2, NT, D])
        wn = y12[:, :, :, :].rearrange("p c t d -> p (c t) d")[:, 0:12, :]
        wT = sb("wT", [P, 12, D])
        rows = sb("rows", [NROWS, D])
        setup = y12[0:2, :, :, :].rearrange("p c t d -> p (c t) d")
        qk_rows = setup[:, 12:14, :]
        qk_perm = setup[:, 14:16, :]
        col = sb("col", [P, NCOLS])
        bc = sb("bc", [P, len(BC), D])
        gates_in = sb("gates_in", [P, 4])
        tg = sb("tg", [P, 4])
        tgs = sb("tgs", [P, 1])
        bk2 = sb("bk2", [P, 1])
        rw = sb("rw", [P, E])
        w1 = sb("w1", [P, E, F])
        w2 = sb("w2", [P, E, FC, D])
        b2 = sb("b2", [P, E, D])
        sw1 = sb("sw1", [P, F])
        sw2 = sb("sw2", [P, FC, D])
        ident = sb("ident", [P, P])
        identb = sb("identb", [P, P], BF16)
        onesb = sb("onesb", [P, P], BF16)
        trib = sb("trib", [P, P], BF16)
        half = sb("half", [P, 8])
        stats = sb("stats", [P, TB, 6])
        mv = sb("mv", [P, B, TB, 2])
        ve = sb("ve", [P, B, 2, TB])
        rstd = sb("rstd", [P, B, 2, TB])
        rtg = sb("rtg", [P, B, TB])
        qf = sb("qf", [P, S])
        kf2 = early[:, 0:S]
        qr = sb("qr", [P, S])
        kf = sb("kf", [P, B * NK])
        kr = sb("kr", [P, B * NK])
        parts = [sb(f"parts{i}", [P, 3 * S], BF16)[:, :].rearrange("p (s n) -> p s n", s=3) for i in range(2)]
        qst = sb("qst", [P, B, H, S], BF16)
        kst = sb("kst", [P, 2, H, B, P], BF16)
        kst2 = w1[:, :, :].rearrange("p e f -> p (e f)").bitcast(BF16).rearrange("p (b h n) -> p b h n", b=B, h=H2)
        vst = [sb(f"vst{i}", [P, B, H, 32]) for i in range(2)]
        vst2 = w2[:, :, :, :].rearrange("p e c h -> p (e c h)")[:, 0:B * TB * H2 * 32].rearrange(
            "p (b t h r) -> p b t h r", b=B, t=TB, h=H2)
        nmx = sb("nmx", [P, TB, H])
        nmr = sb("nmr", [P, TB, H])
        nsp = sb("nsp", [P, TB, 3, H], BF16)
        nsT = sb("nsT", [3 * H, S], BF16)
        pr = sb("pr", [P, H, S])
        oo = sb("oo", [P, 4 * S + TB * D])
        oT = oo[:, 0:4 * S].rearrange("p (g n) -> p g n", g=4)
        on = oo[:, 4 * S:4 * S + TB * D].rearrange("p (t d) -> p t d", d=D)
        rden = sb("rden", [P, 32])
        onT = sb("onT", [P, S])

        pr_flat = pr[:, :, :].rearrange("p a b -> p (a b)")
        pr2 = pr_flat[:, 0:TB * P2W].rearrange("p (k c) -> p k c", k=TB)
        hs = pr_flat[:, 0:FC * NTOK].rearrange("p (c n) -> p c n", c=FC)
        he = pr_flat[:, FC * NTOK:FC * NTOK + 3 * FC * CAP].rearrange("p (r c n) -> p r c n", r=3, c=FC)
        xgT = oo[:, :]
        ostage = onT[:, :].rearrange("p (i d) -> p i d", d=D)
        kparts = [t[:, 0:3 * B * P].rearrange("p (s b k) -> p s b k", s=3, b=B)
                  for t in (pr_flat.bitcast(BF16), parts[1].rearrange("p s n -> p (s n)"))]
        sums = sb("sums", [P, NT])
        lg, gates, gates2, cand = (qf[:, NT * E * i:NT * E * i + NT * E].rearrange("p (t e) -> p t e", e=E) for i in range(4))
        hot, rt = (qr[:, 2 * NT * E * i:2 * NT * E * (i + 1)].rearrange("p (c t e) -> p c t e", c=2, e=E) for i in range(2))
        best = sb("best", [P, NT])
        first = sb("first", [P, NT])
        iota8 = sb("iota8", [P, NT, E])
        iota8i = sb("iota8i", [P, NT, E], I32)
        toki = sb("toki", [P, NT], I32)
        hotb = sb("hotb", [P, 2, NT, E], BF16)
        n1 = sb("n1", [P, E])
        g12 = sb("g12", [P, 2, NT])
        p12 = sb("p12", [P, 2, NT])
        k12 = sb("k12", [P, 2, NT])
        s12 = sb("s12", [P, 2, NT])
        den = sb("den", [P, NT])
        slot_i = sb("slot_i", [P, 2, NT], I32)
        sidx_i = sb("sidx_i", [P, ST], I32)
        sidx = sb("sidx", [P, ST])
        sidx_t = sb("sidx_t", [P, ST])
        n1s = sb("n1s", [P, ST])
        dst_i = sb("dst_i", [P, ST], I32)

        xs_d = dram("xs_d", [SLOTS, ROW], F32)
        y_d = dram("y_d", [2 * NTOK, D], F32)

        x_in = [sem(f"x_in{b}") for b in range(B)]
        ctx_in, mask_in, rows_in, rows2_in, gate_in, bc_in = (
            sem(n) for n in ("ctx_in", "mask_in", "rows_in", "rows2_in", "gate_in", "bc_in"))
        bc2_in, rows3_in = sem("bc2_in"), sem("rows3_in")
        perm_ready = [sem(f"perm_ready{i}") for i in range(2)]
        w_in = [sem(f"w_in{i}") for i in range(3)]
        moe_in = [sem(f"moe_in{i}") for i in range(3)]
        const = sem("const")
        dve = sem("dve_chain")
        pol = sem("pool_chain")
        mneg_ready, some_ready = sem("mneg_ready"), sem("some_ready")
        setup_mm, setup_ev = sem("setup_mm"), sem("setup_ev")
        tg_ready, tgs_ready, bias_ready = sem("tg_ready"), sem("tgs_ready"), sem("bias_ready")
        kv_mm, kparts_ready, vst_ready = sem("kv_mm"), sem("kparts_ready"), sem("vst_ready")
        kst_in = [sem(f"kst_in{i}") for i in range(2)]
        mask_rows_in = [sem(f"mask_rows_in{b}") for b in range(B)]
        var_ready, rstd_ready, xn_ready, xb_ready = sem("var_ready"), sem("rstd_ready"), sem("xn_ready"), sem("xb_ready")
        job_mm, job_dve, job_act = sem("job_mm"), sem("job_dve"), sem("job_act")
        qparts_ready, k2parts_ready, kpad = sem("qparts_ready"), sem("k2parts_ready"), sem("kpad")
        qst_in = [sem(f"qst_in{i}") for i in range(6)]
        k2st_in = [sem(f"k2st_in{i}") for i in range(2)]
        nst_in = [sem(f"nst_in{i}") for i in range(6)]
        qm_mm, qm_max, nsp_ready = sem("qm_mm"), sem("qm_max"), sem("nsp_ready")
        t_mm, t_exp = sem("t_mm"), sem("t_exp")
        pr_used = sem("pr_used")
        pv1_mm, pv1_taken = sem("pv1_mm"), sem("pv1_taken")
        bk2_ready = sem("bk2_ready")
        o_mm, o_taken = sem("o_mm"), sem("o_taken")
        xT_zero = sem("xT_zero")
        x_moe = sem("x_moe")
        ex_ready, hot_ready, slot_ready, dst_ready = (sem(n) for n in ("ex_ready", "hot_ready", "slot_ready", "dst_ready"))
        hid_mm, hid_act, out_mm, out_ev = sem("hid_mm"), sem("hid_act"), sem("out_mm"), sem("out_ev")
        fill_src, fill_xs, fill_y, scat = (sem(n) for n in ("fill_src", "fill_xs", "fill_y", "scat"))
        xg_in = [sem(f"xg_in{n}") for n in range(ST // 4)]
        y_in = [sem(f"y_in{b}") for b in range(B)]
        y_scats = [sem(f"y_scat{i}") for i in range(4)]
        out_sem = sem("out_sem")

        def done(*name):
            who, value = taken(JOB[name])
            return (job_dve if who == "dve" else job_act), value

        norm_w, norm_b = (col[:, ROW_AT[n]:ROW_AT[n] + 1] for n in ("L1_ffn_norm_w", "L1_ffn_norm_b"))

        EV_WEIGHTS, EV_SOME0, EV_CONTEXT, EV_MASK, EV_SOME1 = range(1, 6)

        def q_bank(L, b, u):
            n = qm_index(L, b, u)
            if b == 1 and u > T_AFTER[L][0] - 2:
                return qm[:, n % 2, :], 2
            return (qm if n % 4 < 2 else ts)[:, n % 4, :], 4

        def o_banks(b, k):
            return ts[:, 0:2, :] if b == 1 and k == 1 else qm[:, 0:2, :]

        def q_parts(L, b):
            return parts[1 if L != "D" and b == 1 else 0]

        C_IDENT, C_HALF, C_IDENTB, C_ONES, C_KST, C_KID, C_VST, C_KST1, C_TRI, C_IOTA, C_SIDX, C_KST2 = range(2, 14)

        x_dram = a["x"].rearrange("b (t p) d -> p b t d", p=P)
        out_dram = out.rearrange("b (t p) d -> p b t d", p=P)

        block = ctx.enter_context(nc.Block())

        @block.sync
        def _(sp):
            def bcast(name):
                return a[name].partition_broadcast(P)

            def row(name):
                src = a[name]
                src = src.rearrange("e (c p) -> (e c) p", p=D) if len(src.shape) == 2 else src.rearrange("(c p) -> c p", p=D)
                at = ROW_AT[name] - 2
                return rows[at:at + dict(ROWS)[name], :], src

            def weights(g):
                for i in range(4 * g, 4 * g + 4):
                    sp.dma_start(wn[:, i, :], a[WEIGHTS[i]]).then_inc(w_in[g], 16)

            def k_ones(L):
                for b in range(B):
                    sp.dma_start(kst[MROW:MROW + 3, L, :, b, 0:NK], onesb[0:3, 0:NK].unsqueeze(1).broadcast_to([3, H, NK])).then_inc(kst_in[L], 16)

            def k_stack(L):
                sp.wait_ge(kparts_ready, L + 1)
                for j, part in enumerate(KPART):
                    sp.dma_start(kst[QROW + DH * j:QROW + DH * j + DH, L, :, :, :].rearrange("p h b k -> p h (b k)"),
                                 kparts[L][:, part, :, :].rearrange("p b k -> p (b k)")).then_inc(kst_in[L], 16)

            def q_stack(L, b):
                i = XI[L, b]
                dh, nh, row0 = (DH2, H2, 0) if L == "D" else (DH, H, QROW)
                for part in range(3):
                    sp.wait_ge(qparts_ready, 3 * i + part + 1)
                    for j in (j for j in range(6) if QPART[j] == part):
                        sp.dma_start(qst[row0 + dh * j:row0 + dh * j + dh, b, 0:nh, :], q_parts(L, b)[:, part, :]).then_inc(qst_in[i], 16)

            def k2_stack(b):
                for part in range(3):
                    sp.wait_ge(k2parts_ready, 3 * b + part + 1)
                    for j in (j for j in range(6) if KPART[j] == part):
                        sp.dma_start(kst2[DH2 * j:DH2 * j + DH2, b, :, :], parts[1][:, part, :]).then_inc(k2st_in[b], 16)

            def max_rows(L, b):
                i = XI[L, b]
                nh = H2 if L == "D" else H
                row = MROW2 if L == "D" else MROW
                sp.wait_ge(*done("nT", L, b))
                sp.dma_start(qst[row:row + 3, b, 0:nh, :], nsT[0:3 * nh, :]).then_inc(nst_in[i], 16)

            sp.dma_start(x[:, 0:TB, :], x_dram[:, 0]).then_inc(x_in[0], 16)
            sp.dma_start(mask_i[:, :, :], a["mask_Bx1xSxS2_ik1"].rearrange("b o (t p) k -> p (b o t) k", p=P)).then_inc(mask_in, 16)
            weights(0)
            sp.dma_start(ctx_sb[:, :, :], a["ctx_1024"].rearrange("b k d -> k b d")).then_inc(ctx_in, 16)
            for j, name in enumerate(QK_ROWS[0]):
                sp.dma_start(qk_rows[j:j + 1, 0, :], a[name].rearrange("(c p) -> c p", p=D)).then_inc(rows_in, 16)
            sp.dma_start(x[:, TB:NT, :], x_dram[:, 1]).then_inc(x_in[1], 16)
            for i, name in enumerate(BC[:2]):
                sp.dma_start(bc[:, BC_AT[name], :], bcast(name)).then_inc(bc_in, 16)
            weights(1)
            sp.wait_ge(const, C_KST)
            k_ones(0)
            for j, name in enumerate(QK_ROWS[1]):
                sp.dma_start(qk_rows[j:j + 1, 1, :], a[name].rearrange("(c p) -> c p", p=D)).then_inc(rows3_in, 16)
            k_stack(0)
            q_stack("A", 0)
            q_stack("A", 1)
            sp.dma_start(gates_in[:, 0:2], bcast("g_xattn")).then_inc(gate_in, 16)
            sp.dma_start(gates_in[:, 2:4], bcast("g_ffn")).then_inc(gate_in, 16)
            weights(2)
            for name, _ in ROWS:
                sp.dma_start(*row(name)).then_inc(rows2_in, 16)
            max_rows("A", 0)
            for name in BC[2:]:
                sp.dma_start(bc[:, BC_AT[name], :], bcast(name)).then_inc(bc2_in, 16)
            sp.wait_ge(const, C_KST1)
            k_ones(1)
            sp.dma_start(rw[:, :], a["L0_ffn_router_w"]).then_inc(moe_in[0], 16)
            sp.dma_start(sw1[:, :], a["L0_ffn_sw1"]).then_inc(moe_in[0], 16)
            sp.dma_start(sw2[:, :, :], a["L0_ffn_sw2"].rearrange("(c p) h -> p c h", p=P)).then_inc(moe_in[0], 16)
            max_rows("A", 1)
            k_stack(1)
            for e in range(E):
                sp.dma_start(w1[:, e, :], a["L0_ffn_w1"][e]).then_inc(moe_in[1], 16)
                sp.dma_start(w2[:, e, :, :], a["L0_ffn_w2"][e].rearrange("(c p) h -> p c h", p=P)).then_inc(moe_in[2], 16)
            sp.dma_start(b2[:, :, :], bcast("L0_ffn_b2")).then_inc(moe_in[2], 16)

            sp.wait_ge(fill_src, 1)
            sp.dma_start(xs_d.rearrange("(i p) r -> p i r", p=P), fill[:, :].unsqueeze(1).broadcast_to([P, ST, ROW])).then_inc(fill_xs, 16)
            sp.dma_start(y_d.rearrange("(c t p) d -> p (c t) d", p=P, t=NT), fill[:, 0:D].unsqueeze(1).broadcast_to([P, 2 * NT, D])).then_inc(fill_y, 16)

            sp.wait_ge(scat, 16 * 2 * NT)
            xs_v = xs_d.rearrange("(i p) r -> p i r", p=P)
            for n in range(ST // 4):
                sp.dma_start(xg[:, 4 * n:4 * n + 4, :], xs_v[:, 4 * n:4 * n + 4, :]).then_inc(xg_in[n], 16)
            for i in range(4):
                sp.wait_ge(y_scats[i], 16 * (ST // 4))
            y_v = y_d.rearrange("(c t p) d -> p c t d", p=P, t=NT)
            for b in range(B):
                for c in range(2):
                    t = slice(TB * b, TB * b + TB)
                    sp.dma_start(y12[:, c, t, :], y_v[:, c, t, :]).then_inc(y_in[b], 16)

            for b in range(B):
                q_stack("C", b)
            for b in range(B):
                max_rows("C", b)
            for b in range(B):
                q_stack("D", b)
                k2_stack(b)
            for b in range(B):
                max_rows("D", b)
            for b in range(B):
                sp.wait_ge(*done("y", "D", b))
                sp.dma_start(out_dram[:, b], xb[:, TB * b:TB * b + TB, :]).then_inc(out_sem, 16)
            sp.wait_ge(out_sem, 32)

        @block.gpsimd
        def _(pool):
            n_own = [0]

            def own(ins):
                n_own[0] += 1
                ins.then_inc(pol, 1)
                pool.wait_ge(pol, n_own[0])

            pool.memset(ident[:, :], 0.0).then_inc(const, 1)
            pool.wait_ge(const, 1)
            pool.affine_select(out=ident[:, :], in_=ident[:, :], compare_op=ALU.not_equal, fill=1.0, base=0,
                               pattern=[[-1, P]], channel_multiplier=1).then_inc(const, 1)
            pool.memset(half[:, :], -0.5).then_inc(const, 1)
            pool.wait_ge(const, C_IDENT)
            pool.tensor_copy(identb[:, :], ident[:, :]).then_inc(const, 1)
            pool.memset(onesb[:, :], 1.0).then_inc(const, 1)

            def pow_rstd(L, b):
                n = 2 if L == "D" else 1
                pool.wait_ge(var_ready, LN[L, b] + 1)
                pool.tensor_tensor(rstd[:, b, 0:n, :], ve[:, b, 0:n, :],
                                   half[:, 0:n * TB].rearrange("p (n t) -> p n t", n=n), ALU.pow).then_inc(rstd_ready, 1)

            pool.wait_ge(const, C_HALF)
            pow_rstd("A", 0)
            pool.memset(kst[:, 0, :, :, :].rearrange("p h b k -> p (h b k)").bitcast(U32), 0).then_inc(const, 1)
            pow_rstd("A", 1)
            def mask_rows(b):
                c = slice(S * b, S * b + S)
                pool.dma_start(qst[0:NK, b, :, :], mnegT[:, c].unsqueeze(1).broadcast_to([NK, H, S])).then_inc(mask_rows_in[b], 16)

            pool.wait_ge(setup_ev, EV_MASK)
            mask_rows(0)
            pool.wait_ge(const, C_KST)
            kid = kst[0:NK, 0, :, :, 0:NK].rearrange("p h b k -> p (h b) k")
            pool.affine_select(out=kid, in_=kid, compare_op=ALU.not_equal, fill=BIG, base=0,
                               pattern=[[0, H * B], [-1, NK]], channel_multiplier=1).then_inc(const, 1)
            for L in range(2):
                own(pool.memset(vst[L][:, :, :, :], 0.0))
            for L in range(2):
                m = pool.memset(vst[L][0:NK, :, :, DH:DH + 1], 1.0)
                if L == 0:
                    own(m)
            m.then_inc(const, 1)
            pool.memset(kst[:, 1, :, :, :].rearrange("p h b k -> p (h b k)").bitcast(U32), 0).then_inc(const, 1)
            pool.affine_select(out=trib[:, :], in_=onesb[:, :], compare_op=ALU.is_gt, fill=0.0, base=0,
                               pattern=[[1, P]], channel_multiplier=-1).then_inc(const, 1)
            pool.wait_ge(qst_in[XI["A", 0]], 96)
            mask_rows(1)
            pool.memset(fill[:, 0:D], 0.0)
            pool.memset(fill[:, D:ROW], NONE).then_inc(fill_src, 1)
            own(pool.iota(iota8i[:, :, :], pattern=[[0, NT], [1, E]], base=-E, channel_multiplier=0))
            own(pool.tensor_copy(iota8[:, :, :], iota8i[:, :, :]))
            own(pool.iota(toki[:, :], pattern=[[P, NT]], base=0, channel_multiplier=1))
            pool.tensor_copy(xn[:, :, D], toki[:, :]).then_inc(const, 1)
            own(pool.iota(sidx_i[:, :], pattern=[[0, ST // 5], [P, 5]], base=0, channel_multiplier=1))
            own(pool.tensor_copy(sidx[:, :], sidx_i[:, :]))
            own(pool.tensor_scalar(sidx_t[:, :], sidx[:, :], float(CAP), float(-CAP), ALU.is_ge, ALU.mult))
            pool.tensor_tensor(sidx[:, :], sidx[:, :], sidx_t[:, :], ALU.add).then_inc(const, 1)

            def x_bias(L, b, row, x_ready, value):
                pool.wait_ge(x_ready, value)
                t = slice(TB * b, TB * b + TB)
                pool.tensor_tensor(xb[:, t, :], x[:, t, :], bc[:, row, :].unsqueeze(1).broadcast_to([P, TB, D]),
                                   ALU.add).then_inc(xb_ready, 1)

            pool.wait_ge(rows3_in, 32)
            pool.tensor_copy(qk_perm[:, 1, :].rearrange("c (d h) -> c h d", h=H2),
                             qk_rows[:, 1, :].rearrange("c (h d) -> c h d", h=H2)).then_inc(perm_ready[1], 1)
            pool.wait_ge(bc_in, 32)
            pool.wait_ge(bc2_in, 16 * (len(BC) - 2))
            pool.wait_ge(tg_ready, 1)
            pool.wait_ge(tgs_ready, 1)
            pool.tensor_scalar(bc[:, BC_AT["L0_xattn_bo"], :], bc[:, BC_AT["L0_xattn_bo"], :], tg[:, 0:1], None, ALU.mult).then_inc(bias_ready, 1)
            pool.tensor_scalar(bc[:, BC_AT["L1_xattn_bo"], :], bc[:, BC_AT["L1_xattn_bo"], :], tg[:, 1:2], None, ALU.mult).then_inc(bias_ready, 1)
            pool.tensor_scalar(bc[:, BC_AT["L0_ffn_sb2"], :], bc[:, BC_AT["L0_ffn_sb2"], :], tgs[:, 0:1], None, ALU.mult).then_inc(bias_ready, 1)
            pool.tensor_scalar(bc[:, BC_AT["L1_ffn_o_b"], :], bc[:, BC_AT["L1_ffn_o_b"], :], tg[:, 3:4], None, ALU.mult).then_inc(bias_ready, 1)
            pool.wait_ge(bias_ready, 4)
            for b in range(B):
                x_bias("A", b, BC_AT["L0_xattn_bo"], x_in[b], 16)

            for b in range(B):
                pow_rstd("B", b)
            for b in range(B):
                x_bias("B", b, BC_AT["L0_ffn_sb2"], *done("y", "A", b))
            pool.wait_ge(fill_xs, 16)
            for c in range(2):
                pool.wait_ge(slot_ready, c + 1)
                for t in range(NT):
                    pool.indirect_dma_start(xs_d, bass.IndirectOffsetOnAxis(ap=slot_i[:, c, t:t + 1], axis=0),
                                            xn[:, t, :], None, bounds_check=SLOTS - 1, oob_is_err=False).then_inc(scat, 16)
            pool.wait_ge(dst_ready, 1)
            pool.wait_ge(fill_y, 16)
            for i in range(ST):
                pool.wait_ge(out_ev, 2 + i + 1)
                pool.indirect_dma_start(y_d, bass.IndirectOffsetOnAxis(ap=dst_i[:, i:i + 1], axis=0),
                                        ostage[:, i % 4, :], None, bounds_check=2 * NTOK - 1, oob_is_err=False).then_inc(y_scats[i % 4], 16)

            for b in range(B):
                pow_rstd("C", b)
            for b in range(B):
                x_bias("C", b, BC_AT["L1_xattn_bo"], x_moe, b + 1)

            pool.wait_ge(out_mm, 2 + ST)
            own(pool.memset(vst2, 0.0))
            own(pool.memset(vst2[:, :, :, :, DH2:DH2 + 1], 1.0))
            pool.memset(kst2[MROW2:MROW2 + 3, :, :, :], 1.0).then_inc(const, 1)
            pool.wait_ge(const, C_KST2)

            for b in range(B):
                pool.wait_ge(*done("q", "C", b))
                pool.memset(xT[:, S * b + P:S * b + S], 0.0).then_inc(xT_zero, 1)
            for b in range(B):
                pow_rstd("D", b)
            for b in range(B):
                pool.wait_ge(rstd_ready, LN["D", b] + 1)
                own(pool.tensor_scalar(rtg[:, b, :], rstd[:, b, 0, :], tg[:, 3:4], None, ALU.mult))
                for t in range(TB):
                    m = pool.tensor_scalar(xb[:, TB * b + t, :], x[:, TB * b + t, :], mv[:, b, t, 0:1], rtg[:, b, t:t + 1],
                                           ALU.subtract, ALU.mult)
                own(m)
                own(pool.tensor_tensor(xb[:, TB * b:TB * b + TB, :], xb[:, TB * b:TB * b + TB, :], x[:, TB * b:TB * b + TB, :], ALU.add))
                for t in range(TB):
                    k = D >> t
                    m = pool.tensor_tensor(xb[:, TB * b + t, 0:k], xb[:, TB * b + t, 0:k], bc[:, BC_AT["L1_ffn_o_b"], 0:k], ALU.add)
                m.then_inc(xb_ready, 1)

        @block.tensor
        def _(pe):
            def wait_bank(n):
                if n >= 2:
                    who, value = taken(n - 2)
                    pe.wait_ge(job_dve if who == "dve" else job_act, value)
                return wk[:, n % 2, :]

            def transposes_x(L, b):
                w = wait_bank(JOB["xT", L, b])
                for t in range(TB):
                    pe.wait_ge(xn_ready, TB * LN[L, b] + t + 1)
                    m = pe.transpose(w[:, P * t:P * t + P], xn[:, TB * b + t, 0:D], ident[:, :])
                m.then_inc(job_mm, 1)

            def x_cols(b, t=None):
                return xT[:, S * b:S * b + S] if t is None else xT[:, S * b + P * t:S * b + P * t + P]

            def wait_taken(name):
                pe.wait_ge(*done(*name))

            def project_q(L, b):
                w = wait_bank(JOB["q", L, b])
                wait_taken(("xT", L, b))
                pe.matmul(w, wT[:, 0 if L == "A" else 4, :], x_cols(b), start=True, stop=True).then_inc(job_mm, 1)

            def project_d(b, name):
                w = wait_bank(JOB[name, "D", b])
                wait_taken(("xT", "D", b))
                if name == "v":
                    for t in range(TB):
                        m = pe.matmul(w[:, P * t:P * t + P], x_cols(b, t), wT[:, 10, :], start=True, stop=True)
                else:
                    m = pe.matmul(w, wT[:, 8 if name == "q" else 9, :], x_cols(b), start=True, stop=True)
                m.then_inc(job_mm, 1)

            def scores_q(L, b, u):
                n = qm_index(L, b, u)
                bank, back = q_bank(L, b, u)
                if n >= back:
                    pe.wait_ge(qm_max, n - back + 1)
                if u == 0:
                    pe.wait_ge(qst_in[XI[L, b]], 96)
                    if L == "A":
                        pe.wait_ge(mask_rows_in[b], 16)
                        pe.wait_ge(kst_in[0], 16 * 8)
                        pe.wait_ge(const, C_KID)
                    if L == "C":
                        pe.wait_ge(kst_in[1], 16 * 8)
                    if L == "D":
                        pe.wait_ge(k2st_in[b], 96)
                        pe.wait_ge(const, C_KST2)
                if L == "D":
                    e, h = QM2[u]
                    m = pe.matmul(bank, qst[0:MROW2, b, h, P * e:P * e + P],
                                  kst2[0:MROW2, b, h, :], start=True, stop=True)
                else:
                    t, g = u // 4, u % 4
                    for j in range(4):
                        h = 4 * g + j
                        m = pe.matmul(bank[:, NK * j:NK * j + NK], qst[0:MROW, b, h, P * t:P * t + P],
                                      kst[0:MROW, 0 if L == "A" else 1, h, b, 0:NK], start=True, stop=True)
                m.then_inc(qm_mm, 1)

            def transposes_max(L, b):
                nh = 3 * (H2 if L == "D" else H)
                w = wait_bank(JOB["nT", L, b])
                pe.wait_ge(nsp_ready, XI[L, b] + 1)
                wb = w.bitcast(BF16)
                src = nsp[:, :, :, :].rearrange("p t s h -> p (t s h)")
                for t in range(TB):
                    m = pe.transpose(wb[0:nh, P * t:P * t + P], src[:, nh * t:nh * t + nh], identb[:, :])
                m.then_inc(job_mm, 1)

            def scores_t(L, b, u):
                n = t_index(L, b, u)
                if u == 0:
                    pe.wait_ge(nst_in[XI[L, b]], 16)
                if b == 0 and u < 2:
                    pe.wait_ge(qm_max, qm_index(L, 1, T_AFTER[L][0] - 2) + 1)
                if n >= 2:
                    pe.wait_ge(t_exp, n - 1)
                dst = ts[:, 2 * (n % 2):2 * (n % 2) + 2, :].rearrange("p a b -> p (a b)")
                if L == "D":
                    kt, k = u // 2, u % 2
                    for h, at in PACKS[k]:
                        m = pe.matmul(dst[:, at:at + NQ[h]], kst2[0:MROW2 + 3, b, h, P * kt:P * kt + P],
                                      qst[0:MROW2 + 3, b, h, 0:NQ[h]], start=True, stop=True)
                else:
                    for j in range(2):
                        h = 2 * u + j
                        m = pe.matmul(dst[:, S * j:S * j + S], kst[:, 0 if L == "A" else 1, h, b, :],
                                      qst[:, b, h, :], start=True, stop=True)
                m.then_inc(t_mm, 1)

            def values(L, b, g):
                w = wait_bank(JOB["pv", L, b, g])
                if b == 0 and g == 0:
                    pe.wait_ge(vst_ready, 2)
                pe.wait_ge(t_exp, t_index(L, b, 2 * g + 1) + 1)
                for j in range(4):
                    h = 4 * g + j
                    m = pe.matmul(w[32 * j:32 * j + 32, :], vst[0 if L == "A" else 1][:, b, h, :], pr[:, h, :],
                                  start=True, stop=True)
                m.then_inc(job_mm, 1)

            def values_d(b, kt):
                bank = wk[:, JOB["pv", "D", 0] % 2, :] if b == 0 else qm[:, 0, :]
                if kt == 0:
                    if b == 0:
                        wait_bank(JOB["pv", "D", 0])
                    wait_taken(("v", "D", b))
                pe.wait_ge(t_exp, t_index("D", b, 2 * kt + 1) + 1)
                for i in range(3):
                    for j in range(4):
                        if i < len(O_AT[j]):
                            h, at = O_AT[j][i]
                            m = pe.matmul(bank[32 * j:32 * j + 32, at:at + NQ[h]], vst2[:, b, kt, h, :],
                                          pr2[:, kt, P2AT[h]:P2AT[h] + NQ[h]],
                                          start=(kt == 0 and i == 0), stop=(kt == TB - 1), skip_group_check=True)
                if kt == TB - 1:
                    m.then_inc(job_mm if b == 0 else pv1_mm, 1)
                elif b == 0:
                    m.then_inc(pr_used, 1)

            def token_major(L, b, k):
                wait_taken(("pv", L, b, 2 * k + 1))
                if (b, k) in ((0, 1), (1, 0)):
                    pe.wait_ge(o_taken, O_N[L, b, k] - 1)
                for i in range(2):
                    for t in range(TB):
                        m = pe.transpose(o_banks(b, k)[:, i, P * t:P * t + P], oT[:, 2 * k + i, P * t:P * t + P], ident[:, :])
                m.then_inc(o_mm, 1)

            def channel_major(L, b):
                w = wait_bank(JOB["onT", L, b])
                pe.wait_ge(o_taken, O_N[L, b, 1])
                for t in range(TB):
                    m = pe.transpose(w[:, P * t:P * t + P], on[:, t, :], ident[:, :])
                m.then_inc(job_mm, 1)

            def project_out(L, b):
                w = wait_bank(JOB["y", L, b])
                wait_taken(("onT", L, b))
                for t in range(TB):
                    m = pe.matmul(w[:, P * t:P * t + P], onT[:, P * t:P * t + P], wT[:, 3 if L == "A" else 7, :],
                                  start=True, stop=True)
                m.then_inc(job_mm, 1)

            def token_major_d(b):
                w = wait_bank(JOB["oT", "D", b, 0])
                if b == 0:
                    wait_taken(("pv", "D", 0))
                else:
                    pe.wait_ge(pv1_taken, 1)
                for t in range(TB):
                    n = P if t < TB - 1 else 96
                    m = pe.transpose(w[:, P * t:P * t + n], oT[0:n, 0, P * t:P * t + P], ident[0:n, 0:n])
                m.then_inc(job_mm, 1)

            def channel_major_d(b):
                w = wait_bank(JOB["onT", "D", b])
                wait_taken(("oT", "D", b, 0))
                for e in range(TB):
                    n = D >> e
                    m = pe.transpose(w[0:n, P * e:P * e + P], on[:, e, 0:n], ident[:, :])
                m.then_inc(job_mm, 1)

            def project_out_d(b):
                w = wait_bank(JOB["y", "D", b])
                wait_taken(("onT", "D", b))
                for e in range(TB):
                    n = D >> e
                    m = pe.matmul(w[:, P * e:P * e + n], onT[0:n, P * e:P * e + P], wT[0:n, 11, 0:n], start=True, stop=True)
                m.then_inc(job_mm, 1)

            def later_weights():
                for g in (1, 2):
                    w = wait_bank(JOB["weights", g])
                    pe.wait_ge(w_in[g], 64)
                    for i in range(4):
                        m = pe.transpose(w[:, P * i:P * i + P], wn[:, 4 * g + i, :], ident[:, :])
                    m.then_inc(job_mm, 1)
                w = wait_bank(JOB["columns",])
                pe.wait_ge(rows2_in, 16 * len(ROWS))
                pe.wait_ge(perm_ready[1], 1)
                pe.transpose(w[:, 2:2 + NROWS], rows[:, :], ident[0:NROWS, 0:NROWS])
                pe.transpose(w[:, 2 + NROWS:NCOLS], qk_perm[:, 1, :], ident[0:2, 0:2]).then_inc(job_mm, 1)

            def logits(b):
                w = wait_bank(JOB["logits", b])
                wait_taken(("xT", "B", b))
                if b == 0:
                    pe.wait_ge(moe_in[0], 48)
                for t in range(TB):
                    m = pe.matmul(w[:, E * t:E * t + E], x_cols(b, t), rw[:, :], start=True, stop=True)
                m.then_inc(job_mm, 1)

            def positions(c):
                w = wait_bank(JOB["pos", c])
                pe.wait_ge(hot_ready, c + 1)
                chosen = hotb[:, c, :, :].rearrange("p t e -> p (t e)")
                wv = w[:, 0:NT * E].rearrange("p (t e) -> p t e", t=NT)
                pe.matmul(w[:, 0:NT * E], trib[:, :], chosen, start=True, stop=False, skip_group_check=True)
                for t in range(NT - 1):
                    m = pe.matmul(wv[:, t + 1:, :], onesb[:, :], hotb[:, c, t, :].unsqueeze(1).broadcast_to([P, NT - 1 - t, E]),
                                  start=False, stop=(c == 1 and t == NT - 2), skip_group_check=True)
                if c == 0:
                    m = pe.matmul(w[:, NT * E:2 * NT * E], onesb[:, :], chosen, start=False, stop=True, skip_group_check=True)
                m.then_inc(job_mm, 1)

            def key_product(k_out, layer):
                return pe.matmul(k_out, wT[:, 4 * layer + 1, :], ctxT[:, :], start=True, stop=True)

            def value_products(v_out, layer):
                for b in range(B):
                    m = pe.matmul(v_out[:, P * b:P * b + P], ctxT[:, NK * b:NK * b + NK], wT[:, 4 * layer + 2, :],
                                  start=True, stop=True)
                return m

            def some_rows(b, bank):
                pe.wait_ge(some_ready, 1)
                for t in range(TB):
                    tt = TB * b + t
                    m = pe.matmul(bank[:, P * t:P * t + P], some_b[:, tt:tt + 1].broadcast_to([P, P]), identb[:, :], start=True, stop=True)
                m.then_inc(setup_mm, 1)

            def keys_and_values_c():
                w = wait_bank(JOB["kv", "C"])
                wait_taken(("weights", 1))
                key_product(w[:, 0:B * NK], 1)
                value_products(w[0:NK, 2 * P:4 * P], 1).then_inc(job_mm, 1)

            def scores_and_maxima(L):
                for u in range(QM_UNITS[L]):
                    scores_q(L, 0, u)
                for u in range(LEAD):
                    scores_q(L, 1, u)
                transposes_max(L, 0)
                if L == "A":
                    later_weights()
                for u in range(LEAD, QM_UNITS[L]):
                    scores_q(L, 1, u)
                    if u in T_AFTER[L]:
                        scores_t(L, 0, T_AFTER[L].index(u))
                (values_d(0, 0) if L == "D" else values(L, 0, 0))
                transposes_max(L, 1)
                if L == "A":
                    keys_and_values_c()

            def cross_attention(L):
                scores_and_maxima(L)
                for k in range(2, 4):
                    scores_t(L, 0, 2 * k)
                    scores_t(L, 0, 2 * k + 1)
                    values(L, 0, k - 1)
                token_major(L, 0, 0)
                scores_t(L, 1, 0)
                scores_t(L, 1, 1)
                values(L, 0, 3)
                token_major(L, 0, 1)
                scores_t(L, 1, 2)
                scores_t(L, 1, 3)
                values(L, 1, 0)
                channel_major(L, 0)
                scores_t(L, 1, 4)
                scores_t(L, 1, 5)
                values(L, 1, 1)
                project_out(L, 0)
                scores_t(L, 1, 6)
                scores_t(L, 1, 7)
                values(L, 1, 2)
                token_major(L, 1, 0)
                values(L, 1, 3)
                token_major(L, 1, 1)
                transposes_x("B" if L == "A" else "D", 0)
                channel_major(L, 1)

            pe.wait_ge(const, C_IDENT)
            pe.wait_ge(w_in[0], 64)
            for i in range(4):
                m = pe.transpose(ts[:, 0, P * i:P * i + P], wn[:, i, :], ident[:, :])
            m.then_inc(setup_mm, 1)
            pe.wait_ge(const, C_IDENTB)
            some_rows(0, qm[:, 1, :])
            pe.wait_ge(perm_ready[0], 1)
            pe.wait_ge(ctx_in, 16)
            pe.transpose(ts[:, 1, 0:2], qk_perm[:, 0, :], ident[0:2, 0:2])
            for b in range(B):
                m = pe.transpose(ts[:, 1, P + NK * b:P + NK * b + NK], ctx_sb[:, b, :], ident[0:NK, 0:NK])
            m.then_inc(setup_mm, 1)
            transposes_x("A", 0)
            pe.wait_ge(setup_ev, EV_CONTEXT)
            key_product(ts[:, 2, 0:B * NK], 0).then_inc(kv_mm, 1)
            project_q("A", 0)
            pe.wait_ge(mneg_ready, 1)
            for t in range(NT):
                m = pe.transpose(qm[:, 0, :].bitcast(BF16)[0:NK, P * t:P * t + P], mneg[:, t, :], identb[:, :])
            m.then_inc(setup_mm, 1)
            value_products(ts[0:NK, 1, 2 * P:4 * P], 0).then_inc(kv_mm, 1)
            transposes_x("A", 1)
            some_rows(1, ts[:, 3, :])
            project_q("A", 1)

            pe.wait_ge(setup_ev, EV_SOME1)
            pe.wait_ge(vst_ready, 2)
            pe.wait_ge(kparts_ready, 1)
            cross_attention("A")
            project_out("A", 1)
            logits(0)

            transposes_x("B", 1)
            logits(1)

            def hidden(n, lhs, rhs, width):
                if n >= 4:
                    pe.wait_ge(hid_act, n - 3)
                elif n == 0:
                    pe.wait_ge(t_exp, t_index("A", 1, T_UNITS - 1) + 1)
                pe.matmul(ts[:, n % 4, 0:width], lhs, rhs, start=True, stop=True).then_inc(hid_mm, 1)

            for c in range(FC):
                for b in range(B):
                    hidden(2 * c + b, sw1[:, P * c:P * c + P], x_cols(b), S)
                if c < 2:
                    positions(c)
            for b in range(B):
                pe.wait_ge(hid_act, 2 * FC)
                if b == 0:
                    pe.wait_ge(qm_max, qm_index("A", 1, 15) + 1)
                for t in range(TB):
                    for c in range(FC):
                        m = pe.matmul(qm[:, b, P * t:P * t + P], hs[:, c, S * b + P * t:S * b + P * t + P], sw2[:, c, :],
                                      start=(c == 0), stop=(c == FC - 1))
                m.then_inc(out_mm, 1)
            for n in range(ST // 4):
                w = wait_bank(JOB["xg", n])
                pe.wait_ge(xg_in[n], 16)
                for j in range(4):
                    m = pe.transpose(w[:, P * j:P * j + P], xg[:, 4 * n + j, 0:D], ident[:, :])
                m.then_inc(job_mm, 1)

            def expert_hidden(e):
                if e == 0:
                    pe.wait_ge(moe_in[1], 16 * E)
                who, value = taken(JOB["xg", (CAP * (e + 1) - 1) // 512])
                pe.wait_ge(job_act, value)
                for c in range(FC):
                    hidden(2 * FC + FC * e + c, w1[:, e, P * c:P * c + P], xgT[:, CAP * e:CAP * e + CAP], CAP)

            def expert_out(i):
                n = 2 + i
                pe.wait_ge(out_ev, n - 1)
                k, r = 2 * (i // 5), i % 5
                pieces = {0: [(k, 0, P, 0)], 1: [(k, P, P, 0)], 2: [(k, 2 * P, 64, 0), (k + 1, 0, 64, 64)],
                          3: [(k + 1, 64, P, 0)], 4: [(k + 1, 64 + P, P, 0)]}[r]
                for e, s0, m_, p0 in pieces:
                    pe.wait_ge(hid_act, 2 * FC + FC * e + FC)
                    for c in range(FC):
                        m = pe.matmul(qm[p0:p0 + m_, n % 2, 0:D], he[:, e % 3, c, s0:s0 + m_], w2[:, e, c, :],
                                      start=(c == 0), stop=(c == FC - 1))
                m.then_inc(out_mm, 1)

            expert_hidden(0)
            pe.wait_ge(moe_in[2], 16 * (E + 1))
            for e in range(E):
                if e + 1 < E:
                    expert_hidden(e + 1)
                for i in ((5 * (e // 2), 5 * (e // 2) + 1) if e % 2 == 0 else (5 * (e // 2) + 2, 5 * (e // 2) + 3, 5 * (e // 2) + 4)):
                    expert_out(i)

            transposes_x("C", 0)
            project_q("C", 0)
            transposes_x("C", 1)
            project_q("C", 1)
            pe.wait_ge(out_ev, 2 + ST)
            pe.wait_ge(hid_act, 2 * FC + FC * E)
            cross_attention("C")
            project_out("C", 1)

            project_d(0, "q")
            project_d(0, "k")
            project_d(0, "v")
            transposes_x("D", 1)
            project_d(1, "q")
            project_d(1, "k")
            project_d(1, "v")
            scores_and_maxima("D")
            for kt in range(2, 4):
                scores_t("D", 0, 2 * kt)
                scores_t("D", 0, 2 * kt + 1)
                values_d(0, kt - 1)
            scores_t("D", 1, 0)
            scores_t("D", 1, 1)
            values_d(0, 3)
            scores_t("D", 1, 2)
            scores_t("D", 1, 3)
            values_d(1, 0)
            token_major_d(0)
            scores_t("D", 1, 4)
            scores_t("D", 1, 5)
            values_d(1, 1)
            channel_major_d(0)
            scores_t("D", 1, 6)
            scores_t("D", 1, 7)
            values_d(1, 2)
            project_out_d(0)
            values_d(1, 3)
            token_major_d(1)
            channel_major_d(1)
            project_out_d(1)

        @block.scalar
        def _(act):
            def job(name):
                n = JOB[name]
                act.wait_ge(job_mm, n + 1)
                return wk[:, n % 2, :]

            def take_weights(g, w):
                nh = HEADS_OF_WEIGHT[WEIGHTS[4 * g]]
                act.activation(wT[:, 4 * g:4 * g + 2, :].rearrange("p i (d h) -> p i h d", h=nh),
                               w[:, 0:2 * P].rearrange("p (i h d) -> p i h d", i=2, h=nh), ACT.Copy)
                return act.activation(wT[:, 4 * g + 2:4 * g + 4, :].rearrange("p i d -> p (i d)"), w[:, 2 * P:4 * P], ACT.Copy)

            def take_xT(L, b):
                w = job(("xT", L, b))
                dst = xT[:, S * b:S * b + S]
                if L == "D":
                    act.wait_ge(xT_zero, b + 1)
                    for t in range(TB):
                        n = D >> t
                        m = act.activation(dst[0:n, P * t:P * t + P], w[0:n, P * t:P * t + P], ACT.Identity,
                                           scale=norm_w[0:n], bias=norm_b[0:n])
                    m.then_inc(job_act, 1)
                else:
                    act.activation(dst, w, ACT.Copy).then_inc(job_act, 1)

            def take_onT(L, b):
                act.activation(onT[:, :], job(("onT", L, b)), ACT.Copy).then_inc(job_act, 1)

            def take_qk(L, b, name):
                w = job((name, L, b))
                if name == "q":
                    i = XI[L, b]
                    dst, high, ready, before = qf[:, :], q_parts(L, b)[:, 0, :], qparts_ready, 3 * i
                    scale, bias = 1.0, col[:, ROW_AT["L1_ffn_q_b"]:ROW_AT["L1_ffn_q_b"] + 1]
                    if (L, b) == ("C", 1):
                        act.wait_ge(kst_in[1], 16 * 8)
                    else:
                        act.wait_ge(qst_in[XI[{("C", 0): ("A", 0), ("D", 0): ("C", 0), ("D", 1): ("D", 0)}[L, b]]], 96)
                else:
                    dst, high, ready, before = kf2, parts[1][:, 0, :], k2parts_ready, 3 * b
                    scale, bias = float(D) ** -0.5, bk2[:, 0:1]
                    if b == 0:
                        act.wait_ge(bk2_ready, 1)
                    act.wait_ge(qst_in[XI["C", 1]] if b == 0 else k2st_in[0], 96)
                if before > 0:
                    act.wait_ge(ready, before)
                if L == "C":
                    act.activation(dst, w, ACT.Copy).then_inc(job_act, 1)
                else:
                    act.activation(dst, w, ACT.Identity, scale=scale, bias=bias).then_inc(job_act, 1)
                act.wait_ge(*done(name, L, b))
                act.activation(high, dst, ACT.Copy).then_inc(ready, 1)

            def exps(L, b, u):
                n = t_index(L, b, u)
                act.wait_ge(t_mm, n + 1)
                src = ts[:, 2 * (n % 2):2 * (n % 2) + 2, :].rearrange("p a b -> p (a b)")
                if L == "D":
                    kt, k = u // 2, u % 2
                    if b == 1 and u % 2 == 0:
                        if kt < TB - 1:
                            act.wait_ge(pr_used, kt + 1)
                        else:
                            act.wait_ge(job_mm, JOB["pv", L, 0] + 1)
                    act.activation(pr2[:, kt, PACK_AT[k]:PACK_AT[k] + PACK_W[k]], src[:, 0:PACK_W[k]], ACT.Exp).then_inc(t_exp, 1)
                else:
                    if b == 1 and u % 2 == 0:
                        act.wait_ge(job_mm, JOB["pv", L, 0, u // 2] + 1)
                    act.activation(pr[:, 2 * u:2 * u + 2, :].rearrange("p h n -> p (h n)"), src, ACT.Exp).then_inc(t_exp, 1)

            act.wait_ge(setup_mm, 1)
            take_weights(0, ts[:, 0, :]).then_inc(setup_ev, 1)
            act.wait_ge(setup_mm, 2)
            act.activation(someB[:, 0:S], qm[:, 1, :], ACT.Copy).then_inc(setup_ev, 1)
            act.wait_ge(setup_mm, 3)
            act.activation(ctxT[:, :], ts[:, 1, P:P + B * NK], ACT.Copy)
            act.activation(col[:, 0:2], ts[:, 1, 0:2], ACT.Copy).then_inc(setup_ev, 1)
            take_xT("A", 0)
            act.wait_ge(setup_mm, 4)
            act.activation(mnegT[:, :], qm[:, 0, :].bitcast(BF16)[0:NK, :], ACT.Copy).then_inc(setup_ev, 1)
            take_xT("A", 1)
            act.wait_ge(setup_mm, 5)
            act.activation(someB[:, S:2 * S], ts[:, 3, :], ACT.Copy).then_inc(setup_ev, 1)

            act.wait_ge(gate_in, 32)
            act.activation(tg[:, :], gates_in[:, :], ACT.Tanh).then_inc(tg_ready, 1)
            for g in (1, 2):
                take_weights(g, job(("weights", g))).then_inc(job_act, 1)
            act.activation(col[:, 2:NCOLS], job(("columns",))[:, 2:NCOLS], ACT.Copy).then_inc(job_act, 1)

            def attention(L):
                for b in range(B):
                    for u in range(T_UNITS):
                        exps(L, b, u)

            attention("A")

            take_xT("B", 0)
            take_onT("A", 1)

            take_xT("B", 1)
            act.wait_ge(*done("logits", 1))
            act.activation(gates[:, :, :], lg[:, :, :], ACT.Exp).then_inc(ex_ready, 1)
            for n in range(2 * FC):
                c, b = n // 2, n % 2
                act.wait_ge(hid_mm, n + 1)
                k = ROW_AT["L0_ffn_sb1"] + c
                act.activation(hs[:, c, S * b:S * b + S], ts[:, n % 4, :], ACT.Silu, bias=col[:, k:k + 1]).then_inc(hid_act, 1)
            for n in range(ST // 4):
                w = job(("xg", n))
                act.activation(xgT[:, 512 * n:512 * n + 512], w, ACT.Copy).then_inc(job_act, 1)
            for e in range(E):
                if e >= 3:
                    last = 5 * ((e - 3) // 2) + (2 if (e - 3) % 2 == 0 else 4)
                    act.wait_ge(out_mm, 2 + last + 1)
                for c in range(FC):
                    n = 2 * FC + FC * e + c
                    act.wait_ge(hid_mm, n + 1)
                    k = ROW_AT["L0_ffn_b1"] + FC * e + c
                    act.activation(he[:, e % 3, c, :], ts[:, n % 4, 0:CAP], ACT.Silu, bias=col[:, k:k + 1]).then_inc(hid_act, 1)

            for b in range(B):
                take_xT("C", b)
                take_qk("C", b, "q")
            attention("C")
            take_xT("D", 0)
            take_onT("C", 1)
            take_qk("D", 0, "q")
            take_qk("D", 0, "k")
            take_xT("D", 1)
            take_qk("D", 1, "q")
            take_qk("D", 1, "k")
            attention("D")

        @block.vector
        def _(v):
            n_own = [0]

            def own(ins):
                n_own[0] += 1
                ins.then_inc(dve, 1)
                v.wait_ge(dve, n_own[0])

            def job(name):
                n = JOB[name]
                v.wait_ge(job_mm, n + 1)
                return wk[:, n % 2, :]

            def norm_stats(L, b):
                for t in range(TB):
                    m = v.bn_stats(stats[:, t, :], x[:, TB * b + t, :])
                own(m)
                for t in range(TB):
                    m = v.bn_aggr(mv[:, b, t, :], stats[:, t, :])
                own(m)
                if L == "D":
                    v.tensor_scalar(ve[:, b, 1, :], mv[:, b, :, 1], 1.0 + EPS, EPS * EPS, ALU.mult, ALU.add)
                v.tensor_scalar(ve[:, b, 0, :], mv[:, b, :, 1], EPS, None, ALU.add).then_inc(var_ready, 1)

            def norm(L, b):
                v.wait_ge(rstd_ready, LN[L, b] + 1)
                for t in range(TB):
                    v.tensor_scalar(xn[:, TB * b + t, 0:D], x[:, TB * b + t, :], mv[:, b, t, 0:1],
                                    rstd[:, b, 1 if L == "D" else 0, t:t + 1], ALU.subtract, ALU.mult).then_inc(xn_ready, 1)

            def split3(src, rest, dst, ready, before=None):
                def part(ins, s):
                    if before is None:
                        own(ins)
                    else:
                        ins.then_inc(ready, 1)
                        v.wait_ge(ready, before + s + 1)

                part(v.tensor_copy(dst[0], src), 0)
                own(v.tensor_tensor(rest, src, dst[0], ALU.subtract))
                part(v.tensor_copy(dst[1], rest), 1)
                v.tensor_tensor(dst[2], rest, dst[1], ALU.subtract).then_inc(ready, 1)

            def take_q(L, b):
                i = XI[L, b]
                w = job(("q", L, b))
                v.wait_ge(setup_ev, EV_CONTEXT if b == 0 else EV_SOME1)
                k = ROW_AT["L0_xattn_bq"]
                v.scalar_tensor_tensor(qf[:, :], w, col[:, k:k + 1], someB[:, S * b:S * b + S], ALU.add, ALU.mult).then_inc(job_dve, 1)
                v.wait_ge(*done("q", L, b))
                split3(qf[:, :], qr[:, :], [q_parts(L, b)[:, s, :] for s in range(3)], qparts_ready, 3 * i)

            def split_rest(L, b, name):
                src, dst, ready, before = ((qf[:, :], q_parts(L, b), qparts_ready, 3 * XI[L, b]) if name == "q" else
                                           (kf2, parts[1], k2parts_ready, 3 * b))
                v.wait_ge(ready, before + 1)
                own(v.tensor_tensor(qr[:, :], src, dst[:, 0, :], ALU.subtract))
                v.tensor_copy(dst[:, 1, :], qr[:, :]).then_inc(ready, 1)
                v.wait_ge(ready, before + 2)
                v.tensor_tensor(dst[:, 2, :], qr[:, :], dst[:, 1, :], ALU.subtract).then_inc(ready, 1)
                v.wait_ge(ready, before + 3)

            def take_v2(b):
                w = job(("v", "D", b))
                v.tensor_tensor(vst2[:, b, :, :, 0:DH2], w.rearrange("p (t h d) -> p t h d", t=TB, d=DH2),
                                bc[:, BC_AT["L1_ffn_v_b"], :].rearrange("p (h d) -> p h d", d=DH2).unsqueeze(1).broadcast_to([P, TB, H2, DH2]),
                                ALU.add).then_inc(job_dve, 1)

            def take_max(L, b, u):
                n = qm_index(L, b, u)
                v.wait_ge(qm_mm, n + 1)
                if L == "D":
                    e, h = QM2[u]
                    dst = nmx[:, :, :].rearrange("p t h -> p (t h)")[:, H2 * e + h:H2 * e + h + 1]
                    v.tensor_reduce(dst, q_bank(L, b, u)[0], AX.X, ALU.max, negate=True).then_inc(qm_max, 1)
                else:
                    t, g = u // 4, u % 4
                    v.tensor_reduce(nmx[:, t, 4 * g:4 * g + 4], q_bank(L, b, u)[0][:, 0:4 * NK].rearrange("p (h k) -> p h k", k=NK),
                                    AX.X, ALU.max, negate=True).then_inc(qm_max, 1)

            def split_max(L, b):
                i = XI[L, b]
                nh = H2 if L == "D" else H
                v.wait_ge(qm_max, qm_index(L, b, QM_UNITS[L] - 1) + 1)
                if L == "D":
                    src = nmx[:, :, :].rearrange("p t h -> p (t h)")[:, 0:TB * nh].rearrange("p (t h) -> p t h", h=nh)
                    rest = nmr[:, :, :].rearrange("p t h -> p (t h)")[:, 0:TB * nh].rearrange("p (t h) -> p t h", h=nh)
                    sp_ = nsp[:, :, :, :].rearrange("p t s h -> p (t s h)")[:, 0:TB * 3 * nh].rearrange("p (t s h) -> p t s h", s=3, h=nh)
                else:
                    src, rest, sp_ = nmx[:, :, :], nmr[:, :, :], nsp[:, :, :, :]
                split3(src, rest, [sp_[:, :, s, :] for s in range(3)], nsp_ready)

            def take_nT(L, b):
                i = XI[L, b]
                nh = H2 if L == "D" else H
                if i >= 1:
                    v.wait_ge(nst_in[i - 1], 16)
                w = job(("nT", L, b))
                v.tensor_copy(nsT[0:3 * nh, :], w.bitcast(BF16)[0:3 * nh, 0:S]).then_inc(job_dve, 1)

            def take_pv(L, b, g):
                if L == "D":
                    if b == 0:
                        w, taken_sem = job(("pv", "D", 0)), job_dve
                    else:
                        w, taken_sem = qm[:, 0, :], pv1_taken
                        v.wait_ge(pv1_mm, 1)
                    v.tensor_copy(oT[:, 0, 0:3 * P], w[:, 0:3 * P])
                    v.tensor_copy(oT[0:96, 0, 3 * P:4 * P], w[0:96, 3 * P:4 * P]).then_inc(taken_sem, 1)
                else:
                    w = job(("pv", L, b, g))
                    v.tensor_copy(oT[:, g, :], w).then_inc(job_dve, 1)

            def take_onT(L, b):
                w = job(("onT", L, b))
                if L == "D":
                    for e in range(TB):
                        n = D >> e
                        m = v.tensor_copy(onT[0:n, P * e:P * e + P], w[0:n, P * e:P * e + P])
                    m.then_inc(job_dve, 1)
                else:
                    v.tensor_copy(onT[:, :], w).then_inc(job_dve, 1)

            def divide(L, b, k):
                n = O_N[L, b, k]
                v.wait_ge(o_mm, n)
                w = o_banks(b, k)
                own(v.reciprocal(rden[:, :].rearrange("p (i n) -> p i n", i=2), w.rearrange("p i (n r) -> p i n r", r=32)[:, :, :, DH]))
                for i in range(2):
                    g = 2 * k + i
                    m = v.tensor_tensor(on[:, :, 32 * g:32 * g + 32].rearrange("p t (j d) -> p t j d", d=DH),
                                        w[:, i, :].rearrange("p (t j r) -> p t j r", t=TB, r=32)[:, :, :, 0:DH],
                                        rden[:, 16 * i:16 * i + 16].rearrange("p (t j) -> p t j", t=TB).unsqueeze(3).broadcast_to(
                                            [P, TB, 4, DH]), ALU.mult)
                m.then_inc(o_taken, 1)
                v.wait_ge(o_taken, n)

            def divide_d(b):
                w = job(("oT", "D", b, 0))
                nb = 15
                wv = w[:, 0:32 * nb].rearrange("p (n r) -> p n r", r=32)
                own(v.reciprocal(rden[:, 0:nb], wv[:, :, DH2]))
                for n0, k, dst in ((0, 8, on[:, 0:2, 0:64].rearrange("p t (j d) -> p t j d", d=DH2)),
                                   (8, 2, on[:, 2, 0:32].rearrange("p (j d) -> p j d", d=DH2)),
                                   (12, 1, on[:, 3, 0:16].rearrange("p (j d) -> p j d", d=DH2)),
                                   (13, 2, on[:, 0, 64:128].rearrange("p (j x) -> p j x", j=2)[:, :, 0:DH2]),
                                   (10, 2, on[:, 0, 64:128].rearrange("p (j x) -> p j x", j=2)[:, :, DH2:2 * DH2])):
                    src, by = wv[:, n0:n0 + k, 0:DH2], rden[:, n0:n0 + k]
                    if k == 8:
                        src, by = src.rearrange("p (t j) d -> p t j d", t=2), by.rearrange("p (t j) -> p t j", t=2).unsqueeze(3)
                    else:
                        by = by.unsqueeze(2)
                    m = v.tensor_tensor(dst, src, by.broadcast_to([P] + ([2, 4] if k == 8 else [k]) + [DH2]), ALU.mult)
                m.then_inc(job_dve, 1)

            def residual(L, b):
                w = job(("y", L, b))
                v.wait_ge(xb_ready, {"A": 0, "B": 2, "C": 4, "D": 6}[L] + b + 1)
                if L == "D":
                    for e in range(TB):
                        k = D >> e
                        o = xb[:, TB * b + e, 0:k]
                        m = v.scalar_tensor_tensor(o, w[:, P * e:P * e + k], tg[:, 3:4], o, ALU.mult, ALU.add)
                else:
                    g = 0 if L == "A" else 1
                    t = slice(TB * b, TB * b + TB)
                    m = v.scalar_tensor_tensor(x[:, t, :].rearrange("p t d -> p (t d)"), w, tg[:, g:g + 1],
                                               xb[:, t, :].rearrange("p t d -> p (t d)"), ALU.mult, ALU.add)
                m.then_inc(job_dve, 1)
                v.wait_ge(*done("y", L, b))

            def take_k(L):
                k_in = (ts[:, 2, :] if L == 0 else wk[:, JOB["kv", "C"] % 2, :])[:, 0:B * NK]
                k = ROW_AT["L0_xattn_bk"]
                if L == 1:
                    v.wait_ge(qst_in[XI["A", 1]], 96)
                    v.memset(kparts[1][:, :, :, NK:P], 0.0).then_inc(kpad, 1)
                v.wait_ge(kpad, L + 1)
                if L == 0:
                    v.wait_ge(kv_mm, 1)
                    own(v.tensor_scalar(kf[:, :], k_in, col[:, k:k + 1], float(DH) ** -0.5, ALU.add, ALU.mult))
                else:
                    v.wait_ge(job_mm, JOB["kv", "C"] + 1)
                    own(v.tensor_scalar(kf[:, :], k_in, float(DH) ** -0.5, None, ALU.mult))
                split3(kf[:, :].rearrange("p (b k) -> p b k", b=B), kr[:, :].rearrange("p (b k) -> p b k", b=B),
                       [kparts[L][:, s, :, 0:NK] for s in range(3)], kparts_ready)

            def take_v(L):
                v_in = (ts[0:NK, 1, :] if L == 0 else wk[0:NK, JOB["kv", "C"] % 2, :])[:, 2 * P:4 * P]
                v.wait_ge(const, C_VST)
                if L == 0:
                    v.wait_ge(kv_mm, 2)
                    v.wait_ge(bc_in, 32)
                for b in range(B):
                    src = v_in[:, P * b:P * b + P].rearrange("p (h d) -> p h d", d=DH)
                    dst = vst[L][0:NK, b, :, 0:DH]
                    if L == 0:
                        bv = bc[0:NK, BC_AT["L0_xattn_bv"], :].rearrange("p (h d) -> p h d", d=DH)
                        m = v.tensor_tensor(dst, src, bv, ALU.add)
                        m.then_inc(vst_ready, 1)
                    elif b == 0:
                        v.tensor_copy(dst, src)
                    else:
                        v.tensor_copy(dst, src).then_inc(job_dve, 1)

            def maxima(L):
                for u in range(QM_UNITS[L]):
                    take_max(L, 0, u)
                split_max(L, 0)
                for u in range(LEAD):
                    take_max(L, 1, u)
                take_nT(L, 0)
                for u in range(LEAD, QM_UNITS[L]):
                    take_max(L, 1, u)
                split_max(L, 1)
                if L != "D":
                    take_pv(L, 0, 0)
                take_nT(L, 1)
                if L == "A":
                    take_k(1)
                    take_v(1)
                    v.wait_ge(tg_ready, 1)
                    v.tensor_scalar(tgs[:, :], tg[:, 2:3], SHARED_SCALE, None, ALU.mult).then_inc(tgs_ready, 1)
                    v.wait_ge(*done("columns"))
                    k = ROW_AT["L1_ffn_k_b"]
                    v.tensor_scalar(bk2[:, :], col[:, k:k + 1], float(D) ** -0.5, None, ALU.mult).then_inc(bk2_ready, 1)

            def take_logits(b):
                w = job(("logits", b))
                lv = w[:, 0:TB * E].rearrange("p (t e) -> p t e", e=E)
                t = slice(TB * b, TB * b + TB)
                own(v.tensor_reduce(best[:, t], lv, AX.X, ALU.max))
                v.tensor_tensor(lg[:, t, :], lv, best[:, t].unsqueeze(2).broadcast_to([P, TB, E]), ALU.subtract).then_inc(job_dve, 1)

            def cross_attention(L, following):
                maxima(L)
                for g in range(1, 4):
                    take_pv(L, 0, g)
                    if g == 2:
                        divide(L, 0, 0)
                divide(L, 0, 1)
                take_pv(L, 1, 0)
                take_onT(L, 0)
                take_pv(L, 1, 1)
                residual(L, 0)
                norm_stats(following, 0)
                take_pv(L, 1, 2)
                divide(L, 1, 0)
                take_pv(L, 1, 3)
                norm(following, 0)
                divide(L, 1, 1)

            v.memset(kparts[0][:, :, :, NK:P], 0.0).then_inc(kpad, 1)
            own(v.memset(nmx[:, :, :], 0.0))
            v.wait_ge(x_in[0], 16)
            norm_stats("A", 0)
            v.wait_ge(mask_in, 16)
            own(v.tensor_scalar(keep[:, :, :], mask_i[:, :, :], 0.0, None, ALU.not_equal))
            own(v.tensor_reduce(some[:, :], keep[:, :, :], AX.X, ALU.max))
            v.tensor_copy(some_b[:, :], some[:, :]).then_inc(some_ready, 1)
            v.wait_ge(rows_in, 32)
            v.tensor_copy(qk_perm[:, 0, :].rearrange("c (d h) -> c h d", h=H),
                          qk_rows[:, 0, :].rearrange("c (h d) -> c h d", h=H)).then_inc(perm_ready[0], 1)
            norm("A", 0)
            own(v.tensor_scalar(none[:, :], some[:, :], -1.0, 1.0, ALU.mult, ALU.add))
            own(v.tensor_tensor(keep[:, :, :], keep[:, :, :], none[:, :].unsqueeze(2).broadcast_to([P, NT, NK]), ALU.max))
            v.tensor_scalar(mneg[:, :, :], keep[:, :, :], -1.0, None, ALU.add).then_inc(mneg_ready, 1)
            take_k(0)
            v.wait_ge(x_in[1], 16)
            norm_stats("A", 1)
            take_q("A", 0)
            norm("A", 1)
            take_v(0)
            take_q("A", 1)
            cross_attention("A", "B")
            residual("A", 1)
            norm_stats("B", 1)
            take_logits(0)
            norm("B", 1)

            wide = lambda t: t.unsqueeze(2).broadcast_to([P, NT, E])
            v.wait_ge(const, C_SIDX)
            take_logits(1)
            v.wait_ge(ex_ready, 1)
            own(v.tensor_reduce(sums[:, :], gates[:, :, :], AX.X, ALU.add))
            own(v.reciprocal(sums[:, :], sums[:, :]))
            own(v.tensor_tensor(gates[:, :, :], gates[:, :, :], wide(sums[:, :]), ALU.mult))

            def choose(src, c):
                own(v.tensor_reduce(g12[:, c, :], src, AX.X, ALU.max))
                own(v.tensor_tensor(cand[:, :, :], src, wide(g12[:, c, :]), ALU.is_equal))
                own(v.tensor_tensor(cand[:, :, :], cand[:, :, :], iota8[:, :, :], ALU.mult))
                own(v.tensor_reduce(first[:, :], cand[:, :, :], AX.X, ALU.min))
                v.tensor_tensor(hotb[:, c, :, :], iota8[:, :, :], wide(first[:, :]), ALU.is_equal).then_inc(hot_ready, 1)
                v.tensor_tensor(hot[:, c, :, :], iota8[:, :, :], wide(first[:, :]), ALU.is_equal)
                own(v.tensor_scalar(s12[:, c, :], first[:, :], float(CAP), float(CAP * E), ALU.mult, ALU.add))

            def slots(c):
                w = job(("pos", c))
                wv = w[:, 0:NT * E].rearrange("p (t e) -> p t e", t=NT)
                if c == 0:
                    v.tensor_tensor(rt[:, c, :, :], wv, hot[:, c, :, :], ALU.mult)
                    v.tensor_reduce(n1[:, :], w[:, NT * E:2 * NT * E].rearrange("p (t e) -> p e t", e=E), AX.X, ALU.add).then_inc(job_dve, 1)
                    v.wait_ge(*done("pos", 0))
                    v.tensor_scalar(n1[:, :], n1[:, :], float(CAP), None, ALU.min)
                else:
                    v.tensor_tensor(rt[:, c, :, :], wv, n1[:, :].unsqueeze(1).broadcast_to([P, NT, E]), ALU.add).then_inc(job_dve, 1)
                    v.wait_ge(*done("pos", 1))
                    own(v.tensor_tensor(rt[:, c, :, :], rt[:, c, :, :], hot[:, c, :, :], ALU.mult))
                own(v.tensor_reduce(p12[:, c, :], rt[:, c, :, :], AX.X, ALU.add))
                v.tensor_tensor(s12[:, c, :], s12[:, c, :], p12[:, c, :], ALU.add)
                own(v.tensor_scalar(k12[:, c, :], p12[:, c, :], float(CAP), NONE, ALU.is_ge, ALU.mult))
                v.tensor_tensor(slot_i[:, c, :], s12[:, c, :], k12[:, c, :], ALU.add).then_inc(slot_ready, 1)

            choose(gates[:, :, :], 0)
            own(v.tensor_tensor(cand[:, :, :], iota8[:, :, :], wide(first[:, :]), ALU.not_equal))
            own(v.tensor_tensor(gates2[:, :, :], gates[:, :, :], cand[:, :, :], ALU.mult))
            slots(0)
            choose(gates2[:, :, :], 1)
            slots(1)
            own(v.scalar_tensor_tensor(g12[:, :, :], k12[:, :, :], 0.0, g12[:, :, :], ALU.is_equal, ALU.mult))
            own(v.tensor_tensor(den[:, :], g12[:, 0, :], g12[:, 1, :], ALU.add))
            own(v.tensor_scalar(den[:, :], den[:, :], FEPS, None, ALU.max))
            own(v.reciprocal(den[:, :], den[:, :]))
            own(v.tensor_scalar(den[:, :], den[:, :], tg[:, 2:3], None, ALU.mult))
            own(v.tensor_tensor(g12[:, :, :], g12[:, :, :], den[:, :].unsqueeze(1).broadcast_to([P, 2, NT]), ALU.mult))
            nv = n1s[:, :].rearrange("p (k r) -> p k r", r=5)
            pair = n1[:, :].rearrange("p (k r) -> p k r", r=2)
            v.tensor_copy(nv[:, :, 0:2], pair[:, :, 0:1].broadcast_to([P, ST // 5, 2]))
            v.tensor_copy(nv[:, :, 3:5], pair[:, :, 1:2].broadcast_to([P, ST // 5, 2]))
            v.tensor_copy(nv[0:64, :, 2:3], pair[0:64, :, 0:1])
            own(v.tensor_copy(nv[64:P, :, 2:3], pair[64:P, :, 1:2]))
            own(v.tensor_tensor(n1s[:, :], sidx[:, :], n1s[:, :], ALU.is_ge))
            for b in range(B):
                v.wait_ge(xb_ready, 2 + b + 1)
                v.wait_ge(out_mm, b + 1)
                xv = xb[:, TB * b:TB * b + TB, :].rearrange("p t d -> p (t d)")
                v.scalar_tensor_tensor(xv, qm[:, b, :], tgs[:, 0:1], xv, ALU.mult, ALU.add).then_inc(out_ev, 1)
            for n in range(ST // 4):
                v.wait_ge(xg_in[n], 16)
            v.scalar_tensor_tensor(dst_i[:, :], n1s[:, :], float(NTOK), xg[:, :, D], ALU.mult, ALU.add).then_inc(dst_ready, 1)
            v.wait_ge(moe_in[2], 16 * (E + 1))
            for i in range(ST):
                v.wait_ge(out_mm, 2 + i + 1)
                if i >= 4:
                    v.wait_ge(y_scats[i % 4], 16 * (i // 4))
                k, r = 2 * (i // 5), i % 5
                src = qm[:, (2 + i) % 2, 0:D]
                if r == 2:
                    v.tensor_tensor(ostage[0:64, i % 4, :], src[0:64], b2[0:64, k, :], ALU.add)
                    m = v.tensor_tensor(ostage[64:P, i % 4, :], src[64:P], b2[64:P, k + 1, :], ALU.add)
                else:
                    m = v.tensor_tensor(ostage[:, i % 4, :], src, b2[:, k + (r > 2), :], ALU.add)
                m.then_inc(out_ev, 1)
            v.wait_ge(out_ev, 2)
            def combine(b):
                v.wait_ge(y_in[b], 32)
                for t in range(TB * b, TB * b + TB):
                    m = v.scalar_tensor_tensor(xb[:, t, :], y12[:, 0, t, :], g12[:, 0, t:t + 1], xb[:, t, :], ALU.mult, ALU.add)
                own(m)
                for t in range(TB * b, TB * b + TB):
                    m = v.scalar_tensor_tensor(x[:, t, :], y12[:, 1, t, :], g12[:, 1, t:t + 1], xb[:, t, :], ALU.mult, ALU.add)
                m.then_inc(x_moe, 1)
                v.wait_ge(x_moe, b + 1)

            combine(0)
            norm_stats("C", 0)
            norm("C", 0)
            combine(1)
            norm_stats("C", 1)

            norm("C", 1)
            split_rest("C", 0, "q")
            split_rest("C", 1, "q")
            cross_attention("C", "D")
            residual("C", 1)
            norm_stats("D", 1)
            split_rest("D", 0, "q")
            norm("D", 1)
            split_rest("D", 0, "k")
            take_v2(0)
            split_rest("D", 1, "q")
            split_rest("D", 1, "k")
            take_v2(1)
            maxima("D")
            take_pv("D", 0, 0)
            divide_d(0)
            take_onT("D", 0)
            residual("D", 0)
            take_pv("D", 1, 0)
            divide_d(1)
            take_onT("D", 1)
            residual("D", 1)


INS = ["x", "ctx_1024", "mask_Bx1xSxS2_ik1", "g_xattn", "g_ffn", "L0_xattn_Wq", "L0_xattn_bq", "L0_xattn_Wk",
       "L0_xattn_bk", "L0_xattn_Wv", "L0_xattn_bv", "L0_xattn_Wo", "L0_xattn_bo", "L0_ffn_router_w", "L0_ffn_w1",
       "L0_ffn_b1", "L0_ffn_w2", "L0_ffn_b2", "L0_ffn_sw1", "L0_ffn_sb1", "L0_ffn_sw2", "L0_ffn_sb2", "L1_xattn_Wv",
       "L1_xattn_Wk", "L1_xattn_Wq", "L1_xattn_Wo", "L1_xattn_bo", "L1_ffn_norm_w", "L1_ffn_norm_b", "L1_ffn_q_w",
       "L1_ffn_q_b", "L1_ffn_k_w", "L1_ffn_k_b", "L1_ffn_v_w", "L1_ffn_v_b", "L1_ffn_o_w", "L1_ffn_o_b"]


def kernel(**inputs):
    import concourse.bacc as bacc
    from concourse.bass_utils import run_bass_kernel_spmd

    nc = bacc.Bacc("TRN2", target_bir_lowering=False, num_devices=1)
    arrays, args = {}, {}
    for name in INS:
        arr = np.ascontiguousarray(inputs[name])
        arrays[f"in_{name}"] = arr
        args[name] = nc.dram_tensor(f"in_{name}", arr.shape, mybir.dt.from_np(arr.dtype), kind="ExternalInput").ap()
    out = nc.dram_tensor("out_x", (B, S, D), F32, kind="ExternalOutput").ap()
    build(nc, args, out)
    r = run_bass_kernel_spmd(nc, [arrays], core_ids=[0])
    return r.results[0]["out_x"]
```
